# Optimizing a Trainium2 kernel written in Bass

```python
import numpy as np
import jax
import jax.numpy as jnp

def _softmax(x, axis=-1):
    return jax.nn.softmax(x, axis=axis)

def _gelu(x):
    return jax.nn.gelu(x, approximate=True)

def _silu(x):
    return jax.nn.silu(x)

def _sigmoid(x):
    return jax.nn.sigmoid(x)

def _layernorm(x, axis=-1, eps=1e-05):
    m = jnp.mean(x, axis=axis, keepdims=True)
    v = jnp.var(x, axis=axis, keepdims=True)
    return (x - m) / jnp.sqrt(v + eps)

def _scatter_add(tgt, idx, src, axis=0):
    return tgt.at[idx].add(src)

def _segment_sum(src, seg, n):
    return jax.ops.segment_sum(src, seg, n)
kernel_name = 'mk_prb_d4_jaxref_r8_dbf986'

def setup_inputs(seed: int=0):
    np.random.seed(seed)
    _w = jnp.asarray

    def _L0_attn_setup():
        import jax, jax.numpy as jnp
        import numpy as np
        DIM = 256
        HID = 512
        H = 64
        P = HID // H
        N = 128
        G = 1
        K = 4
        Q = 128
        CONV_DIM = HID + 2 * G * N
        D_IN = 2 * HID + 2 * G * N + H
        EPS = 1e-05

        def _causal_conv_silu(xBC, w):
            kern = w.T[:, None, :]
            y = jax.lax.conv_general_dilated(xBC, kern, window_strides=(1,), padding=[(K - 1, 0)], dimension_numbers=('NHC', 'HIO', 'NHC'), feature_group_count=xBC.shape[-1])
            return y * jax.nn.sigmoid(y)

        def _ssm(x, W_in, conv_w, dt_bias, A_log, D, norm_w, W_out):
            Bsz, L, _ = x.shape
            zxbcdt = x @ W_in.T
            z = zxbcdt[..., :HID]
            xBC = zxbcdt[..., HID:HID + CONV_DIM]
            dt_raw = zxbcdt[..., HID + CONV_DIM:]
            xBC = _causal_conv_silu(xBC, conv_w)
            xs = xBC[..., :HID].reshape(Bsz, L, H, P)
            rep = H // G
            Bh = jnp.repeat(xBC[..., HID:HID + G * N].reshape(Bsz, L, G, N), rep, axis=2)
            Ch = jnp.repeat(xBC[..., HID + G * N:].reshape(Bsz, L, G, N), rep, axis=2)
            dt = jax.nn.softplus(dt_raw + dt_bias)
            A = -jnp.exp(A_log)
            nc = L // Q
            a = (dt * A).reshape(Bsz, nc, Q, H)
            cum = jnp.cumsum(a, axis=2)
            xs_c = xs.reshape(Bsz, nc, Q, H, P)
            dtc = dt.reshape(Bsz, nc, Q, H)
            Bc = Bh.reshape(Bsz, nc, Q, H, N)
            Cc = Ch.reshape(Bsz, nc, Q, H, N)
            diff = cum[:, :, :, None, :] - cum[:, :, None, :, :]
            tril = jnp.tril(jnp.ones((Q, Q), bool))[None, None, :, :, None]
            Lmat = jnp.exp(jnp.where(tril, diff, -jnp.inf))
            CB = jnp.einsum('bcihn,bcjhn->bcijh', Cc, Bc)
            M = CB * Lmat * dtc[:, :, None, :, :]
            Yd = jnp.einsum('bcijh,bcjhp->bcihp', M, xs_c)
            wdec = jnp.exp(cum[:, :, -1:, :] - cum) * dtc
            states = jnp.einsum('bcqh,bcqhn,bcqhp->bchpn', wdec, Bc, xs_c)
            chunk_decay = jnp.exp(cum[:, :, -1, :])

            def step(S, inp):
                dec, st = inp
                return (S * dec[..., None, None] + st, S)
            S0 = jnp.zeros((Bsz, H, P, N), x.dtype)
            _, Sprev = jax.lax.scan(step, S0, (chunk_decay.transpose(1, 0, 2), states.transpose(1, 0, 2, 3, 4)))
            Sprev = Sprev.transpose(1, 0, 2, 3, 4)
            Yoff = jnp.einsum('bcqh,bcqhn,bchpn->bcqhp', jnp.exp(cum), Cc, Sprev)
            y = (Yd + Yoff).reshape(Bsz, L, H, P) + D[None, None, :, None] * xs
            y = y.reshape(Bsz, L, HID)
            yz = y * (z * jax.nn.sigmoid(z))
            yn = yz * jax.lax.rsqrt(jnp.mean(yz * yz, axis=-1, keepdims=True) + EPS) * norm_w
            return yn @ W_out.T
        key = jax.random.key(seed)
        k = jax.random.split(key, 6)
        return {'x': jax.random.normal(k[0], (2, 512, DIM), jnp.float32), 'W_in': jax.random.normal(k[1], (D_IN, DIM), jnp.float32) * DIM ** (-0.5), 'conv_w': jax.random.normal(k[2], (CONV_DIM, K), jnp.float32) * K ** (-0.5), 'dt_bias': jax.random.uniform(k[3], (H,), jnp.float32, minval=0.001, maxval=0.1), 'A_log': jnp.log(jax.random.uniform(k[4], (H,), jnp.float32, minval=1.0, maxval=16.0)), 'D': jnp.ones((H,), jnp.float32), 'norm_w': jnp.ones((HID,), jnp.float32), 'W_out': jax.random.normal(k[5], (DIM, HID), jnp.float32) * HID ** (-0.5)}
    _L0_attn_in = _L0_attn_setup()

    def _L0_ffn_setup():
        import jax, jax.numpy as jnp
        import numpy as np
        H = 256
        E = 8
        TOPK = 2
        I_MOE = 128
        I_SH = 512

        def _silu_and_mul(gu):
            g, u = jnp.split(gu, 2, axis=-1)
            return jax.nn.silu(g) * u
        key = jax.random.key(seed)
        ks = jax.random.split(key, 6)
        s = lambda *sh: 1.0 / np.sqrt(sh[-2])
        hidden_states = jax.random.normal(ks[0], (2, 128, H), dtype=jnp.float32)
        w_gate = jax.random.normal(ks[1], (H, E), dtype=jnp.float32) * (1.0 / np.sqrt(H))
        w_gate_up = jax.random.normal(ks[2], (E, H, 2 * I_MOE), dtype=jnp.float32) * (1.0 / np.sqrt(H))
        w_down = jax.random.normal(ks[3], (E, I_MOE, H), dtype=jnp.float32) * (1.0 / np.sqrt(I_MOE))
        w_sh_gate_up = jax.random.normal(ks[4], (H, 2 * I_SH), dtype=jnp.float32) * (1.0 / np.sqrt(H))
        w_sh_down = jax.random.normal(ks[5], (I_SH, H), dtype=jnp.float32) * (1.0 / np.sqrt(I_SH))
        return {'hidden_states': hidden_states, 'w_gate': w_gate, 'w_gate_up': w_gate_up, 'w_down': w_down, 'w_sh_gate_up': w_sh_gate_up, 'w_sh_down': w_sh_down}
    _L0_ffn_in = _L0_ffn_setup()

    def _L1_attn_setup():
        import jax, jax.numpy as jnp
        import numpy as np
        B, S, H = (4, 256, 256)
        key = jax.random.key(seed)
        k1, k2, k3 = jax.random.split(key, 3)
        xav_qkv = float(np.sqrt(6.0 / (H + 3 * H)))
        xav_out = float(np.sqrt(6.0 / (H + H)))
        return {'hidden_states': jax.random.normal(k1, (B, S, H), dtype=jnp.float32), 'w_qkv': jax.random.uniform(k2, (3 * H, H), minval=-xav_qkv, maxval=xav_qkv, dtype=jnp.float32), 'b_qkv': jnp.zeros((3 * H,), dtype=jnp.float32), 'w_out': jax.random.uniform(k3, (H, H), minval=-xav_out, maxval=xav_out, dtype=jnp.float32), 'b_out': jnp.zeros((H,), dtype=jnp.float32)}
    _L1_attn_in = _L1_attn_setup()

    def _L1_ffn_setup():
        import jax, jax.numpy as jnp
        import numpy as np
        EPS = 1e-08

        def _bit_quant(w):
            scale = jnp.maximum(jnp.mean(jnp.abs(w)), EPS)
            w_ternary = jnp.clip(jnp.round(w / scale), -1.0, 1.0)
            return w + jax.lax.stop_gradient(w_ternary - w)
        key = jax.random.key(seed)
        k = jax.random.split(key, 5)
        emb, dff = (256, 1024)
        B, S = (4, 256)
        x = jax.random.normal(k[0], (B, S, emb), dtype=jnp.float32)
        w1 = jax.random.normal(k[1], (dff, emb), dtype=jnp.float32) * 0.02
        b1 = jax.random.normal(k[2], (dff,), dtype=jnp.float32) * 0.02
        w2 = jax.random.normal(k[3], (emb, dff), dtype=jnp.float32) * 0.02
        b2 = jax.random.normal(k[4], (emb,), dtype=jnp.float32) * 0.02
        return {'x': x, 'w1': w1, 'b1': b1, 'w2': w2, 'b2': b2}
    _L1_ffn_in = _L1_ffn_setup()

    def _L2_attn_setup():
        import jax, jax.numpy as jnp
        import numpy as np
        B, T, H = (8, 256, 256)
        LN_EPS = 1e-05

        def _timemix(x, ln_scale, ln_bias, mix_k, mix_v, mix_r, time_first, time_decay, Wk, Wv, Wr, Wo):
            mean = jnp.mean(x, axis=-1, keepdims=True)
            var = jnp.mean((x - mean) ** 2, axis=-1, keepdims=True)
            xn = (x - mean) * jax.lax.rsqrt(var + LN_EPS) * ln_scale + ln_bias
            prev = jnp.concatenate([jnp.zeros_like(xn[:, :1]), xn[:, :-1]], axis=1)
            kx = xn * mix_k + prev * (1.0 - mix_k)
            vx = xn * mix_v + prev * (1.0 - mix_v)
            rx = xn * mix_r + prev * (1.0 - mix_r)
            r = jax.nn.sigmoid(jnp.einsum('bth,hd->btd', rx, Wr))
            k = jnp.einsum('bth,hd->btd', kx, Wk)
            v = jnp.einsum('bth,hd->btd', vx, Wv)
            w = -jnp.exp(time_decay)
            kT = jnp.moveaxis(k, 1, 0)
            vT = jnp.moveaxis(v, 1, 0)

            def step(carry, kv):
                a, b, p = carry
                kt, vt = kv
                uk = kt + time_first
                q = jnp.maximum(uk, p)
                e1 = jnp.exp(p - q)
                e2 = jnp.exp(uk - q)
                num = e1 * a + e2 * vt
                den = e1 * b + e2
                den_safe = jnp.where(den == 0.0, 1.0, den)
                wkv = jnp.where(den == 0.0, 0.0, num / den_safe)
                cw = w + p
                q2 = jnp.maximum(cw, kt)
                ce1 = jnp.exp(cw - q2)
                ce2 = jnp.exp(kt - q2)
                return ((ce1 * a + ce2 * vt, ce1 * b + ce2, q2), wkv)
            bz = x.shape[0]
            init = (jnp.zeros((bz, H), jnp.float32), jnp.zeros((bz, H), jnp.float32), jnp.full((bz, H), 1.0 - 1e+30, jnp.float32))
            _, wkvT = jax.lax.scan(step, init, (kT, vT))
            wkv = jnp.moveaxis(wkvT, 0, 1)
            out = x + jnp.einsum('bth,hd->btd', r * wkv, Wo)
            return out
        key = jax.random.key(seed)
        ks = jax.random.split(key, 12)
        x = jax.random.normal(ks[0], (B, T, H), dtype=jnp.float32)
        ln_scale = jnp.ones((H,), jnp.float32) + 0.1 * jax.random.normal(ks[1], (H,), jnp.float32)
        ln_bias = 0.1 * jax.random.normal(ks[2], (H,), jnp.float32)
        mix_k = jax.random.uniform(ks[3], (H,), jnp.float32)
        mix_v = jax.random.uniform(ks[4], (H,), jnp.float32)
        mix_r = jax.random.uniform(ks[5], (H,), jnp.float32)
        time_first = 0.3 * jax.random.normal(ks[6], (H,), jnp.float32)
        time_decay = 0.5 * jax.random.normal(ks[7], (H,), jnp.float32)
        std = 0.02
        Wk = std * jax.random.normal(ks[8], (H, H), jnp.float32)
        Wv = std * jax.random.normal(ks[9], (H, H), jnp.float32)
        Wr = std * jax.random.normal(ks[10], (H, H), jnp.float32)
        Wo = std * jax.random.normal(ks[11], (H, H), jnp.float32)
        return {'x': x, 'ln_scale': ln_scale, 'ln_bias': ln_bias, 'mix_k': mix_k, 'mix_v': mix_v, 'mix_r': mix_r, 'time_first': time_first, 'time_decay': time_decay, 'Wk': Wk, 'Wv': Wv, 'Wr': Wr, 'Wo': Wo}
    _L2_attn_in = _L2_attn_setup()

    def _L2_ffn_setup():
        import jax, jax.numpy as jnp
        import numpy as np
        DIM = 256
        HID = 704
        ZERO_POINT = 128.0

        def _qlinear(x, wq, scale):
            W = (wq.astype(jnp.float32) - ZERO_POINT) * scale[:, None]
            return jnp.einsum('bsd,hd->bsh', x, W)
        key = jax.random.key(seed)
        ks = jax.random.split(key, 7)
        B, S = (4, 256)
        sg = jax.random.uniform(ks[1], (HID,)) * (0.02 / np.sqrt(DIM)) + 0.0001
        su = jax.random.uniform(ks[3], (HID,)) * (0.02 / np.sqrt(DIM)) + 0.0001
        sd = jax.random.uniform(ks[5], (DIM,)) * (0.02 / np.sqrt(HID)) + 0.0001
        return {'x': jax.random.normal(ks[0], (B, S, DIM), dtype=jnp.float32), 'wq_gate': jax.random.randint(ks[2], (HID, DIM), 0, 32, dtype=jnp.int32), 's_gate': sg, 'wq_up': jax.random.randint(ks[4], (HID, DIM), 0, 32, dtype=jnp.int32), 's_up': su, 'wq_down': jax.random.randint(ks[6], (DIM, HID), 0, 32, dtype=jnp.int32), 's_down': sd}
    _L2_ffn_in = _L2_ffn_setup()

    def _L3_attn_setup():
        import jax, jax.numpy as jnp
        import numpy as np
        EPS = 1e-12

        def _ln(x, g, b):
            m = x.mean(-1, keepdims=True)
            v = x.var(-1, keepdims=True)
            return (x - m) / jnp.sqrt(v + EPS) * g + b

        def _shift(x):
            return jnp.pad(x[:, :-1], ((0, 0), (1, 0), (0, 0)))
        key = jax.random.key(seed)
        ks = jax.random.split(key, 20)
        B, T, H = (4, 256, 256)
        I = 4 * H
        f32 = jnp.float32

        def gamma(k):
            return 1.0 + 0.1 * jax.random.normal(k, (H,), f32)

        def beta(k):
            return 0.1 * jax.random.normal(k, (H,), f32)

        def w(k, i, o):
            return 0.02 * jax.random.normal(k, (i, o), f32)
        return {'x': jax.random.normal(ks[0], (B, T, H), f32), 'ln1_g': gamma(ks[1]), 'ln1_b': beta(ks[2]), 'ln2_g': gamma(ks[3]), 'ln2_b': beta(ks[4]), 'tm_g': gamma(ks[5]), 'tm_b': beta(ks[6]), 'time_decay': -(0.2 + jax.random.uniform(ks[7], (H,), f32)), 'time_first': jax.random.uniform(ks[8], (H,), f32), 'Wk': w(ks[9], H, H), 'Wv': w(ks[10], H, H), 'Wr': w(ks[11], H, H), 'Wo': w(ks[12], H, H), 'bo': jnp.zeros((H,), f32), 'cm_g': gamma(ks[13]), 'cm_b': beta(ks[14]), 'Wck': w(ks[15], H, I), 'Wcv': w(ks[16], I, H), 'Wcr': w(ks[17], H, H)}
    _L3_attn_in = _L3_attn_setup()

    def _L3_ffn_setup():
        import jax, jax.numpy as jnp
        import numpy as np
        ALPHA = 1.702
        LIMIT = 7.0
        TOP_K = 2
        E, H, I = (8, 256, 256)
        B, S = (2, 256)
        key = jax.random.key(seed)
        ks = jax.random.split(key, 7)
        return {'hidden_states': jax.random.normal(ks[0], (B, S, H), dtype=jnp.float32), 'router_weight': jax.random.normal(ks[1], (E, H), dtype=jnp.float32) * 0.02, 'router_bias': jax.random.normal(ks[2], (E,), dtype=jnp.float32) * 0.02, 'gate_up_proj': jax.random.normal(ks[3], (E, H, 2 * I), dtype=jnp.float32) * 0.02, 'gate_up_proj_bias': jax.random.normal(ks[4], (E, 2 * I), dtype=jnp.float32) * 0.02, 'down_proj': jax.random.normal(ks[5], (E, I, H), dtype=jnp.float32) * 0.02, 'down_proj_bias': jax.random.normal(ks[6], (E, H), dtype=jnp.float32) * 0.02}
    _L3_ffn_in = _L3_ffn_setup()
    _d = {'L0_attn_x': _L0_attn_in['x'], 'L0_attn_W_in': _L0_attn_in['W_in'], 'L0_attn_conv_w': _L0_attn_in['conv_w'], 'L0_attn_dt_bias': _L0_attn_in['dt_bias'], 'L0_attn_A_log': _L0_attn_in['A_log'], 'L0_attn_D': _L0_attn_in['D'], 'L0_attn_norm_w': _L0_attn_in['norm_w'], 'L0_attn_W_out': _L0_attn_in['W_out'], 'L0_ffn_w_gate': _L0_ffn_in['w_gate'], 'L0_ffn_w_gate_up': _L0_ffn_in['w_gate_up'], 'L0_ffn_w_down': _L0_ffn_in['w_down'], 'L0_ffn_w_sh_gate_up': _L0_ffn_in['w_sh_gate_up'], 'L0_ffn_w_sh_down': _L0_ffn_in['w_sh_down'], 'L1_attn_w_qkv': _L1_attn_in['w_qkv'], 'L1_attn_b_qkv': _L1_attn_in['b_qkv'], 'L1_attn_w_out': _L1_attn_in['w_out'], 'L1_attn_b_out': _L1_attn_in['b_out'], 'L1_ffn_w1': _L1_ffn_in['w1'], 'L1_ffn_b1': _L1_ffn_in['b1'], 'L1_ffn_w2': _L1_ffn_in['w2'], 'L1_ffn_b2': _L1_ffn_in['b2'], 'L2_attn_ln_scale': _L2_attn_in['ln_scale'], 'L2_attn_ln_bias': _L2_attn_in['ln_bias'], 'L2_attn_mix_k': _L2_attn_in['mix_k'], 'L2_attn_mix_v': _L2_attn_in['mix_v'], 'L2_attn_mix_r': _L2_attn_in['mix_r'], 'L2_attn_time_first': _L2_attn_in['time_first'], 'L2_attn_time_decay': _L2_attn_in['time_decay'], 'L2_attn_Wk': _L2_attn_in['Wk'], 'L2_attn_Wv': _L2_attn_in['Wv'], 'L2_attn_Wr': _L2_attn_in['Wr'], 'L2_attn_Wo': _L2_attn_in['Wo'], 'L2_ffn_wq_gate': _L2_ffn_in['wq_gate'], 'L2_ffn_s_gate': _L2_ffn_in['s_gate'], 'L2_ffn_wq_up': _L2_ffn_in['wq_up'], 'L2_ffn_s_up': _L2_ffn_in['s_up'], 'L2_ffn_wq_down': _L2_ffn_in['wq_down'], 'L2_ffn_s_down': _L2_ffn_in['s_down'], 'L3_attn_ln1_g': _L3_attn_in['ln1_g'], 'L3_attn_ln1_b': _L3_attn_in['ln1_b'], 'L3_attn_ln2_g': _L3_attn_in['ln2_g'], 'L3_attn_ln2_b': _L3_attn_in['ln2_b'], 'L3_attn_tm_g': _L3_attn_in['tm_g'], 'L3_attn_tm_b': _L3_attn_in['tm_b'], 'L3_attn_time_decay': _L3_attn_in['time_decay'], 'L3_attn_time_first': _L3_attn_in['time_first'], 'L3_attn_Wk': _L3_attn_in['Wk'], 'L3_attn_Wv': _L3_attn_in['Wv'], 'L3_attn_Wr': _L3_attn_in['Wr'], 'L3_attn_Wo': _L3_attn_in['Wo'], 'L3_attn_bo': _L3_attn_in['bo'], 'L3_attn_cm_g': _L3_attn_in['cm_g'], 'L3_attn_cm_b': _L3_attn_in['cm_b'], 'L3_attn_Wck': _L3_attn_in['Wck'], 'L3_attn_Wcv': _L3_attn_in['Wcv'], 'L3_attn_Wcr': _L3_attn_in['Wcr'], 'L3_ffn_router_weight': _L3_ffn_in['router_weight'], 'L3_ffn_router_bias': _L3_ffn_in['router_bias'], 'L3_ffn_gate_up_proj': _L3_ffn_in['gate_up_proj'], 'L3_ffn_gate_up_proj_bias': _L3_ffn_in['gate_up_proj_bias'], 'L3_ffn_down_proj': _L3_ffn_in['down_proj'], 'L3_ffn_down_proj_bias': _L3_ffn_in['down_proj_bias']}
    _x0 = _d['L0_attn_x']
    _d['L0_attn_x'] = jax.random.normal(jax.random.fold_in(jax.random.key(seed), 1), (2, 1024, 256), dtype=_x0.dtype)
    del _x0
    return _d

def reference(L0_attn_x, L0_attn_W_in, L0_attn_conv_w, L0_attn_dt_bias, L0_attn_A_log, L0_attn_D, L0_attn_norm_w, L0_attn_W_out, L0_ffn_w_gate, L0_ffn_w_gate_up, L0_ffn_w_down, L0_ffn_w_sh_gate_up, L0_ffn_w_sh_down, L1_attn_w_qkv, L1_attn_b_qkv, L1_attn_w_out, L1_attn_b_out, L1_ffn_w1, L1_ffn_b1, L1_ffn_w2, L1_ffn_b2, L2_attn_ln_scale, L2_attn_ln_bias, L2_attn_mix_k, L2_attn_mix_v, L2_attn_mix_r, L2_attn_time_first, L2_attn_time_decay, L2_attn_Wk, L2_attn_Wv, L2_attn_Wr, L2_attn_Wo, L2_ffn_wq_gate, L2_ffn_s_gate, L2_ffn_wq_up, L2_ffn_s_up, L2_ffn_wq_down, L2_ffn_s_down, L3_attn_ln1_g, L3_attn_ln1_b, L3_attn_ln2_g, L3_attn_ln2_b, L3_attn_tm_g, L3_attn_tm_b, L3_attn_time_decay, L3_attn_time_first, L3_attn_Wk, L3_attn_Wv, L3_attn_Wr, L3_attn_Wo, L3_attn_bo, L3_attn_cm_g, L3_attn_cm_b, L3_attn_Wck, L3_attn_Wcv, L3_attn_Wcr, L3_ffn_router_weight, L3_ffn_router_bias, L3_ffn_gate_up_proj, L3_ffn_gate_up_proj_bias, L3_ffn_down_proj, L3_ffn_down_proj_bias):

    def _L0_attn_ref(x, W_in, conv_w, dt_bias, A_log, D, norm_w, W_out):
        import jax, jax.numpy as jnp
        import numpy as np
        DIM = 256
        HID = 512
        H = 64
        P = HID // H
        N = 128
        G = 1
        K = 4
        Q = 128
        CONV_DIM = HID + 2 * G * N
        D_IN = 2 * HID + 2 * G * N + H
        EPS = 1e-05

        def _causal_conv_silu(xBC, w):
            kern = w.T[:, None, :]
            y = jax.lax.conv_general_dilated(xBC, kern, window_strides=(1,), padding=[(K - 1, 0)], dimension_numbers=('NHC', 'HIO', 'NHC'), feature_group_count=xBC.shape[-1])
            return y * jax.nn.sigmoid(y)

        def _ssm(x, W_in, conv_w, dt_bias, A_log, D, norm_w, W_out):
            Bsz, L, _ = x.shape
            zxbcdt = x @ W_in.T
            z = zxbcdt[..., :HID]
            xBC = zxbcdt[..., HID:HID + CONV_DIM]
            dt_raw = zxbcdt[..., HID + CONV_DIM:]
            xBC = _causal_conv_silu(xBC, conv_w)
            xs = xBC[..., :HID].reshape(Bsz, L, H, P)
            rep = H // G
            Bh = jnp.repeat(xBC[..., HID:HID + G * N].reshape(Bsz, L, G, N), rep, axis=2)
            Ch = jnp.repeat(xBC[..., HID + G * N:].reshape(Bsz, L, G, N), rep, axis=2)
            dt = jax.nn.softplus(dt_raw + dt_bias)
            A = -jnp.exp(A_log)
            nc = L // Q
            a = (dt * A).reshape(Bsz, nc, Q, H)
            cum = jnp.cumsum(a, axis=2)
            xs_c = xs.reshape(Bsz, nc, Q, H, P)
            dtc = dt.reshape(Bsz, nc, Q, H)
            Bc = Bh.reshape(Bsz, nc, Q, H, N)
            Cc = Ch.reshape(Bsz, nc, Q, H, N)
            diff = cum[:, :, :, None, :] - cum[:, :, None, :, :]
            tril = jnp.tril(jnp.ones((Q, Q), bool))[None, None, :, :, None]
            Lmat = jnp.exp(jnp.where(tril, diff, -jnp.inf))
            CB = jnp.einsum('bcihn,bcjhn->bcijh', Cc, Bc)
            M = CB * Lmat * dtc[:, :, None, :, :]
            Yd = jnp.einsum('bcijh,bcjhp->bcihp', M, xs_c)
            wdec = jnp.exp(cum[:, :, -1:, :] - cum) * dtc
            states = jnp.einsum('bcqh,bcqhn,bcqhp->bchpn', wdec, Bc, xs_c)
            chunk_decay = jnp.exp(cum[:, :, -1, :])

            def step(S, inp):
                dec, st = inp
                return (S * dec[..., None, None] + st, S)
            S0 = jnp.zeros((Bsz, H, P, N), x.dtype)
            _, Sprev = jax.lax.scan(step, S0, (chunk_decay.transpose(1, 0, 2), states.transpose(1, 0, 2, 3, 4)))
            Sprev = Sprev.transpose(1, 0, 2, 3, 4)
            Yoff = jnp.einsum('bcqh,bcqhn,bchpn->bcqhp', jnp.exp(cum), Cc, Sprev)
            y = (Yd + Yoff).reshape(Bsz, L, H, P) + D[None, None, :, None] * xs
            y = y.reshape(Bsz, L, HID)
            yz = y * (z * jax.nn.sigmoid(z))
            yn = yz * jax.lax.rsqrt(jnp.mean(yz * yz, axis=-1, keepdims=True) + EPS) * norm_w
            return yn @ W_out.T
        return _ssm(x, W_in, conv_w, dt_bias, A_log, D, norm_w, W_out)

    def _L0_ffn_ref(hidden_states, w_gate, w_gate_up, w_down, w_sh_gate_up, w_sh_down):
        import jax, jax.numpy as jnp
        import numpy as np
        H = 256
        E = 8
        TOPK = 2
        I_MOE = 128
        I_SH = 512

        def _silu_and_mul(gu):
            g, u = jnp.split(gu, 2, axis=-1)
            return jax.nn.silu(g) * u
        orig_shape = hidden_states.shape
        x = hidden_states.reshape(-1, orig_shape[-1])
        router_logits = x @ w_gate
        probs = jax.nn.softmax(router_logits, axis=-1)
        topk_w, topk_ids = jax.lax.top_k(probs, TOPK)
        topk_w = topk_w / jnp.sum(topk_w, axis=-1, keepdims=True)
        combine = jnp.sum(topk_w[..., None] * jax.nn.one_hot(topk_ids, E, dtype=x.dtype), axis=1)
        gu = jnp.einsum('th,ehf->etf', x, w_gate_up)
        act = _silu_and_mul(gu)
        eo = jnp.einsum('eti,eih->eth', act, w_down)
        routed = jnp.einsum('te,eth->th', combine, eo)
        shared = _silu_and_mul(x @ w_sh_gate_up) @ w_sh_down
        return (routed + shared).reshape(orig_shape)

    def _L1_attn_ref(hidden_states, w_qkv, b_qkv, w_out, b_out):
        import jax, jax.numpy as jnp
        import numpy as np
        B, S, H = (4, 256, 256)
        Bc, Sc, Hc = hidden_states.shape
        scaling = jnp.sqrt(jnp.asarray(Hc, hidden_states.dtype))
        qkv = jnp.einsum('bsh,oh->bso', hidden_states, w_qkv) + b_qkv
        q, k, v = jnp.split(qkv, 3, axis=-1)
        scores = jnp.einsum('bqh,bkh->bqk', q, k) / scaling
        probs = jax.nn.softmax(scores, axis=-1)
        context = jnp.einsum('bqk,bkh->bqh', probs, v)
        out = jnp.einsum('bsh,oh->bso', context, w_out) + b_out
        return out

    def _L1_ffn_ref(x, w1, b1, w2, b2):
        import jax, jax.numpy as jnp
        import numpy as np
        EPS = 1e-08

        def _bit_quant(w):
            scale = jnp.maximum(jnp.mean(jnp.abs(w)), EPS)
            w_ternary = jnp.clip(jnp.round(w / scale), -1.0, 1.0)
            return w + jax.lax.stop_gradient(w_ternary - w)
        w1q = _bit_quant(w1)
        w2q = _bit_quant(w2)
        h = jnp.einsum('bsd,fd->bsf', x, w1q) + b1
        h = jax.nn.gelu(h, approximate=False)
        return jnp.einsum('bsf,df->bsd', h, w2q) + b2

    def _L2_attn_ref(x, ln_scale, ln_bias, mix_k, mix_v, mix_r, time_first, time_decay, Wk, Wv, Wr, Wo):
        import jax, jax.numpy as jnp
        import numpy as np
        B, T, H = (8, 256, 256)
        LN_EPS = 1e-05

        def _timemix(x, ln_scale, ln_bias, mix_k, mix_v, mix_r, time_first, time_decay, Wk, Wv, Wr, Wo):
            mean = jnp.mean(x, axis=-1, keepdims=True)
            var = jnp.mean((x - mean) ** 2, axis=-1, keepdims=True)
            xn = (x - mean) * jax.lax.rsqrt(var + LN_EPS) * ln_scale + ln_bias
            prev = jnp.concatenate([jnp.zeros_like(xn[:, :1]), xn[:, :-1]], axis=1)
            kx = xn * mix_k + prev * (1.0 - mix_k)
            vx = xn * mix_v + prev * (1.0 - mix_v)
            rx = xn * mix_r + prev * (1.0 - mix_r)
            r = jax.nn.sigmoid(jnp.einsum('bth,hd->btd', rx, Wr))
            k = jnp.einsum('bth,hd->btd', kx, Wk)
            v = jnp.einsum('bth,hd->btd', vx, Wv)
            w = -jnp.exp(time_decay)
            kT = jnp.moveaxis(k, 1, 0)
            vT = jnp.moveaxis(v, 1, 0)

            def step(carry, kv):
                a, b, p = carry
                kt, vt = kv
                uk = kt + time_first
                q = jnp.maximum(uk, p)
                e1 = jnp.exp(p - q)
                e2 = jnp.exp(uk - q)
                num = e1 * a + e2 * vt
                den = e1 * b + e2
                den_safe = jnp.where(den == 0.0, 1.0, den)
                wkv = jnp.where(den == 0.0, 0.0, num / den_safe)
                cw = w + p
                q2 = jnp.maximum(cw, kt)
                ce1 = jnp.exp(cw - q2)
                ce2 = jnp.exp(kt - q2)
                return ((ce1 * a + ce2 * vt, ce1 * b + ce2, q2), wkv)
            bz = x.shape[0]
            init = (jnp.zeros((bz, H), jnp.float32), jnp.zeros((bz, H), jnp.float32), jnp.full((bz, H), 1.0 - 1e+30, jnp.float32))
            _, wkvT = jax.lax.scan(step, init, (kT, vT))
            wkv = jnp.moveaxis(wkvT, 0, 1)
            out = x + jnp.einsum('bth,hd->btd', r * wkv, Wo)
            return out
        return _timemix(x, ln_scale, ln_bias, mix_k, mix_v, mix_r, time_first, time_decay, Wk, Wv, Wr, Wo)

    def _L2_ffn_ref(x, wq_gate, s_gate, wq_up, s_up, wq_down, s_down):
        import jax, jax.numpy as jnp
        import numpy as np
        DIM = 256
        HID = 704
        ZERO_POINT = 128.0

        def _qlinear(x, wq, scale):
            W = (wq.astype(jnp.float32) - ZERO_POINT) * scale[:, None]
            return jnp.einsum('bsd,hd->bsh', x, W)
        gate = _qlinear(x, wq_gate, s_gate)
        gate = jax.nn.silu(gate)
        up = _qlinear(x, wq_up, s_up)
        return _qlinear(gate * up, wq_down, s_down)

    def _L3_attn_ref(x, ln1_g, ln1_b, ln2_g, ln2_b, tm_g, tm_b, time_decay, time_first, Wk, Wv, Wr, Wo, bo, cm_g, cm_b, Wck, Wcv, Wcr):
        import jax, jax.numpy as jnp
        import numpy as np
        EPS = 1e-12

        def _ln(x, g, b):
            m = x.mean(-1, keepdims=True)
            v = x.var(-1, keepdims=True)
            return (x - m) / jnp.sqrt(v + EPS) * g + b

        def _shift(x):
            return jnp.pad(x[:, :-1], ((0, 0), (1, 0), (0, 0)))
        B, T, H = x.shape
        x1 = _ln(x, ln1_g, ln1_b)
        xln = _ln(x1, tm_g, tm_b)
        xs = _shift(xln)
        mix = xln * time_first + xs * (1.0 - time_first)
        v = xln @ Wv
        r = jax.nn.sigmoid(mix @ Wr)
        dec = jnp.exp(time_decay[None, :] * (T - 1 - jnp.arange(T))[:, None])
        vmix = jnp.einsum('bth,th->bh', v, dec)[:, None, :]
        time_out = r * (vmix @ Wo + bo)
        x2 = x + time_out
        xc = _ln(_ln(x2, ln2_g, ln2_b), cm_g, cm_b)
        xcs = _shift(xc)
        kc = jnp.square(jax.nn.relu(xcs @ Wck))
        vc = kc @ Wcv
        rc = jax.nn.sigmoid(xc @ Wcr)
        return x2 + rc * vc

    def _L3_ffn_ref(hidden_states, router_weight, router_bias, gate_up_proj, gate_up_proj_bias, down_proj, down_proj_bias):
        import jax, jax.numpy as jnp
        import numpy as np
        ALPHA = 1.702
        LIMIT = 7.0
        TOP_K = 2
        E, H, I = (8, 256, 256)
        B, S = (2, 256)
        bsz, seq_len, hidden = hidden_states.shape
        h = hidden_states.reshape(-1, hidden)
        T = h.shape[0]
        logits = h @ router_weight.T + router_bias
        top_vals, top_idx = jax.lax.top_k(logits, TOP_K)
        top_w = jax.nn.softmax(top_vals, axis=-1)
        scores = jnp.zeros_like(logits).at[jnp.arange(T)[:, None], top_idx].set(top_w)
        gate_up = jnp.einsum('th,ehj->etj', h, gate_up_proj) + gate_up_proj_bias[:, None, :]
        gate = gate_up[..., ::2]
        up = gate_up[..., 1::2]
        gate = jnp.minimum(gate, LIMIT)
        up = jnp.clip(up, -LIMIT, LIMIT)
        glu = gate * jax.nn.sigmoid(gate * ALPHA)
        act = (up + 1.0) * glu
        expert_out = jnp.einsum('eti,eih->eth', act, down_proj) + down_proj_bias[:, None, :]
        out = jnp.einsum('te,eth->th', scores, expert_out)
        return out.reshape(bsz, seq_len, hidden)
    x = L0_attn_x
    xn = _layernorm(x, axis=-1)
    x = x + _L0_attn_ref(xn, L0_attn_W_in, L0_attn_conv_w, L0_attn_dt_bias, L0_attn_A_log, L0_attn_D, L0_attn_norm_w, L0_attn_W_out) + _L0_ffn_ref(xn, L0_ffn_w_gate, L0_ffn_w_gate_up, L0_ffn_w_down, L0_ffn_w_sh_gate_up, L0_ffn_w_sh_down)
    xn = _layernorm(x, axis=-1)
    x = x + _L1_attn_ref(xn, L1_attn_w_qkv, L1_attn_b_qkv, L1_attn_w_out, L1_attn_b_out) + _L1_ffn_ref(xn, L1_ffn_w1, L1_ffn_b1, L1_ffn_w2, L1_ffn_b2)
    xn = _layernorm(x, axis=-1)
    x = x + _L2_attn_ref(xn, L2_attn_ln_scale, L2_attn_ln_bias, L2_attn_mix_k, L2_attn_mix_v, L2_attn_mix_r, L2_attn_time_first, L2_attn_time_decay, L2_attn_Wk, L2_attn_Wv, L2_attn_Wr, L2_attn_Wo) + _L2_ffn_ref(xn, L2_ffn_wq_gate, L2_ffn_s_gate, L2_ffn_wq_up, L2_ffn_s_up, L2_ffn_wq_down, L2_ffn_s_down)
    xn = _layernorm(x, axis=-1)
    x = x + _L3_attn_ref(xn, L3_attn_ln1_g, L3_attn_ln1_b, L3_attn_ln2_g, L3_attn_ln2_b, L3_attn_tm_g, L3_attn_tm_b, L3_attn_time_decay, L3_attn_time_first, L3_attn_Wk, L3_attn_Wv, L3_attn_Wr, L3_attn_Wo, L3_attn_bo, L3_attn_cm_g, L3_attn_cm_b, L3_attn_Wck, L3_attn_Wcv, L3_attn_Wcr) + _L3_ffn_ref(xn, L3_ffn_router_weight, L3_ffn_router_bias, L3_ffn_gate_up_proj, L3_ffn_gate_up_proj_bias, L3_ffn_down_proj, L3_ffn_down_proj_bias)
    return x

_drawn_inputs = setup_inputs


def setup_inputs(seed=0):
    import zlib

    import numpy as np

    out = dict(_drawn_inputs(seed))
    spreads = {'L0_attn_D': (1.0, 0.2),
     'L0_attn_norm_w': (1.0, 0.2),
     'L1_attn_b_qkv': (0.0, 0.8),
     'L1_attn_b_out': (0.0, 2.0),
     'L3_attn_bo': (0.0, 2.0)}
    factors = {'L0_attn_dt_bias': 6.27,
     'L1_attn_w_qkv': 8.0,
     'L1_attn_w_out': 8.0,
     'L1_ffn_b1': 8.0,
     'L1_ffn_b2': 64.0,
     'L2_attn_ln_scale': 8.0,
     'L2_attn_ln_bias': 8.0,
     'L2_attn_mix_k': 8.0,
     'L2_attn_mix_v': 8.0,
     'L2_attn_mix_r': 8.0,
     'L2_attn_time_first': 8.0,
     'L2_attn_time_decay': 8.0,
     'L2_attn_Wk': 8.0,
     'L2_attn_Wv': 8.0,
     'L2_attn_Wr': 8.0,
     'L2_attn_Wo': 8.0,
     'L2_ffn_s_gate': 8.0,
     'L2_ffn_s_up': 8.0,
     'L2_ffn_s_down': 8.0,
     'L3_attn_ln1_g': 8.0,
     'L3_attn_ln1_b': 8.0,
     'L3_attn_ln2_g': 8.0,
     'L3_attn_ln2_b': 8.0,
     'L3_attn_tm_g': 8.0,
     'L3_attn_tm_b': 8.0,
     'L3_attn_time_decay': 8.0,
     'L3_attn_time_first': 8.0,
     'L3_attn_Wv': 8.0,
     'L3_attn_Wr': 8.0,
     'L3_attn_Wo': 8.0,
     'L3_attn_cm_g': 8.0,
     'L3_attn_cm_b': 8.0,
     'L3_attn_Wck': 8.0,
     'L3_attn_Wcv': 8.0,
     'L3_attn_Wcr': 8.0,
     'L3_ffn_router_weight': 64.0,
     'L3_ffn_router_bias': 64.0,
     'L3_ffn_gate_up_proj': 64.0,
     'L3_ffn_gate_up_proj_bias': 64.0,
     'L3_ffn_down_proj': 64.0,
     'L3_ffn_down_proj_bias': 64.0}
    for name, (base, spread) in spreads.items():
        noise = np.random.default_rng([zlib.crc32(name.encode()), seed]).standard_normal(out[name].shape)
        drawn = base * np.exp(spread * noise) if base else spread * noise
        out[name] = jnp.asarray(drawn.astype(out[name].dtype))
    for name, factor in factors.items():
        out[name] = (out[name] * factor).astype(out[name].dtype)
    return out
```

```python
from contextlib import ExitStack

import concourse.bass as bass
from concourse import mybir
from concourse.alu_op_type import AluOpType as ALU

F32 = mybir.dt.float32
I32 = mybir.dt.int32
ACT = mybir.ActivationFunctionType
AX = mybir.AxisListType

P = 128
BATCH, SEQ, DIM = 2, 1024, 256
TOKENS = BATCH * SEQ
TILES = TOKENS // P
GROUP = 512
GT = GROUP // P
HALVES = SEQ // GROUP
DK = DIM // P

HID, HEADS, HEAD_P, STATE, CONV_K = 512, 64, 8, 128, 4
CONV_BLK = (HID + 2 * STATE) // P
Z_BLK = HID // P
D_IN = 2 * HID + 2 * STATE + HEADS
N_EXP = 8
L0_UNITS = N_EXP + 4

COLS = [("conv_w", CONV_BLK * CONV_K), ("D", Z_BLK), ("norm_w", Z_BLK), ("b_qkv", 6), ("b1", 8),
        ("ln_scale", 2), ("ln_bias", 2), ("mix_k", 2), ("mix_v", 2), ("mix_r", 2),
        ("time_first", 2), ("time_decay", 2), ("s_gate", 6), ("s_up", 6),
        ("l3_time_decay", 2), ("l3_time_first", 2), ("eb_gate", 16), ("eb_up", 16),
        ("tm_g", 2), ("tm_b", 2), ("cm_g", 2), ("cm_b", 2), ("bo", 2)]
L0_ROWS = [("dt_bias", HEADS), ("A_log", HEADS)]
ROWS = [("b_v", DIM), ("b_out", DIM), ("b2", DIM), ("s_down", DIM),
        ("ln1_g", DIM), ("ln1_b", DIM), ("ln2_g", DIM), ("ln2_b", DIM), ("router_bias", N_EXP)]


def offsets(table):
    at, found = 0, {}
    for name, n in table:
        found[name] = at
        at += n
    return found, at


COL_AT, N_COLS = offsets(COLS)
ROW_AT, N_ROWS = offsets(ROWS)
L0_ROW_AT, N_L0_ROWS = offsets(L0_ROWS)


class Event:

    def __init__(self, sem, per, credit=0, base=0):
        self.sem, self.per, self.credit, self.base = sem, per, credit, base

    def grant(self, eng):
        eng.sem_inc(self.sem, self.credit)

    def done(self, trip, n=None):
        n = self.per - 1 if n is None else n
        return self.base + self.credit + trip * self.per + n + 1

    def room(self, trip, n=0):
        return self.base + trip * self.per + n + 1


class Bank:

    def __init__(self, sem, name, per):
        self.filled = Event(sem(name + "_filled"), per)
        self.freed = Event(sem(name + "_freed"), per, credit=1)

    def wait_room(self, pe, trip, n):
        pe.wait_ge(self.freed.sem, self.freed.room(trip, n))

    def wait_filled(self, eng, trip, n):
        eng.wait_ge(self.filled.sem, self.filled.done(trip, n))


def spread(ap, axis, n):
    wide = ap.unsqueeze(axis)
    shape = list(wide.shape)
    shape[axis] = n
    return wide.broadcast_to(shape)


def layer0(nc, mem, ctx, io):
    sb, ps, sem = mem.scoped(ctx, "l0")
    x, ident, ones = mem.x, mem.ident, mem.ones
    col, row = mem.col, mem.l0_row
    w = mem.l0

    before = sb("before", [P, 1, P])
    after = sb("after", [P, P])
    lower = mem.lower
    exp_a = sb("exp_a", [P, HEADS])
    stats = sb("stats", [P, GT, 6])
    moments = sb("moments", [P, GT, 2])
    rstd = sb("rstd", [P, GT])
    xnT = sb("xnT", [P, DK, GROUP])
    pre = sb("pre", [P, CONV_BLK, CONV_K - 1 + GROUP])
    xbc = sb("xbc", [P, CONV_BLK, GROUP])
    zs = sb("zs", [P, Z_BLK, GROUP])
    hT = sb("hT", [P, L0_UNITS, GROUP])
    lg = sb("lg", [P, GT, N_EXP])
    lmax = sb("lmax", [P, GT])
    le = sb("le", [P, GT, N_EXP])
    rank = sb("rank", [P, GT, N_EXP])
    esum = sb("esum", [P, GT])
    comb = sb("comb", [P, GT, N_EXP])
    dtp = sb("dtp", [P, GT, HEADS])
    dta = sb("dta", [P, GT, HEADS])
    dt = sb("dt", [P, GT, HEADS])
    a = sb("a", [P, GT, HEADS])
    decay = sb("decay", [P, 3, GT, HEADS])
    wdt = sb("wdt", [P, GT, HEADS])
    xp = sb("xp", [P, 2, HEADS, 32])
    wx = sb("wx", [P, HID])
    btok = sb("btok", [P, STATE])
    cbm = sb("cbm", [P, P])
    yoff = sb("yoff", [P, HID])
    st = sb("st", [P, HID])
    r = sb("r", [P, 2, 4, P])
    e = sb("e", [P, 2, 4, P])
    m = sb("m", [P, 2, 4, P])
    xn = r[:, :, :, :].rearrange("p a h i -> p (a h i)").rearrange("p (t d) -> p t d", t=GT)
    sg = e[:, :, :, :].rearrange("p a h i -> p a (h i)")
    pair = m[:, :, :, :].rearrange("p a h i -> p a (h i)")[:, :, 0:GT * N_EXP * N_EXP]
    gt = pair[:, 0, :].rearrange("p (t e f) -> p t e f", t=GT, e=N_EXP)
    eq = pair[:, 1, :].rearrange("p (t e f) -> p t e f", t=GT, e=N_EXP)
    yg = sb("yg", [P, Z_BLK, P])
    ysq = sb("ysq", [P, Z_BLK, P])
    yr = sb("yr", [P, 2])

    bank = [ps(f"l0_b{i}", [P, GROUP]) for i in range(8)]
    HB = 16
    NCH = GT
    gate_b = Bank(sem, "l0_gate_bank", 1 + 5 + L0_UNITS)
    up_b = Bank(sem, "l0_up_bank", 1 + 5 + L0_UNITS)
    diff_b = [Bank(sem, f"l0_diff_bank{i}", NCH * HB // 2) for i in range(2)]
    y_b = Bank(sem, "l0_y_bank", NCH)
    tok_b = Bank(sem, "l0_tok_bank", 2 * NCH)
    down_b = Bank(sem, "l0_down_bank", L0_UNITS * GT // 2)
    misc_b = Bank(sem, "l0_misc_bank", 3 + 3 * NCH)

    moments_ready = Event(sem("l0_moments_ready"), 1)
    rstd_ready = Event(sem("l0_rstd_ready"), 1)
    xn_ready = Event(sem("l0_xn_ready"), 1)
    xnT_dve = Event(sem("l0_xnT_dve"), 1)
    xnT_act = Event(sem("l0_xnT_act"), 1)
    pre_ready = Event(sem("l0_pre_ready"), CONV_BLK)
    z_ready = Event(sem("l0_z_ready"), Z_BLK)
    conv_ready = Event(sem("l0_conv_ready"), CONV_BLK, credit=CONV_BLK)
    xbc_ready = Event(sem("l0_xbc_ready"), CONV_BLK)
    silu_ready = Event(sem("l0_silu_ready"), L0_UNITS)
    hid_ready = Event(sem("l0_hid_ready"), L0_UNITS, credit=2)
    scores_ready = Event(sem("l0_scores_ready"), 1)
    soft_ready = Event(sem("l0_soft_ready"), 1)
    a_ready = Event(sem("l0_a_ready"), 1)
    decay_ready = Event(sem("l0_decay_ready"), 2)
    bc_ready = Event(sem("l0_bc_ready"), NCH)
    xs_ready = Event(sem("l0_xs_ready"), NCH)
    yoff_ready = Event(sem("l0_yoff_ready"), NCH)
    state_ready = Event(sem("l0_state_ready"), NCH, credit=1)
    r_ready = Event(sem("l0_r_ready"), NCH * HB)
    e_ready = Event(sem("l0_e_ready"), NCH * HB)
    m_ready = Event(sem("l0_m_ready"), NCH * HB)
    strip_done = Event(sem("l0_strip_done"), NCH * HB, credit=2)
    yg_ready = Event(sem("l0_yg_ready"), NCH)
    ysq_ready = Event(sem("l0_ysq_ready"), NCH)
    ssq_ready = Event(sem("l0_ssq_ready"), NCH)
    yr_ready = Event(sem("l0_yr_ready"), NCH)
    mask_ready = Event(sem("l0_mask_ready"), 1)
    expa_ready = Event(sem("l0_expa_ready"), 1)
    wn_ready = Event(sem("l0_wn_ready"), 1)
    reset_done = Event(sem("l0_reset_done"), 1)
    group_done = Event(sem("l0_group_done"), 1, credit=1)

    def heads_of(k):
        return [16 * (k // 4) + 4 * s + k % 4 for s in range(4)]

    def down_job(n):
        return n // 2, (2 * (n % 2), 2 * (n % 2) + 1)

    def bc_job(c):
        return 3 if c == 0 else 2 + 3 * c

    def off_job(c):
        return bc_job(c) + 1

    def out_job(c):
        return 4 + 3 * (c + 1) if c < NCH - 1 else 2 + 3 * NCH

    EARLY = 8

    block = ctx.enter_context(nc.Block())

    @block.tensor
    def _(pe):
        def mm(out, lhsT, rhs, start=True, stop=True, **kw):
            return nc.tensor.matmul(out, lhsT, rhs, start=start, stop=stop, **kw)

        def down(g, n):
            u, tiles = down_job(n)
            down_b.wait_room(pe, g, n)
            if n % 2 == 0:
                pe.wait_ge(hid_ready.sem, hid_ready.done(g, u))
            for i, t in enumerate(tiles):
                last = mm(bank[6][:, DIM * i:DIM * (i + 1)], hT[:, u, t * P:(t + 1) * P], w.down[:, u, :])
            last.then_inc(down_b.filled.sem, 1)

        def out_proj(g, c):
            pe.wait_ge(yg_ready.sem, yg_ready.done(g, c))
            pe.wait_ge(ysq_ready.sem, ysq_ready.done(g, c))
            misc_b.wait_room(pe, g, out_job(c))
            for k in range(Z_BLK):
                mm(bank[7][:, 256:257], ysq[:, k, :], ones[:, 0:1], k == 0, k == Z_BLK - 1)
            for k in range(Z_BLK):
                last = mm(bank[7][:, 0:DIM], yg[:, k, :], w.out[:, k, :], k == 0, k == Z_BLK - 1)
            last.then_inc(misc_b.filled.sem, 1)

        pe.wait_ge(mem.const_ready, mem.n_const)
        pe.wait_ge(mask_ready.sem, 1)
        pe.wait_ge(wn_ready.sem, 1)
        with pe.Fori(0, BATCH) as b:
            with pe.Fori(0, HALVES) as half:
                g = b * HALVES + half
                pe.wait_ge(xn_ready.sem, xn_ready.done(g))
                for k, bk in ((0, gate_b), (1, up_b)):
                    bk.wait_room(pe, g, 0)
                    for t in range(GT):
                        last = nc.tensor.transpose(bank[4 + k][:, t * P:(t + 1) * P],
                                                   xn[:, t, k * P:(k + 1) * P], ident[:, :])
                    last.then_inc(bk.filled.sem, 1)
                pe.wait_ge(xnT_dve.sem, xnT_dve.done(g))
                pe.wait_ge(xnT_act.sem, xnT_act.done(g))
                pe.wait_ge(w.gate_sem, 16)
                pe.wait_ge(w.in_sem, 16)
                misc_b.wait_room(pe, g, 0)
                for t in range(GT):
                    for k in range(DK):
                        xt = xnT[:, k, t * P:(t + 1) * P]
                        mm(bank[7][:, 8 * t:8 * t + 8], xt, w.router[:, k, :], k == 0, k == DK - 1)
                    for k in range(DK):
                        xt = xnT[:, k, t * P:(t + 1) * P]
                        last = mm(bank[7][:, 64 + 64 * t:128 + 64 * t], xt,
                                  w.win[:, k, D_IN - HEADS:D_IN], k == 0, k == DK - 1)
                last.then_inc(misc_b.filled.sem, 1)
                for j in range(CONV_BLK + Z_BLK):
                    c0 = HID + j * P if j < CONV_BLK else (j - CONV_BLK) * P
                    bk = (gate_b, up_b)[j % 2]
                    bk.wait_room(pe, g, 1 + j // 2)
                    for k in range(DK):
                        last = mm(bank[4 + j % 2][:, :], w.win[:, k, c0:c0 + P], xnT[:, k, :],
                                  k == 0, k == DK - 1)
                    last.then_inc(bk.filled.sem, 1)
                pe.wait_ge(w.ffn_sem, 16 * 4)
                for u in range(L0_UNITS):
                    for i, bk in ((0, gate_b), (1, up_b)):
                        bk.wait_room(pe, g, 6 + u)
                        for k in range(DK):
                            last = mm(bank[4 + i][:, :], w.gu(u, k, i), xnT[:, k, :],
                                      k == 0, k == DK - 1)
                        last.then_inc(bk.filled.sem, 1)
                for n in range(EARLY):
                    down(g, n)
                pe.wait_ge(a_ready.sem, a_ready.done(g))
                misc_b.wait_room(pe, g, 1)
                a_all = a[:, :, :].rearrange("p c h -> p (c h)")
                mm(bank[7][:, 0:256], before[:, 0, :], a_all)
                mm(bank[7][:, 256:512], after[:, :], a_all).then_inc(misc_b.filled.sem, 1)
                misc_b.wait_room(pe, g, 2)
                mm(bank[7][:, 0:256], ones[:, 0:P], a_all).then_inc(misc_b.filled.sem, 1)
                for c in range(NCH):
                    tok = slice(c * P, (c + 1) * P)
                    pe.wait_ge(xbc_ready.sem, xbc_ready.done(g))
                    tok_b.wait_room(pe, g, 2 * c)
                    for k in range(Z_BLK):
                        last = nc.tensor.transpose(bank[3][:, k * P:(k + 1) * P], xbc[:, k, tok], ident[:, :])
                    last.then_inc(tok_b.filled.sem, 1)
                    misc_b.wait_room(pe, g, bc_job(c))
                    nc.tensor.transpose(bank[7][:, 0:P], xbc[:, 4, tok], ident[:, :])
                    mm(bank[7][:, P:2 * P], xbc[:, 4, tok], xbc[:, 5, tok]).then_inc(misc_b.filled.sem, 1)

                    def diff(k):
                        n = c * HB + k
                        pe.wait_ge(r_ready.sem, r_ready.done(g, n))
                        diff_b[n % 2].wait_room(pe, g, n // 2)
                        mm(bank[n % 2][:, :], after[:, :], r[:, n % 2, :, :]).then_inc(
                            diff_b[n % 2].filled.sem, 1)

                    diff(0)
                    diff(1)
                    if c == 0:
                        pe.wait_ge(reset_done.sem, reset_done.done(b))
                    pe.wait_ge(state_ready.sem, state_ready.room(g, c))
                    misc_b.wait_room(pe, g, off_job(c))
                    mm(bank[7][:, :], xbc[:, 5, tok], st[:, :]).then_inc(misc_b.filled.sem, 1)
                    pe.wait_ge(xs_ready.sem, xs_ready.done(g, c))
                    pe.wait_ge(bc_ready.sem, bc_ready.done(g, c))
                    tok_b.wait_room(pe, g, 2 * c + 1)
                    mm(bank[3][:, :], btok[:, :], wx[:, :]).then_inc(tok_b.filled.sem, 1)
                    for k in range(HB):
                        n = c * HB + k
                        blk = k // 4
                        if k == 0:
                            y_b.wait_room(pe, g, c)
                        pe.wait_ge(m_ready.sem, m_ready.done(g, n))
                        for s, h in enumerate(heads_of(k)):
                            last = mm(bank[2][32 * s:32 * s + 32, blk * P:(blk + 1) * P],
                                      xp[:, c % 2, h, :], m[:, n % 2, s, :], k % 4 == 0, False,
                                      skip_group_check=True)
                        last.then_inc(strip_done.sem, 1)
                        if k + 2 < HB:
                            diff(k + 2)
                        if k % 4 == 3:
                            if k == 3:
                                pe.wait_ge(yoff_ready.sem, yoff_ready.done(g, c))
                            last = mm(bank[2][:, blk * P:(blk + 1) * P], yoff[:, blk * P:(blk + 1) * P],
                                      ident[:, :], False, True, skip_group_check=True)
                            if k == HB - 1:
                                last.then_inc(y_b.filled.sem, 1)
                        if k % 4 == 1:
                            down(g, EARLY + c * 4 + k // 4)
                        if k == 5 and c > 0:
                            out_proj(g, c - 1)
                out_proj(g, NCH - 1)

    @block.scalar
    def _(act):
        act.wait_ge(mem.l0_row_ready, 16)
        nc.scalar.activation(exp_a[:, :], row("A_log"), ACT.Exp).then_inc(expa_ready.sem, 1)
        with act.Fori(0, BATCH) as b:
            with act.Fori(0, HALVES) as half:
                g = b * HALVES + half
                up_b.wait_filled(act, g, 0)
                nc.scalar.activation(xnT[:, 1, :], bank[5][:, :], ACT.Copy).then_inc(xnT_act.sem, 1)
                act.drain().then_inc(up_b.freed.sem, 1)
                for j in range(CONV_BLK + Z_BLK):
                    bk = (gate_b, up_b)[j % 2]
                    bk.wait_filled(act, g, 1 + j // 2)
                    if j < CONV_BLK:
                        if j == 0:
                            act.wait_ge(conv_ready.sem, conv_ready.room(g, CONV_BLK - 1))
                            act.wait_ge(reset_done.sem, reset_done.done(b))
                        nc.scalar.activation(pre[:, j, CONV_K - 1:], bank[4 + j % 2][:, :],
                                             ACT.Copy).then_inc(pre_ready.sem, 1)
                    else:
                        if j == CONV_BLK:
                            act.wait_ge(group_done.sem, group_done.room(g))
                        nc.scalar.activation(zs[:, j - CONV_BLK, :], bank[4 + j % 2][:, :],
                                             ACT.Silu).then_inc(z_ready.sem, 1)
                    act.drain().then_inc(bk.freed.sem, 1)
                for u in range(L0_UNITS):
                    gate_b.wait_filled(act, g, 6 + u)
                    act.wait_ge(hid_ready.sem, hid_ready.room(g, u))
                    nc.scalar.activation(sg[:, u % 2, :], bank[4][:, :], ACT.Silu).then_inc(silu_ready.sem, 1)
                    act.drain().then_inc(gate_b.freed.sem, 1)
                for j in range(CONV_BLK):
                    act.wait_ge(conv_ready.sem, conv_ready.done(g, j))
                    nc.scalar.activation(xbc[:, j, :], xbc[:, j, :], ACT.Silu).then_inc(xbc_ready.sem, 1)
                act.wait_ge(scores_ready.sem, scores_ready.done(g))
                nc.scalar.activation(dta[:, :, :], dtp[:, :, :], ACT.Abs)
                nc.scalar.activation(le[:, :, :], lg[:, :, :], ACT.Exp)
                act.drain()
                nc.scalar.activation(dta[:, :, :], dta[:, :, :], ACT.Exp, scale=-1.0)
                act.drain()
                nc.scalar.activation(dta[:, :, :], dta[:, :, :], ACT.Ln, bias=1.0).then_inc(soft_ready.sem, 1)
                misc_b.wait_filled(act, g, 1)
                nc.scalar.activation(decay[:, 0:2, :, :].rearrange("p s c h -> p (s c h)"), bank[7][:, :],
                                     ACT.Exp).then_inc(decay_ready.sem, 1)
                act.drain().then_inc(misc_b.freed.sem, 1)
                misc_b.wait_filled(act, g, 2)
                nc.scalar.activation(decay[:, 2, :, :].rearrange("p c h -> p (c h)"), bank[7][:, 0:256],
                                     ACT.Exp).then_inc(decay_ready.sem, 1)
                act.drain().then_inc(misc_b.freed.sem, 1)
                for c in range(NCH):
                    for k in range(HB):
                        n = c * HB + k
                        diff_b[n % 2].wait_filled(act, g, n // 2)
                        if n >= 2:
                            act.wait_ge(m_ready.sem, m_ready.done(g, n - 2))
                        nc.scalar.activation(e[:, n % 2, :, :].rearrange("p h i -> p (h i)"),
                                             bank[n % 2][:, :], ACT.Exp).then_inc(e_ready.sem, 1)
                        act.drain().then_inc(diff_b[n % 2].freed.sem, 1)
                    act.wait_ge(yg_ready.sem, yg_ready.done(g, c))
                    if c > 0:
                        act.wait_ge(misc_b.filled.sem, misc_b.filled.done(g, out_job(c - 1)))
                    nc.scalar.activation(ysq[:, :, :], yg[:, :, :], ACT.Square).then_inc(ysq_ready.sem, 1)

    @block.gpsimd
    def _(pool):
        nc.gpsimd.memset(before[:, :, :], 1.0)
        nc.gpsimd.memset(after[:, :], 1.0)
        pool.drain()
        nc.gpsimd.affine_select(out=before[:, 0, :], in_=before[:, 0, :], compare_op=ALU.is_ge, fill=0.0,
                                base=0, pattern=[[1, P]], channel_multiplier=-1)
        nc.gpsimd.affine_select(out=after[:, :], in_=after[:, :], compare_op=ALU.is_gt, fill=0.0,
                                base=0, pattern=[[-1, P]], channel_multiplier=1)
        pool.drain().then_inc(mask_ready.sem, 1)
        with pool.Fori(0, BATCH) as b:
            with pool.Fori(0, HALVES) as half:
                g = b * HALVES + half
                pool.wait_ge(moments_ready.sem, moments_ready.done(g))
                nc.gpsimd.tensor_tensor(rstd[:, :], moments[:, :, 1], mem.neg_half[:, 0:GT], ALU.pow).then_inc(
                    rstd_ready.sem, 1)
                pool.wait_ge(a_ready.sem, a_ready.done(g))

                def out_scale(c):
                    pool.wait_ge(ssq_ready.sem, ssq_ready.done(g, c))
                    nc.gpsimd.tensor_tensor(yr[:, 1:2], yr[:, 0:1], mem.neg_half[:, 0:1], ALU.pow).then_inc(
                        yr_ready.sem, 1)

                for c in range(NCH):
                    for k in range(HB):
                        n = c * HB + k
                        if n >= 2:
                            pool.wait_ge(diff_b[n % 2].filled.sem, diff_b[n % 2].filled.done(g, n // 2 - 1))
                        h0 = 16 * (k // 4) + k % 4
                        nc.gpsimd.tensor_tensor(r[:, n % 2, :, :], spread(before[:, 0, :], 1, 4),
                                                spread(a[:, c, h0:h0 + 13:4], 2, P), ALU.mult).then_inc(
                            r_ready.sem, 1)
                        if k == 7 and c > 0:
                            out_scale(c - 1)
                out_scale(NCH - 1)

    @block.vector
    def _(dve):
        def down_add(g, n):
            u, tiles = down_job(n)
            dve.drain()
            down_b.wait_filled(dve, g, n)
            for i, t in enumerate(tiles):
                xt = x[:, g * GT + t, :]
                scale = comb[:, t, u:u + 1] if u < N_EXP else 1.0
                last = nc.vector.scalar_tensor_tensor(out=xt, in0=bank[6][:, DIM * i:DIM * (i + 1)], scalar=scale,
                                                      in1=xt, op0=ALU.mult, op1=ALU.add)
            last.then_inc(down_b.freed.sem, 1)

        def out_stats(g, c):
            misc_b.wait_filled(dve, g, out_job(c))
            nc.vector.tensor_scalar(yr[:, 0:1], bank[7][:, 256:257], 1.0 / HID, 1e-5, ALU.mult, ALU.add).then_inc(
                ssq_ready.sem, 1)

        def out_add(g, c):
            dve.drain()
            dve.wait_ge(yr_ready.sem, yr_ready.done(g, c))
            xt = x[:, g * GT + c, :]
            nc.vector.scalar_tensor_tensor(out=xt, in0=bank[7][:, 0:DIM], scalar=yr[:, 1:2], in1=xt,
                                           op0=ALU.mult, op1=ALU.add).then_inc(misc_b.freed.sem, 1)

        for bk in (gate_b, up_b, *diff_b, y_b, tok_b, down_b, misc_b):
            bk.freed.grant(dve)
        for ev in (conv_ready, hid_ready, group_done, state_ready, strip_done):
            ev.grant(dve)
        nc.vector.memset(xp[:, :, :, :], 0.0)
        dve.wait_ge(mem.col_ready, 16)
        dve.wait_ge(w.out_sem, 16)
        for k in range(Z_BLK):
            nc.vector.tensor_scalar(w.out[:, k, :], w.out[:, k, :], col("norm_w", k), None, ALU.mult)
        dve.drain().then_inc(wn_ready.sem, 1)
        dve.wait_ge(mem.const_ready, mem.n_const)
        dve.wait_ge(mask_ready.sem, 1)
        dve.wait_ge(expa_ready.sem, 1)
        dve.wait_ge(mem.l0_row_ready, 16)
        dve.wait_ge(mem.x_ready, 16 * 4)
        with dve.Fori(0, BATCH) as b:
            nc.vector.memset(pre[:, :, 0:CONV_K - 1], 0.0)
            nc.vector.memset(st[:, :], 0.0)
            dve.drain().then_inc(reset_done.sem, 1)
            with dve.Fori(0, HALVES) as half:
                g = b * HALVES + half
                for t in range(GT):
                    nc.vector.bn_stats(stats[:, t, :], x[:, g * GT + t, :])
                dve.drain()
                for t in range(GT):
                    nc.vector.bn_aggr(moments[:, t, :], stats[:, t, :])
                dve.drain()
                nc.vector.tensor_scalar(moments[:, :, 1], moments[:, :, 1], 1e-5, None, ALU.add).then_inc(
                    moments_ready.sem, 1)
                dve.wait_ge(rstd_ready.sem, rstd_ready.done(g))
                for t in range(GT):
                    last = nc.vector.tensor_scalar(xn[:, t, :], x[:, g * GT + t, :], moments[:, t, 0:1],
                                                   rstd[:, t:t + 1], ALU.subtract, ALU.mult)
                last.then_inc(xn_ready.sem, 1)
                gate_b.wait_filled(dve, g, 0)
                nc.vector.tensor_copy(xnT[:, 0, :], bank[4][:, :]).then_inc(xnT_dve.sem, 1)
                dve.drain().then_inc(gate_b.freed.sem, 1)
                misc_b.wait_filled(dve, g, 0)
                nc.vector.tensor_copy(lg[:, :, :], bank[7][:, 0:32].rearrange("p (t e) -> p t e", e=N_EXP))
                nc.vector.tensor_tensor(dtp[:, :, :], bank[7][:, 64:320].rearrange("p (t h) -> p t h", h=HEADS),
                                        spread(row("dt_bias"), 1, GT), ALU.add)
                dve.drain().then_inc(misc_b.freed.sem, 1)
                nc.vector.tensor_reduce(lmax[:, :], lg[:, :, :], AX.X, ALU.max)
                nc.vector.tensor_tensor(gt[:, :, :, :], spread(lg[:, :, :], 2, N_EXP), spread(lg[:, :, :], 3, N_EXP),
                                        ALU.is_gt)
                nc.vector.tensor_tensor(eq[:, :, :, :], spread(lg[:, :, :], 2, N_EXP), spread(lg[:, :, :], 3, N_EXP),
                                        ALU.is_equal)
                dve.drain()
                nc.vector.tensor_tensor(lg[:, :, :], lg[:, :, :], spread(lmax[:, :], 2, N_EXP), ALU.subtract)
                nc.vector.tensor_tensor(eq[:, :, :, :], eq[:, :, :, :], spread(lower[:, :, :], 1, GT), ALU.mult)
                dve.drain().then_inc(scores_ready.sem, 1)
                nc.vector.tensor_tensor(gt[:, :, :, :], gt[:, :, :, :], eq[:, :, :, :], ALU.add)
                dve.drain()
                nc.vector.tensor_reduce(rank[:, :, :], gt[:, :, :, :], AX.X, ALU.add)
                dve.drain()
                nc.vector.tensor_scalar(rank[:, :, :], rank[:, :, :], 2.0, None, ALU.is_lt)

                def conv(j):
                    dve.wait_ge(pre_ready.sem, pre_ready.done(g, j))
                    nc.vector.tensor_scalar(xbc[:, j, :], pre[:, j, 0:GROUP], col("conv_w", j * CONV_K), None, ALU.mult)
                    for i in range(1, CONV_K):
                        dve.drain()
                        nc.vector.scalar_tensor_tensor(out=xbc[:, j, :], in0=pre[:, j, i:i + GROUP],
                                                       scalar=col("conv_w", j * CONV_K + i), in1=xbc[:, j, :],
                                                       op0=ALU.mult, op1=ALU.add)
                    nc.vector.tensor_copy(pre[:, j, 0:CONV_K - 1], pre[:, j, GROUP:])
                    dve.drain().then_inc(conv_ready.sem, 1)

                for u in range(L0_UNITS):
                    up_b.wait_filled(dve, g, 6 + u)
                    dve.wait_ge(silu_ready.sem, silu_ready.done(g, u))
                    nc.vector.tensor_tensor(hT[:, u, :], sg[:, u % 2, :], bank[5][:, :], ALU.mult).then_inc(
                        hid_ready.sem, 1)
                    dve.drain().then_inc(up_b.freed.sem, 1)
                    if u < CONV_BLK:
                        conv(u)
                dve.wait_ge(soft_ready.sem, soft_ready.done(g))
                nc.vector.scalar_tensor_tensor(out=dt[:, :, :], in0=dtp[:, :, :], scalar=0.0, in1=dta[:, :, :],
                                               op0=ALU.max, op1=ALU.add)
                nc.vector.tensor_tensor(comb[:, :, :], le[:, :, :], rank[:, :, :], ALU.mult)
                dve.drain()
                nc.vector.scalar_tensor_tensor(out=a[:, :, :], in0=dt[:, :, :], scalar=-1.0,
                                               in1=spread(exp_a[:, :], 1, GT), op0=ALU.mult, op1=ALU.mult)
                nc.vector.tensor_reduce(esum[:, :], comb[:, :, :], AX.X, ALU.add)
                dve.drain().then_inc(a_ready.sem, 1)
                nc.vector.reciprocal(esum[:, :], esum[:, :])
                dve.drain()
                nc.vector.tensor_tensor(comb[:, :, :], comb[:, :, :], spread(esum[:, :], 2, N_EXP), ALU.mult)
                dve.drain()
                for n in range(EARLY):
                    down_add(g, n)
                dve.wait_ge(decay_ready.sem, decay_ready.done(g, 0))
                nc.vector.tensor_tensor(wdt[:, :, :], decay[:, 1, :, :], dt[:, :, :], ALU.mult)
                dve.drain()
                for c in range(NCH):
                    tok = slice(c * P, (c + 1) * P)
                    xs3 = bank[3][:, :].rearrange("p (h e) -> p h e", e=HEAD_P)
                    tok_b.wait_filled(dve, g, 2 * c)
                    for q in range(4):
                        nc.vector.tensor_tensor(
                            xp[:, c % 2, q::4, 8 * q:8 * q + 8],
                            xs3[:, q::4, :], spread(dt[:, c, q::4], 2, HEAD_P), ALU.mult)
                    nc.vector.tensor_tensor(wx[:, :].rearrange("p (h e) -> p h e", e=HEAD_P), xs3,
                                            spread(wdt[:, c, :], 2, HEAD_P), ALU.mult).then_inc(xs_ready.sem, 1)
                    dve.drain().then_inc(tok_b.freed.sem, 1)
                    misc_b.wait_filled(dve, g, bc_job(c))
                    nc.vector.tensor_copy(btok[:, :], bank[7][:, 0:P])
                    nc.vector.tensor_tensor(cbm[:, :], bank[7][:, P:2 * P], before[:, 0, :], ALU.mult)
                    dve.drain().then_inc(bc_ready.sem, 1)
                    dve.drain().then_inc(misc_b.freed.sem, 1)
                    for k in range(HB):
                        n = c * HB + k
                        dve.wait_ge(e_ready.sem, e_ready.done(g, n))
                        dve.wait_ge(strip_done.sem, strip_done.room(g, n))
                        nc.vector.scalar_tensor_tensor(out=m[:, n % 2, :, :], in0=e[:, n % 2, :, :], scalar=1.0,
                                                       in1=spread(cbm[:, :], 1, 4), op0=ALU.min,
                                                       op1=ALU.mult).then_inc(m_ready.sem, 1)
                        if k == 0:
                            misc_b.wait_filled(dve, g, off_job(c))
                            nc.vector.tensor_tensor(yoff[:, :].rearrange("p (h e) -> p h e", e=HEAD_P),
                                                    bank[7][:, :].rearrange("p (h e) -> p h e", e=HEAD_P),
                                                    spread(decay[:, 0, c, :], 2, HEAD_P), ALU.mult).then_inc(
                                yoff_ready.sem, 1)
                            dve.drain().then_inc(misc_b.freed.sem, 1)
                            if c == 0:
                                dve.wait_ge(decay_ready.sem, decay_ready.done(g, 1))
                            st3 = st[:, :].rearrange("p (h e) -> p h e", e=HEAD_P)
                            nc.vector.tensor_tensor(st3, st3, spread(decay[:, 2, c, :], 2, HEAD_P), ALU.mult)
                            dve.drain()
                            tok_b.wait_filled(dve, g, 2 * c + 1)
                            nc.vector.tensor_tensor(st[:, :], st[:, :], bank[3][:, :], ALU.add).then_inc(
                                state_ready.sem, 1)
                            dve.drain().then_inc(tok_b.freed.sem, 1)
                        if k % 4 == 1:
                            down_add(g, EARLY + c * 4 + k // 4)
                        if k == 5 and c > 0:
                            out_stats(g, c - 1)
                        if k == 9 and c > 0:
                            out_add(g, c - 1)
                    y_b.wait_filled(dve, g, c)
                    for k in range(Z_BLK):
                        nc.vector.scalar_tensor_tensor(out=yg[:, k, :], in0=xbc[:, k, tok], scalar=col("D", k),
                                                       in1=bank[2][:, k * P:(k + 1) * P], op0=ALU.mult, op1=ALU.add)
                    dve.drain().then_inc(y_b.freed.sem, 1)
                    if c == 0:
                        dve.wait_ge(z_ready.sem, z_ready.done(g))
                    nc.vector.tensor_tensor(yg[:, :, :], yg[:, :, :], zs[:, :, tok], ALU.mult).then_inc(
                        yg_ready.sem, 1)
                out_stats(g, NCH - 1)
                out_add(g, NCH - 1)
                dve.drain().then_inc(group_done.sem, 1)



class Jobs:

    def __init__(self, mem, banks, trips, order):
        self.banks, self.place = banks, {}
        uses = {}
        for job, b in order:
            self.place[job] = (b, uses.get(b, 0))
            uses[b] = uses.get(b, 0) + 1
        self.filled, self.freed = {}, {}
        for b, n in uses.items():
            self.filled[b] = Event(mem.psum_filled[b], n, base=mem.filled_base[b])
            self.freed[b] = Event(mem.psum_freed[b], n, credit=1, base=mem.freed_base[b])
            mem.filled_base[b] += trips * n
            mem.freed_base[b] += trips * n + 1

    def grant(self, eng):
        for event in self.freed.values():
            event.grant(eng)

    def bank(self, job):
        return self.banks[:, self.place[job][0], :]

    def wait_room(self, pe, trip, job):
        b, n = self.place[job]
        pe.wait_ge(self.freed[b].sem, self.freed[b].room(trip, n))

    def fill(self, last, job):
        last.then_inc(self.filled[self.place[job][0]].sem, 1)

    def wait_filled(self, eng, trip, job):
        b, n = self.place[job]
        eng.wait_ge(self.filled[b].sem, self.filled[b].done(trip, n))

    def free(self, last, job):
        last.then_inc(self.freed[self.place[job][0]].sem, 1)


HB_TILES = SEQ // P
FFN_BLK = 8
BIT_EPS = 1e-8


def layer1(nc, mem, ctx, io):
    sb, ps, sem = mem.scoped(ctx, "l1")
    x, ident, ones, col, row, w = mem.x, mem.ident, mem.ones, mem.col, mem.row, mem.l1

    stats = sb("stats", [P, GT, 6])
    moments = sb("moments", [P, GT, 2])
    rstd = sb("rstd", [P, GT])
    xn = sb("xn", [P, GT, DIM])
    xnT = sb("xnT", [P, DK, GROUP])
    qT = sb("qT", [P, DK, SEQ])
    kT = sb("kT", [P, DK, SEQ])
    v = sb("v", [P, HB_TILES, DIM])
    hT = sb("hT", [P, FFN_BLK, GROUP])
    prob = sb("prob", [P, 2, SEQ])
    pT = sb("pT", [P, HB_TILES, GROUP])
    cT = sb("cT", [P, DK, GROUP])
    nmax = sb("nmax", [P, 2, 1])
    prob_sum = sb("prob_sum", [P, HB_TILES])
    rsum = sb("rsum", [P, GT])
    bias_row = sb("bias_row", [P, DIM])
    wabs = sb("wabs", [P, 2])
    thr = sb("thr", [P, 2, 2])
    below = pT[:, 0:4, :].rearrange("p a n -> p (a n)")
    banks = ps("l1_banks", [P, 8, GROUP])

    order = []
    at = 0
    for hf in range(HALVES):
        names = [("xnT", hf, k) for k in range(DK)] + [("k", hf, k) for k in range(DK)]
        names += [("q", hf, k) for k in range(DK)] + [("v", hf, t) for t in range(GT // 2)]
        names += [("f", hf, k) for k in range(FFN_BLK)] + [("d", hf, t) for t in range(GT // 2)]
        for n in names:
            order.append((n, at % 8))
            at += 1

    def score_jobs(qt):
        return [(("s", qt, i), 2 * (qt % 2) + i) for i in range(2)]

    order += score_jobs(0)
    for qt in range(HB_TILES):
        if qt + 1 < HB_TILES:
            order += score_jobs(qt + 1)
        order += [(("t", qt, i), 4 + i) for i in range(2)]
        if qt % GT == GT - 1:
            hf = qt // GT
            order += [(("c", hf, k), 6 + k) for k in range(DK)]
            order += [(("o", hf, t), 6 + t) for t in range(GT // 2)]
    jobs = Jobs(mem, banks, BATCH, order)

    moments_ready = Event(sem("l1_moments_ready"), HALVES)
    rstd_ready = Event(sem("l1_rstd_ready"), HALVES)
    xn_ready = Event(sem("l1_xn_ready"), HALVES)
    xnT_dve = Event(sem("l1_xnT_dve"), HALVES)
    xnT_act = Event(sem("l1_xnT_act"), HALVES)
    bias_added = Event(sem("l1_bias_added"), HALVES)
    kq_ready = Event(sem("l1_kq_ready"), 4 * HALVES)
    v_ready = Event(sem("l1_v_ready"), 2 * HALVES)
    h_ready = Event(sem("l1_h_ready"), FFN_BLK * HALVES)
    nmax_ready = Event(sem("l1_nmax_ready"), HB_TILES)
    prob_ready = Event(sem("l1_prob_ready"), HB_TILES)
    pT_dve = Event(sem("l1_pT_dve"), HB_TILES)
    pT_act = Event(sem("l1_pT_act"), HB_TILES)
    c_ready = Event(sem("l1_c_ready"), 2 * HALVES)
    weight_sum = sem("l1_weight_sum")
    weight_mean = sem("l1_weight_mean")
    ternary = sem("l1_ternary")

    block = ctx.enter_context(nc.Block())

    @block.sync
    def _(sp):
        mem.load_l2(sp, io)
        mem.load_l3a(sp, io)

    @block.tensor
    def _(pe):
        def mm(out, lhsT, rhs, start=True, stop=True):
            return nc.tensor.matmul(out, lhsT, rhs, start=start, stop=stop)

        pe.wait_ge(weight_sum, 1)
        mm(banks[:, 0, 0:2], ones[:, :], wabs[:, :]).then_inc(weight_mean, 1)
        pe.wait_ge(w.sem, 16 * 4)
        pe.wait_ge(ternary, 1)
        with pe.Fori(0, BATCH) as b:
            for hf in range(HALVES):
                pe.wait_ge(xn_ready.sem, xn_ready.done(b, hf))
                for k in range(DK):
                    jobs.wait_room(pe, b, ("xnT", hf, k))
                    for t in range(GT):
                        last = nc.tensor.transpose(jobs.bank(("xnT", hf, k))[:, t * P:(t + 1) * P],
                                                   xn[:, t, k * P:(k + 1) * P], ident[:, :])
                    jobs.fill(last, ("xnT", hf, k))
                pe.wait_ge(xnT_dve.sem, xnT_dve.done(b, hf))
                pe.wait_ge(xnT_act.sem, xnT_act.done(b, hf))
                for name, base in (("k", DIM), ("q", 0)):
                    for m in range(DK):
                        jobs.wait_room(pe, b, (name, hf, m))
                        for k in range(DK):
                            last = mm(jobs.bank((name, hf, m)), w.qkv[:, k, base + m * P:base + (m + 1) * P],
                                      xnT[:, k, :], k == 0, k == DK - 1)
                        jobs.fill(last, (name, hf, m))
                for t in range(GT // 2):
                    jobs.wait_room(pe, b, ("v", hf, t))
                    for i in range(2):
                        for k in range(DK):
                            last = mm(jobs.bank(("v", hf, t))[:, i * DIM:(i + 1) * DIM],
                                      xnT[:, k, (2 * t + i) * P:(2 * t + i + 1) * P], w.qkv[:, k, 2 * DIM:],
                                      k == 0, k == DK - 1)
                    jobs.fill(last, ("v", hf, t))
                for f in range(FFN_BLK):
                    jobs.wait_room(pe, b, ("f", hf, f))
                    for k in range(DK):
                        last = mm(jobs.bank(("f", hf, f)), w.w1[:, k, f * P:(f + 1) * P], xnT[:, k, :],
                                  k == 0, k == DK - 1)
                    jobs.fill(last, ("f", hf, f))
                pe.wait_ge(h_ready.sem, h_ready.done(b, (hf + 1) * FFN_BLK - 1))
                for t in range(GT // 2):
                    jobs.wait_room(pe, b, ("d", hf, t))
                    for i in range(2):
                        for f in range(FFN_BLK):
                            last = mm(jobs.bank(("d", hf, t))[:, i * DIM:(i + 1) * DIM],
                                      hT[:, f, (2 * t + i) * P:(2 * t + i + 1) * P], w.w2[:, f, :],
                                      f == 0, f == FFN_BLK - 1)
                    jobs.fill(last, ("d", hf, t))

            def scores(qt):
                for i in range(2):
                    jobs.wait_room(pe, b, ("s", qt, i))
                    for k in range(DK):
                        last = mm(jobs.bank(("s", qt, i)), qT[:, k, qt * P:(qt + 1) * P],
                                  kT[:, k, i * GROUP:(i + 1) * GROUP], k == 0, k == DK - 1)
                    jobs.fill(last, ("s", qt, i))

            pe.wait_ge(kq_ready.sem, kq_ready.done(b))
            pe.wait_ge(v_ready.sem, v_ready.done(b))
            scores(0)
            for qt in range(HB_TILES):
                if qt + 1 < HB_TILES:
                    scores(qt + 1)
                pe.wait_ge(prob_ready.sem, prob_ready.done(b, qt))
                for i in range(2):
                    jobs.wait_room(pe, b, ("t", qt, i))
                    for t in range(GT):
                        kt = i * GT + t
                        last = nc.tensor.transpose(jobs.bank(("t", qt, i))[:, t * P:(t + 1) * P],
                                                   prob[:, qt % 2, kt * P:(kt + 1) * P], ident[:, :])
                    jobs.fill(last, ("t", qt, i))
                if qt % GT == GT - 1:
                    hf = qt // GT
                    pe.wait_ge(pT_dve.sem, pT_dve.done(b, qt))
                    pe.wait_ge(pT_act.sem, pT_act.done(b, qt))
                    for m in range(DK):
                        jobs.wait_room(pe, b, ("c", hf, m))
                        for kt in range(HB_TILES):
                            last = mm(jobs.bank(("c", hf, m)), v[:, kt, m * P:(m + 1) * P], pT[:, kt, :],
                                      kt == 0, kt == HB_TILES - 1)
                        jobs.fill(last, ("c", hf, m))
                    pe.wait_ge(c_ready.sem, c_ready.done(b, 2 * hf + 1))
                    for t in range(GT // 2):
                        jobs.wait_room(pe, b, ("o", hf, t))
                        for i in range(2):
                            for k in range(DK):
                                last = mm(jobs.bank(("o", hf, t))[:, i * DIM:(i + 1) * DIM],
                                          cT[:, k, (2 * t + i) * P:(2 * t + i + 1) * P], w.out[:, k, :],
                                          k == 0, k == DK - 1)
                        jobs.fill(last, ("o", hf, t))

    @block.scalar
    def _(act):
        with act.Fori(0, BATCH) as b:
            for hf in range(HALVES):
                half = slice(hf * GROUP, (hf + 1) * GROUP)
                jobs.wait_filled(act, b, ("xnT", hf, 1))
                nc.scalar.activation(xnT[:, 1, :], jobs.bank(("xnT", hf, 1)), ACT.Copy).then_inc(xnT_act.sem, 1)
                jobs.free(act.drain(), ("xnT", hf, 1))
                for name, dst, base in (("k", kT, 2), ("q", qT, 0)):
                    for m in range(DK):
                        jobs.wait_filled(act, b, (name, hf, m))
                        nc.scalar.activation(dst[:, m, half], jobs.bank((name, hf, m)), ACT.Identity,
                                             bias=col("b_qkv", base + m)).then_inc(kq_ready.sem, 1)
                        jobs.free(act.drain(), (name, hf, m))
                for f in range(FFN_BLK):
                    jobs.wait_filled(act, b, ("f", hf, f))
                    nc.scalar.activation(hT[:, f, :], jobs.bank(("f", hf, f)), ACT.Gelu,
                                         bias=col("b1", f)).then_inc(h_ready.sem, 1)
                    jobs.free(act.drain(), ("f", hf, f))

            def turn(qt):
                jobs.wait_filled(act, b, ("t", qt, 1))
                if qt % GT == 0 and qt > 0:
                    jobs.wait_filled(act, b, ("c", qt // GT - 1, 1))
                at = (qt % GT) * P
                nc.scalar.activation(pT[:, GT:, at:at + P],
                                     jobs.bank(("t", qt, 1)).rearrange("p (t q) -> p t q", t=GT),
                                     ACT.Copy).then_inc(pT_act.sem, 1)
                jobs.free(act.drain(), ("t", qt, 1))

            def context(hf):
                for k in range(DK):
                    jobs.wait_filled(act, b, ("c", hf, k))
                    nc.scalar.activation(cT[:, k, :], jobs.bank(("c", hf, k)), ACT.Copy).then_inc(c_ready.sem, 1)
                    jobs.free(act.drain(), ("c", hf, k))

            for qt in range(HB_TILES):
                act.wait_ge(nmax_ready.sem, nmax_ready.done(b, qt))
                if qt >= 2:
                    jobs.wait_filled(act, b, ("t", qt - 2, 1))
                s0 = 2 * (qt % 2)
                nc.scalar.activation(prob[:, qt % 2, :], banks[:, s0:s0 + 2, :].rearrange("p a k -> p (a k)"),
                                     ACT.Exp, bias=nmax[:, qt % 2, :], scale=1.0 / DIM ** 0.5,
                                     accum_out=prob_sum[:, qt:qt + 1])
                act.drain().then_inc(prob_ready.sem, 1)
                for i in range(2):
                    jobs.free(act.drain(), ("s", qt, i))
                if qt > 0:
                    turn(qt - 1)
                if qt % GT == 0 and qt > 0:
                    context(qt // GT - 1)
            turn(HB_TILES - 1)
            context(HALVES - 1)

    @block.gpsimd
    def _(pool):
        pool.wait_ge(mem.row_ready, 16)
        nc.gpsimd.tensor_tensor(bias_row[:, :], row("b_out"), row("b2"), ALU.add)
        pool.drain()
        with pool.Fori(0, BATCH) as b:
            for hf in range(HALVES):
                pool.wait_ge(moments_ready.sem, moments_ready.done(b, hf))
                nc.gpsimd.tensor_tensor(rstd[:, :], moments[:, :, 1], mem.neg_half[:, 0:GT], ALU.pow).then_inc(
                    rstd_ready.sem, 1)
                pool.wait_ge(xn_ready.sem, xn_ready.done(b, hf))
                xg = x[:, bass.ds(b * HB_TILES + hf * GT, GT), :]
                nc.gpsimd.tensor_tensor(xg, xg, spread(bias_row[:, :], 1, GT), ALU.add).then_inc(bias_added.sem, 1)

    @block.vector
    def _(dve):
        jobs.grant(dve)
        dve.wait_ge(w.sem, 16 * 4)
        for i, part in enumerate((w.w1, w.w2)):
            flat = part.rearrange("p a n -> p (a n)")
            nc.vector.tensor_reduce(wabs[:, i:i + 1], flat, AX.X, ALU.add, apply_absolute_value=True)
        dve.drain().then_inc(weight_sum, 1)
        dve.wait_ge(weight_mean, 1)
        n_w = DIM * FFN_BLK * P
        nc.vector.tensor_scalar(thr[:, 0, :], banks[:, 0, 0:2], 1.0 / n_w, BIT_EPS, ALU.mult, ALU.max)
        dve.drain()
        nc.vector.tensor_scalar(thr[:, 1, :], thr[:, 0, :], -0.5, None, ALU.mult)
        dve.drain()
        nc.vector.tensor_scalar(thr[:, 0, :], thr[:, 0, :], 0.5, None, ALU.mult)
        dve.drain()
        for i, part in enumerate((w.w1, w.w2)):
            flat = part.rearrange("p a n -> p (a n)")
            nc.vector.tensor_scalar(below[:, :], flat, thr[:, 1, i:i + 1], None, ALU.is_lt)
            dve.drain()
            nc.vector.scalar_tensor_tensor(out=flat, in0=flat, scalar=thr[:, 0, i:i + 1], in1=below[:, :],
                                           op0=ALU.is_gt, op1=ALU.subtract)
            dve.drain()
        dve.drain().then_inc(ternary, 1)
        dve.wait_ge(mem.row_ready, 16)
        with dve.Fori(0, BATCH) as b:
            for hf in range(HALVES):
                t0 = b * HB_TILES + hf * GT
                for t in range(GT):
                    nc.vector.bn_stats(stats[:, t, :], x[:, t0 + t, :])
                dve.drain()
                for t in range(GT):
                    nc.vector.bn_aggr(moments[:, t, :], stats[:, t, :])
                dve.drain()
                nc.vector.tensor_scalar(moments[:, :, 1], moments[:, :, 1], 1e-5, None, ALU.add).then_inc(
                    moments_ready.sem, 1)
                dve.wait_ge(rstd_ready.sem, rstd_ready.done(b, hf))
                for t in range(GT):
                    last = nc.vector.tensor_scalar(xn[:, t, :], x[:, t0 + t, :], moments[:, t, 0:1],
                                                   rstd[:, t:t + 1], ALU.subtract, ALU.mult)
                last.then_inc(xn_ready.sem, 1)
                jobs.wait_filled(dve, b, ("xnT", hf, 0))
                nc.vector.tensor_copy(xnT[:, 0, :], jobs.bank(("xnT", hf, 0))).then_inc(xnT_dve.sem, 1)
                jobs.free(dve.drain(), ("xnT", hf, 0))
                for t in range(GT // 2):
                    jobs.wait_filled(dve, b, ("v", hf, t))
                    at = hf * GT + 2 * t
                    nc.vector.tensor_tensor(v[:, at:at + 2, :],
                                            jobs.bank(("v", hf, t)).rearrange("p (t d) -> p t d", t=2),
                                            spread(row("b_v"), 1, 2), ALU.add).then_inc(v_ready.sem, 1)
                    jobs.free(dve.drain(), ("v", hf, t))
                dve.wait_ge(bias_added.sem, bias_added.done(b, hf))
                for t in range(GT // 2):
                    jobs.wait_filled(dve, b, ("d", hf, t))
                    xt = x[:, bass.ds(t0 + 2 * t, 2), :]
                    last = nc.vector.tensor_tensor(xt, xt, jobs.bank(("d", hf, t)).rearrange(
                        "p (t d) -> p t d", t=2), ALU.add)
                    jobs.free(last, ("d", hf, t))

            def turn(qt):
                jobs.wait_filled(dve, b, ("t", qt, 0))
                if qt % GT == 0 and qt > 0:
                    jobs.wait_filled(dve, b, ("c", qt // GT - 1, 1))
                at = (qt % GT) * P
                nc.vector.tensor_copy(pT[:, 0:GT, at:at + P],
                                      jobs.bank(("t", qt, 0)).rearrange("p (t q) -> p t q", t=GT)).then_inc(
                    pT_dve.sem, 1)
                jobs.free(dve.drain(), ("t", qt, 0))

            def project(hf):
                dve.wait_ge(prob_ready.sem, prob_ready.done(b, hf * GT + GT - 1))
                nc.vector.reciprocal(rsum[:, :], prob_sum[:, hf * GT:(hf + 1) * GT])
                dve.drain()
                for t in range(GT // 2):
                    jobs.wait_filled(dve, b, ("o", hf, t))
                    for i in range(2):
                        xt = x[:, b * HB_TILES + hf * GT + 2 * t + i, :]
                        last = nc.vector.scalar_tensor_tensor(
                            out=xt, in0=jobs.bank(("o", hf, t))[:, i * DIM:(i + 1) * DIM],
                            scalar=rsum[:, 2 * t + i:2 * t + i + 1], in1=xt, op0=ALU.mult, op1=ALU.add)
                    jobs.free(last, ("o", hf, t))

            for qt in range(HB_TILES):
                jobs.wait_filled(dve, b, ("s", qt, 1))
                s0 = 2 * (qt % 2)
                nc.vector.tensor_reduce(nmax[:, qt % 2, :], banks[:, s0:s0 + 2, :].rearrange("p a k -> p (a k)"),
                                        AX.X, ALU.max, negate=True)
                dve.drain()
                nc.vector.tensor_scalar(nmax[:, qt % 2, :], nmax[:, qt % 2, :], 1.0 / DIM ** 0.5, None,
                                        ALU.mult).then_inc(nmax_ready.sem, 1)
                if qt > 0:
                    turn(qt - 1)
                if qt % GT == 0 and qt > 0:
                    project(qt // GT - 1)
            turn(HB_TILES - 1)
            project(HALVES - 1)
            dve.drain()



QH = 704
Q_BLK = -(-QH // P)
ZERO_POINT = 128.0
P_START = 1.0 - 1e30


def q_rows(u):
    return min(P, QH - u * P)


def layer2(nc, mem, ctx, io):
    sb, ps, sem = mem.scoped(ctx, "l2")
    x, ident, ones, col, row, w = mem.x, mem.ident, mem.ones, mem.col, mem.row, mem.l2

    stats = sb("stats", [P, GT, 6])
    moments = sb("moments", [P, 2, GT, 2])
    rstd = sb("rstd", [P, 2, GT])
    xn = sb("xn", [P, GT, DIM])
    xnT = sb("xnT", [P, DK, GROUP])
    x2T = sb("x2T", [P, DK, 1 + GROUP])
    keep = sb("keep", [P, 3, DK])
    part = sb("part", [P, DK, GROUP])
    x2 = part[:, :, :].rearrange("p a n -> p (a n)").rearrange("p (t d) -> p t d", t=GT)
    q = part
    mixed = sb("mixed", [P, 3, DK, GROUP])
    wdec = sb("wdec", [P, DK])
    kk = sb("kk", [P, DK, GROUP])
    vv = sb("vv", [P, DK, GROUP])
    rr = sb("rr", [P, DK, GROUP])
    pmax = sb("pmax", [P, DK, 1 + GROUP])
    num = sb("num", [P, DK, 1 + GROUP])
    den = sb("den", [P, DK, 1 + GROUP])
    e1 = sb("e1", [P, DK, GROUP])
    e2 = sb("e2", [P, DK, GROUP])
    c1, c2, c2v = mixed[:, 0, :, :], mixed[:, 1, :, :], mixed[:, 2, :, :]
    e2v = xn[:, :, :].rearrange("p t d -> p (t d)").rearrange("p (a n) -> p a n", a=DK)
    rw = c2v
    sg = sb("sg", [P, 2, GROUP])
    hT = sb("hT", [P, Q_BLK, GROUP])
    banks = ps("l2_banks", [P, 8, GROUP])

    names = [("xnT", k) for k in range(DK)] + [("x2T", k) for k in range(DK)]
    names += [(n, k) for n in ("k", "v", "r") for k in range(DK)]
    for u in range(Q_BLK):
        names += [("g", u), ("u", u)]
    names += [("o", t) for t in range(GT // 2)]
    jobs = Jobs(mem, banks, BATCH * HALVES, [(n, i % 8) for i, n in enumerate(names)])

    moments_ready = Event(sem("l2_moments_ready"), 2)
    rstd_ready = Event(sem("l2_rstd_ready"), 2)
    xn_ready = Event(sem("l2_xn_ready"), 2)
    xT_dve = Event(sem("l2_xT_dve"), 2)
    xT_act = Event(sem("l2_xT_act"), 2)
    skip_added = Event(sem("l2_skip_added"), 1)
    mix_ready = Event(sem("l2_mix_ready"), 3)
    kvr_ready = Event(sem("l2_kvr_ready"), 6)
    max_ready = Event(sem("l2_max_ready"), 1)
    q_ready = Event(sem("l2_q_ready"), 1)
    arg_dve = Event(sem("l2_arg_dve"), 2)
    arg_pool = Event(sem("l2_arg_pool"), 2)
    exp_ready = Event(sem("l2_exp_ready"), 4)
    e2v_ready = Event(sem("l2_e2v_ready"), 1)
    rw_ready = Event(sem("l2_rw_ready"), 1)
    silu_ready = Event(sem("l2_silu_ready"), Q_BLK)
    h_ready = Event(sem("l2_h_ready"), Q_BLK, credit=2)
    weights_ready = sem("l2_weights_ready")
    decay_exp = sem("l2_decay_exp")
    reset_done = Event(sem("l2_reset_done"), 1)

    block = ctx.enter_context(nc.Block())

    @block.sync
    def _(sp):
        mem.load_l3b(sp, io)

    @block.tensor
    def _(pe):
        def mm(out, lhsT, rhs, start=True, stop=True):
            return nc.tensor.matmul(out, lhsT, rhs, start=start, stop=stop)

        def turn(g, name, src):
            for k in range(DK):
                jobs.wait_room(pe, g, (name, k))
                for t in range(GT):
                    last = nc.tensor.transpose(jobs.bank((name, k))[:, t * P:(t + 1) * P],
                                               src[:, t, k * P:(k + 1) * P], ident[:, :])
                jobs.fill(last, (name, k))

        pe.wait_ge(weights_ready, 1)
        with pe.Fori(0, BATCH) as b:
            with pe.Fori(0, HALVES) as half:
                g = b * HALVES + half
                pe.wait_ge(xn_ready.sem, xn_ready.done(g, 0))
                turn(g, "xnT", xn)
                pe.wait_ge(xn_ready.sem, xn_ready.done(g, 1))
                turn(g, "x2T", x2)
                for i, (name, m) in enumerate((("k", w.k), ("v", w.v), ("r", w.r))):
                    pe.wait_ge(mix_ready.sem, mix_ready.done(g, i))
                    for n in range(DK):
                        jobs.wait_room(pe, g, (name, n))
                        for k in range(DK):
                            last = mm(jobs.bank((name, n)), m[:, k, n * P:(n + 1) * P], mixed[:, i, k, :],
                                      k == 0, k == DK - 1)
                        jobs.fill(last, (name, n))
                for u in range(Q_BLK):
                    rows = q_rows(u)
                    for name, m in (("g", w.gate), ("u", w.up)):
                        jobs.wait_room(pe, g, (name, u))
                        for k in range(DK):
                            last = mm(jobs.bank((name, u))[0:rows, :], m[:, k, u * P:u * P + rows], xnT[:, k, :],
                                      k == 0, k == DK - 1)
                        jobs.fill(last, (name, u))
                pe.wait_ge(h_ready.sem, h_ready.done(g))
                pe.wait_ge(rw_ready.sem, rw_ready.done(g))
                for t in range(GT // 2):
                    jobs.wait_room(pe, g, ("o", t))
                    for i in range(2):
                        out = jobs.bank(("o", t))[:, i * DIM:(i + 1) * DIM]
                        tok = slice((2 * t + i) * P, (2 * t + i + 1) * P)
                        for u in range(Q_BLK):
                            rows = q_rows(u)
                            mm(out, hT[0:rows, u, tok], w.down[0:rows, u, :], u == 0, False)
                        for k in range(DK):
                            last = mm(out, rw[:, k, tok], w.o[:, k, :], False, k == DK - 1)
                    jobs.fill(last, ("o", t))

    @block.scalar
    def _(act):
        act.wait_ge(mem.col_ready, 16)
        nc.scalar.activation(wdec[:, :], mem.cols[:, COL_AT["time_decay"]:COL_AT["time_decay"] + DK],
                             ACT.Exp).then_inc(decay_exp, 1)
        with act.Fori(0, BATCH) as b:
            with act.Fori(0, HALVES) as half:
                g = b * HALVES + half
                jobs.wait_filled(act, g, ("xnT", 1))
                nc.scalar.activation(xnT[:, 1, :], jobs.bank(("xnT", 1)), ACT.Copy).then_inc(xT_act.sem, 1)
                jobs.free(act.drain(), ("xnT", 1))
                jobs.wait_filled(act, g, ("x2T", 1))
                act.wait_ge(reset_done.sem, reset_done.done(b))
                nc.scalar.activation(x2T[:, 1, 1:], jobs.bank(("x2T", 1)), ACT.Identity, bias=col("ln_bias", 1),
                                     scale=col("ln_scale", 1)).then_inc(xT_act.sem, 1)
                jobs.free(act.drain(), ("x2T", 1))
                for name, dst in (("k", kk), ("v", vv)):
                    for n in range(DK):
                        jobs.wait_filled(act, g, (name, n))
                        nc.scalar.activation(dst[:, n, :], jobs.bank((name, n)), ACT.Copy).then_inc(kvr_ready.sem, 1)
                        jobs.free(act.drain(), (name, n))
                for n in range(DK):
                    jobs.wait_filled(act, g, ("r", n))
                    nc.scalar.activation(rr[:, n, :], jobs.bank(("r", n)), ACT.Sigmoid).then_inc(kvr_ready.sem, 1)
                    jobs.free(act.drain(), ("r", n))
                for buf, event, n in ((c1, arg_dve, 0), (c2, arg_pool, 0), (e2, arg_dve, 1), (e1, arg_pool, 1)):
                    act.wait_ge(event.sem, event.done(g, n))
                    nc.scalar.activation(buf[:, :, :], buf[:, :, :], ACT.Exp).then_inc(exp_ready.sem, 1)
                for u in range(Q_BLK):
                    rows = q_rows(u)
                    jobs.wait_filled(act, g, ("g", u))
                    act.wait_ge(h_ready.sem, h_ready.room(g, u))
                    nc.scalar.activation(sg[0:rows, u % 2, :], jobs.bank(("g", u))[0:rows, :], ACT.Silu,
                                         scale=col("s_gate", u)[0:rows, :]).then_inc(silu_ready.sem, 1)
                    jobs.free(act.drain(), ("g", u))

    @block.gpsimd
    def _(pool):
        with pool.Fori(0, BATCH) as b:
            with pool.Fori(0, HALVES) as half:
                g = b * HALVES + half
                for i in range(2):
                    pool.wait_ge(moments_ready.sem, moments_ready.done(g, i))
                    nc.gpsimd.tensor_tensor(rstd[:, i, :], moments[:, i, :, 1], mem.neg_half[:, 0:GT],
                                            ALU.pow).then_inc(rstd_ready.sem, 1)
                    if i == 1:
                        xg = x[:, bass.ds(g * GT, GT), :]
                        nc.gpsimd.tensor_tensor(xg, xg, xn[:, :, :], ALU.add).then_inc(skip_added.sem, 1)
                pool.wait_ge(kvr_ready.sem, kvr_ready.done(g, 3))
                pool.wait_ge(max_ready.sem, max_ready.done(g))
                nc.gpsimd.tensor_tensor(c2[:, :, :], kk[:, :, :], pmax[:, :, 1:], ALU.subtract).then_inc(
                    arg_pool.sem, 1)
                pool.wait_ge(q_ready.sem, q_ready.done(g))
                nc.gpsimd.tensor_tensor(e1[:, :, :], pmax[:, :, 0:GROUP], q[:, :, :], ALU.subtract).then_inc(
                    arg_pool.sem, 1)
                pool.wait_ge(exp_ready.sem, exp_ready.done(g, 2))
                nc.gpsimd.tensor_tensor(e2v[:, :, :], e2[:, :, :], vv[:, :, :], ALU.mult).then_inc(e2v_ready.sem, 1)

    @block.vector
    def _(dve):
        jobs.grant(dve)
        h_ready.grant(dve)
        dve.wait_ge(w.sem, 16 * 8)
        for part_ in (w.gate, w.up):
            nc.vector.tensor_scalar(part_, part_.bitcast(I32), ZERO_POINT, None, ALU.subtract)
        for lo, hi, rows in ((0, Q_BLK - 1, P), (Q_BLK - 1, Q_BLK, q_rows(Q_BLK - 1))):
            d = w.down[0:rows, lo:hi, :]
            nc.vector.tensor_scalar(d, d.bitcast(I32), ZERO_POINT, None, ALU.subtract)
        dve.wait_ge(mem.row_ready, 16)
        dve.drain()
        for lo, hi, rows in ((0, Q_BLK - 1, P), (Q_BLK - 1, Q_BLK, q_rows(Q_BLK - 1))):
            d = w.down[0:rows, lo:hi, :]
            nc.vector.tensor_tensor(d, d, spread(row("s_down"), 1, hi - lo)[0:rows], ALU.mult)
        dve.drain().then_inc(weights_ready, 1)
        mix0 = COL_AT["mix_k"]
        nc.vector.tensor_scalar(keep[:, :, :].rearrange("p a b -> p (a b)"), mem.cols[:, mix0:mix0 + 3 * DK],
                                -1.0, 1.0, ALU.mult, ALU.add)
        dve.wait_ge(decay_exp, 1)
        nc.vector.tensor_scalar(wdec[:, :], wdec[:, :], -1.0, None, ALU.mult)
        dve.drain()
        with dve.Fori(0, BATCH) as b:
            nc.vector.memset(x2T[:, :, 0:1], 0.0)
            nc.vector.memset(pmax[:, :, 0:1], P_START)
            nc.vector.memset(num[:, :, 0:1], 0.0)
            nc.vector.memset(den[:, :, 0:1], 0.0)
            dve.drain().then_inc(reset_done.sem, 1)
            with dve.Fori(0, HALVES) as half:
                g = b * HALVES + half
                for i in range(2):
                    for t in range(GT):
                        nc.vector.bn_stats(stats[:, t, :], x[:, g * GT + t, :] if i == 0 else xn[:, t, :])
                    dve.drain()
                    for t in range(GT):
                        nc.vector.bn_aggr(moments[:, i, t, :], stats[:, t, :])
                    dve.drain()
                    nc.vector.tensor_scalar(moments[:, i, :, 1], moments[:, i, :, 1], 1e-5, None,
                                            ALU.add).then_inc(moments_ready.sem, 1)
                    dve.wait_ge(rstd_ready.sem, rstd_ready.done(g, i))
                    for t in range(GT):
                        src, dst = (x[:, g * GT + t, :], xn) if i == 0 else (xn[:, t, :], x2)
                        last = nc.vector.tensor_scalar(dst[:, t, :], src, moments[:, i, t, 0:1],
                                                       rstd[:, i, t:t + 1], ALU.subtract, ALU.mult)
                    last.then_inc(xn_ready.sem, 1)
                    dve.drain()
                jobs.wait_filled(dve, g, ("xnT", 0))
                nc.vector.tensor_copy(xnT[:, 0, :], jobs.bank(("xnT", 0))).then_inc(xT_dve.sem, 1)
                jobs.free(dve.drain(), ("xnT", 0))
                jobs.wait_filled(dve, g, ("x2T", 0))
                nc.vector.tensor_scalar(x2T[:, 0, 1:], jobs.bank(("x2T", 0)), col("ln_scale", 0), col("ln_bias", 0),
                                        ALU.mult, ALU.add).then_inc(xT_dve.sem, 1)
                jobs.free(dve.drain(), ("x2T", 0))
                dve.wait_ge(xT_act.sem, xT_act.done(g))
                for i, name in enumerate(("mix_k", "mix_v", "mix_r")):
                    for k in range(DK):
                        nc.vector.tensor_scalar(part[:, k, :], x2T[:, k, 0:GROUP], keep[:, i, k:k + 1], None, ALU.mult)
                    dve.drain()
                    for k in range(DK):
                        last = nc.vector.scalar_tensor_tensor(out=mixed[:, i, k, :], in0=x2T[:, k, 1:],
                                                              scalar=col(name, k), in1=part[:, k, :],
                                                              op0=ALU.mult, op1=ALU.add)
                    last.then_inc(mix_ready.sem, 1)
                    dve.drain()
                nc.vector.tensor_copy(x2T[:, :, 0:1], x2T[:, :, GROUP:])
                dve.wait_ge(kvr_ready.sem, kvr_ready.done(g, 1))
                for k in range(DK):
                    nc.vector.tensor_tensor_scan(pmax[:, k, 1:], wdec[:, k:k + 1].broadcast_to([P, GROUP]), kk[:, k, :],
                                                 initial=pmax[:, k, 0:1], op0=ALU.add, op1=ALU.max)
                dve.drain().then_inc(max_ready.sem, 1)
                for k in range(DK):
                    nc.vector.scalar_tensor_tensor(out=c1[:, k, :], in0=pmax[:, k, 0:GROUP], scalar=wdec[:, k:k + 1],
                                                   in1=pmax[:, k, 1:], op0=ALU.add, op1=ALU.subtract)
                dve.drain().then_inc(arg_dve.sem, 1)
                for k in range(DK):
                    nc.vector.scalar_tensor_tensor(out=q[:, k, :], in0=kk[:, k, :], scalar=col("time_first", k),
                                                   in1=pmax[:, k, 0:GROUP], op0=ALU.add, op1=ALU.max)
                dve.drain().then_inc(q_ready.sem, 1)
                for k in range(DK):
                    nc.vector.scalar_tensor_tensor(out=e2[:, k, :], in0=kk[:, k, :], scalar=col("time_first", k),
                                                   in1=q[:, k, :], op0=ALU.add, op1=ALU.subtract)
                dve.drain().then_inc(arg_dve.sem, 1)
                dve.wait_ge(kvr_ready.sem, kvr_ready.done(g))
                dve.wait_ge(exp_ready.sem, exp_ready.done(g, 1))
                nc.vector.tensor_tensor(c2v[:, :, :], c2[:, :, :], vv[:, :, :], ALU.mult)
                for k in range(DK):
                    nc.vector.tensor_tensor_scan(den[:, k, 1:], c1[:, k, :], c2[:, k, :], initial=den[:, k, 0:1],
                                                 op0=ALU.mult, op1=ALU.add)
                dve.drain()
                for k in range(DK):
                    nc.vector.tensor_tensor_scan(num[:, k, 1:], c1[:, k, :], c2v[:, k, :], initial=num[:, k, 0:1],
                                                 op0=ALU.mult, op1=ALU.add)
                dve.drain()
                dve.wait_ge(exp_ready.sem, exp_ready.done(g, 3))
                nc.vector.tensor_tensor(c1[:, :, :], e1[:, :, :], den[:, :, 0:GROUP], ALU.mult)
                dve.drain()
                nc.vector.tensor_tensor(c2v[:, :, :], e1[:, :, :], num[:, :, 0:GROUP], ALU.mult)
                nc.vector.tensor_tensor(c1[:, :, :], c1[:, :, :], e2[:, :, :], ALU.add)
                dve.drain()
                nc.vector.scalar_tensor_tensor(out=c2[:, :, :], in0=c1[:, :, :], scalar=0.0, in1=c1[:, :, :],
                                               op0=ALU.is_equal, op1=ALU.add)
                dve.wait_ge(e2v_ready.sem, e2v_ready.done(g))
                nc.vector.tensor_tensor(c2v[:, :, :], c2v[:, :, :], e2v[:, :, :], ALU.add)
                dve.drain()
                nc.vector.reciprocal(c2[:, :, :], c2[:, :, :])
                nc.vector.scalar_tensor_tensor(out=c2v[:, :, :], in0=c1[:, :, :], scalar=0.0, in1=c2v[:, :, :],
                                               op0=ALU.not_equal, op1=ALU.mult)
                dve.drain()
                nc.vector.tensor_tensor(c2v[:, :, :], c2v[:, :, :], c2[:, :, :], ALU.mult)
                for s in (pmax, num, den):
                    nc.vector.tensor_copy(s[:, :, 0:1], s[:, :, GROUP:])
                dve.drain()
                nc.vector.tensor_tensor(rw[:, :, :], c2v[:, :, :], rr[:, :, :], ALU.mult).then_inc(rw_ready.sem, 1)
                for u in range(Q_BLK):
                    rows = q_rows(u)
                    jobs.wait_filled(dve, g, ("u", u))
                    dve.wait_ge(silu_ready.sem, silu_ready.done(g, u))
                    nc.vector.scalar_tensor_tensor(out=hT[0:rows, u, :], in0=jobs.bank(("u", u))[0:rows, :],
                                                   scalar=col("s_up", u)[0:rows, :], in1=sg[0:rows, u % 2, :],
                                                   op0=ALU.mult, op1=ALU.mult).then_inc(h_ready.sem, 1)
                    jobs.free(dve.drain(), ("u", u))
                dve.wait_ge(skip_added.sem, skip_added.done(g))
                for t in range(GT // 2):
                    jobs.wait_filled(dve, g, ("o", t))
                    xt = x[:, bass.ds(g * GT + 2 * t, 2), :]
                    last = nc.vector.tensor_tensor(xt, xt, jobs.bank(("o", t)).rearrange("p (t d) -> p t d", t=2),
                                                   ALU.add)
                    jobs.free(last, ("o", t))
                dve.drain()



L3_EPS = 1e-12
LIMIT = 7.0
ALPHA = 1.702
I_BLK = 2
CM_BLK = 8


def layer3(nc, mem, ctx, io):
    sb, ps, sem = mem.scoped(ctx, "l3")
    x, ident, ones, col, row, w = mem.x, mem.ident, mem.ones, mem.col, mem.row, mem.l3

    stats = sb("stats", [P, GT, 6])
    moments = sb("moments", [P, GT, 2])
    rstd = sb("rstd", [P, GT])
    xn = sb("xn", [P, HB_TILES, DIM])
    tmp = sb("tmp", [P, GT, DIM])
    xnT = sb("xnT", [P, DK, SEQ])
    xlT = sb("xlT", [P, DK, 1 + GROUP])
    mixT = sb("mixT", [P, DK, GROUP])
    dec = sb("dec", [P, DK, SEQ])
    junk = sb("junk", [P, GROUP])
    toT = sb("toT", [P, DK, GROUP])
    g_ = sb("g_", [P, I_BLK, GROUP])
    s_ = sb("s_", [P, I_BLK, GROUP])
    u_ = sb("u_", [P, I_BLK, GROUP])
    gs = sb("gs", [P, I_BLK, GROUP])
    hT = sb("hT", [P, 2, I_BLK, GROUP])
    x2 = sb("x2", [P, GT, DIM])
    xcT = sb("xcT", [P, DK, 1 + GROUP])
    rc = sb("rc", [P, GT, DIM])
    lg = sb("lg", [P, GT, N_EXP])
    lmax = sb("lmax", [P, GT])
    le = sb("le", [P, GT, N_EXP])
    pairs = GT * N_EXP * N_EXP
    gt, eq = [junk[:, i * pairs:(i + 1) * pairs].rearrange("p (t e f) -> p t e f", e=N_EXP, f=N_EXP) for i in range(2)]
    rank = sb("rank", [P, GT, N_EXP])
    esum = sb("esum", [P, GT])
    comb = sb("comb", [P, HB_TILES, N_EXP])
    combT = sb("combT", [N_EXP, GROUP])
    vm = sb("vm", [P, HALVES, DK])
    vmix = sb("vmix", [P, DK])
    ucol = sb("ucol", [P, DK])
    keep = sb("keep", [P, DK])
    kcT = mem.region_c[:, 0:CM_BLK * GROUP].rearrange("p (a n) -> p a n", a=CM_BLK)
    rT = mem.region_c[:, CM_BLK * GROUP:CM_BLK * GROUP + DK * SEQ].rearrange("p (a n) -> p a n", a=DK)
    banks = ps("l3_banks", [P, 8, GROUP])

    N_UNITS = HALVES * N_EXP
    PLAN = [("norms", 0), ("norms", 1), ("hidden", 0)]
    extra = {3: [("time_row", 0)], 4: [("turn", 0)], 7: [("bias", 0)], 9: [("channel", 0)],
             10: [("turn", 1)], 14: [("channel", 1)], 15: [("bias", 1)]}
    for n in range(1, N_UNITS + 1):
        if n < N_UNITS:
            PLAN.append(("hidden", n))
        PLAN.append(("down", n - 1))
        PLAN += extra.get(n - 1, [])

    names = []
    for step, n in PLAN:
        if step == "norms":
            names += [("xnT", n, k) for k in range(DK)] + [("route", n)] + [("xl", n, k) for k in range(DK)]
            names += [("v", n, k) for k in range(DK)] + [("r", n, k) for k in range(DK)]
        elif step == "hidden":
            for m in range(I_BLK):
                names += [("g", n, m), ("u", n, m)]
        elif step == "down":
            names += [("d", n, t) for t in range(GT // 2)]
        elif step == "time_row":
            names += ["time_row"]
        elif step == "turn":
            names += [("to", n, t) for t in range(GT // 2)]
        elif step == "bias":
            names += [("ct", n)] + [("db", n, t) for t in range(GT // 2)]
        else:
            names += [("xc", n, k) for k in range(DK)] + [("rc", n, t) for t in range(GT // 2)]
            names += [("kc", n, f) for f in range(CM_BLK)] + [("vc", n, t) for t in range(GT // 2)]
    jobs = Jobs(mem, banks, BATCH, [(n, i % 8) for i, n in enumerate(names)])

    NORMS = 3 * HALVES + 2 * HALVES
    moments_ready = Event(sem("l3_moments_ready"), NORMS)
    rstd_ready = Event(sem("l3_rstd_ready"), NORMS)
    xn_ready = Event(sem("l3_xn_ready"), HALVES)
    xl_ready = Event(sem("l3_xl_ready"), HALVES)
    xnT_dve = Event(sem("l3_xnT_dve"), HALVES)
    xnT_act = Event(sem("l3_xnT_act"), HALVES)
    xlT_dve = Event(sem("l3_xlT_dve"), HALVES)
    xlT_act = Event(sem("l3_xlT_act"), HALVES)
    mix_ready = Event(sem("l3_mix_ready"), HALVES)
    r_ready = Event(sem("l3_r_ready"), HALVES * DK)
    logits_ready = Event(sem("l3_logits_ready"), HALVES)
    exp_ready = Event(sem("l3_exp_ready"), HALVES)
    comb_ready = Event(sem("l3_comb_ready"), HALVES)
    g_ready = Event(sem("l3_g_ready"), N_UNITS * I_BLK)
    u_ready = Event(sem("l3_u_ready"), N_UNITS * I_BLK)
    s_ready = Event(sem("l3_s_ready"), N_UNITS * I_BLK)
    gs_ready = Event(sem("l3_gs_ready"), N_UNITS * I_BLK)
    h_ready = Event(sem("l3_h_ready"), N_UNITS)
    vmix_ready = Event(sem("l3_vmix_ready"), 1)
    u_row_ready = Event(sem("l3_u_row_ready"), 1)
    to_ready = Event(sem("l3_to_ready"), HALVES)
    xc_ready = Event(sem("l3_xc_ready"), HALVES)
    xcT_dve = Event(sem("l3_xcT_dve"), HALVES)
    xcT_act = Event(sem("l3_xcT_act"), HALVES)
    rc_ready = Event(sem("l3_rc_ready"), HALVES * GT // 2)
    relu_ready = Event(sem("l3_relu_ready"), HALVES * CM_BLK)
    kc_ready = Event(sem("l3_kc_ready"), HALVES * CM_BLK)
    combT_ready = Event(sem("l3_combT_ready"), HALVES)
    reset_done = Event(sem("l3_reset_done"), 1)
    steps_ready = sem("l3_steps_ready")
    dec_ready = sem("l3_dec_ready")

    block = ctx.enter_context(nc.Block())

    @block.tensor
    def _(pe):
        def mm(out, lhsT, rhs, start=True, stop=True):
            return nc.tensor.matmul(out, lhsT, rhs, start=start, stop=stop)

        def turn(b, name, hf, src, t0):
            for k in range(DK):
                jobs.wait_room(pe, b, (name, hf, k))
                for t in range(GT):
                    last = nc.tensor.transpose(jobs.bank((name, hf, k))[:, t * P:(t + 1) * P],
                                               src[:, t0 + t, k * P:(k + 1) * P], ident[:, :])
                jobs.fill(last, (name, hf, k))

        def norms(b, hf):
            pe.wait_ge(xn_ready.sem, xn_ready.done(b, hf))
            turn(b, "xnT", hf, xn, hf * GT)
            pe.wait_ge(xnT_dve.sem, xnT_dve.done(b, hf))
            pe.wait_ge(xnT_act.sem, xnT_act.done(b, hf))
            jobs.wait_room(pe, b, ("route", hf))
            for t in range(GT):
                at = (hf * GT + t) * P
                for k in range(DK):
                    last = mm(jobs.bank(("route", hf))[:, N_EXP * t:N_EXP * (t + 1)], xnT[:, k, at:at + P],
                              w.router[:, k, :], k == 0, k == DK - 1)
            jobs.fill(last, ("route", hf))
            pe.wait_ge(xl_ready.sem, xl_ready.done(b, hf))
            turn(b, "xl", hf, tmp, 0)
            pe.wait_ge(xlT_dve.sem, xlT_dve.done(b, hf))
            pe.wait_ge(xlT_act.sem, xlT_act.done(b, hf))
            for name, m, src in (("v", w.v, xlT[:, :, 1:]), ("r", w.r, mixT)):
                if name == "r":
                    pe.wait_ge(mix_ready.sem, mix_ready.done(b, hf))
                for n in range(DK):
                    jobs.wait_room(pe, b, (name, hf, n))
                    for k in range(DK):
                        last = mm(jobs.bank((name, hf, n)), m[:, k, n * P:(n + 1) * P], src[:, k, :],
                                  k == 0, k == DK - 1)
                    jobs.fill(last, (name, hf, n))

        def hidden(b, n):
            hf, e = n // N_EXP, n % N_EXP
            for m in range(I_BLK):
                for name, base in (("g", 0), ("u", I_BLK * P)):
                    jobs.wait_room(pe, b, (name, n, m))
                    c0 = base + m * P
                    for k in range(DK):
                        last = mm(jobs.bank((name, n, m)), w.gate_up[:, e * DK + k, c0:c0 + P],
                                  xnT[:, k, hf * GROUP:(hf + 1) * GROUP], k == 0, k == DK - 1)
                    jobs.fill(last, (name, n, m))

        def down(b, n):
            e = n % N_EXP
            pe.wait_ge(h_ready.sem, h_ready.done(b, n))
            for t in range(GT // 2):
                jobs.wait_room(pe, b, ("d", n, t))
                for i in range(2):
                    at = (2 * t + i) * P
                    for m in range(I_BLK):
                        last = mm(jobs.bank(("d", n, t))[:, i * DIM:(i + 1) * DIM], hT[:, n % 2, m, at:at + P],
                                  w.down[:, e * I_BLK + m, :], m == 0, m == I_BLK - 1)
                jobs.fill(last, ("d", n, t))

        def time_row(b, _):
            pe.wait_ge(vmix_ready.sem, vmix_ready.done(b))
            jobs.wait_room(pe, b, "time_row")
            for n in range(DK):
                for k in range(DK):
                    last = mm(jobs.bank("time_row")[:, n:n + 1], w.o[:, k, n * P:(n + 1) * P], vmix[:, k:k + 1],
                              k == 0, k == DK - 1)
            jobs.fill(last, "time_row")

        def turn_back(b, hf):
            pe.wait_ge(to_ready.sem, to_ready.done(b, hf))
            for t in range(GT // 2):
                jobs.wait_room(pe, b, ("to", hf, t))
                for i in range(2):
                    for k in range(DK):
                        at = (2 * t + i) * P
                        last = nc.tensor.transpose(
                            jobs.bank(("to", hf, t))[:, i * DIM + k * P:i * DIM + (k + 1) * P],
                            toT[:, k, at:at + P], ident[:, :])
                jobs.fill(last, ("to", hf, t))

        def bias(b, hf):
            pe.wait_ge(comb_ready.sem, comb_ready.done(b, hf))
            jobs.wait_room(pe, b, ("ct", hf))
            for t in range(GT):
                last = nc.tensor.transpose(jobs.bank(("ct", hf))[0:N_EXP, t * P:(t + 1) * P],
                                           comb[:, hf * GT + t, :], ident[:, :])
            jobs.fill(last, ("ct", hf))
            pe.wait_ge(combT_ready.sem, combT_ready.done(b, hf))
            for t in range(GT // 2):
                jobs.wait_room(pe, b, ("db", hf, t))
                for i in range(2):
                    at = (2 * t + i) * P
                    last = mm(jobs.bank(("db", hf, t))[:, i * DIM:(i + 1) * DIM], combT[:, at:at + P],
                              w.down_bias[0:N_EXP, :])
                jobs.fill(last, ("db", hf, t))

        def channel(b, hf):
            pe.wait_ge(xc_ready.sem, xc_ready.done(b, hf))
            turn(b, "xc", hf, tmp, 0)
            pe.wait_ge(xcT_dve.sem, xcT_dve.done(b, hf))
            pe.wait_ge(xcT_act.sem, xcT_act.done(b, hf))
            for t in range(GT // 2):
                jobs.wait_room(pe, b, ("rc", hf, t))
                for i in range(2):
                    at = 1 + (2 * t + i) * P
                    for k in range(DK):
                        last = mm(jobs.bank(("rc", hf, t))[:, i * DIM:(i + 1) * DIM], xcT[:, k, at:at + P],
                                  w.cr[:, k, :], k == 0, k == DK - 1)
                jobs.fill(last, ("rc", hf, t))
            for f in range(CM_BLK):
                jobs.wait_room(pe, b, ("kc", hf, f))
                for k in range(DK):
                    last = mm(jobs.bank(("kc", hf, f)), w.ck[:, k, f * P:(f + 1) * P], xcT[:, k, 0:GROUP],
                              k == 0, k == DK - 1)
                jobs.fill(last, ("kc", hf, f))
            pe.wait_ge(kc_ready.sem, kc_ready.done(b, (hf + 1) * CM_BLK - 1))
            for t in range(GT // 2):
                jobs.wait_room(pe, b, ("vc", hf, t))
                for i in range(2):
                    at = (2 * t + i) * P
                    for f in range(CM_BLK):
                        last = mm(jobs.bank(("vc", hf, t))[:, i * DIM:(i + 1) * DIM], kcT[:, f, at:at + P],
                                  w.cv[:, f, :], f == 0, f == CM_BLK - 1)
                jobs.fill(last, ("vc", hf, t))

        parts = {"norms": norms, "hidden": hidden, "down": down, "time_row": time_row, "turn": turn_back,
                 "bias": bias, "channel": channel}
        pe.wait_ge(w.sem, 16 * w.loads)
        with pe.Fori(0, BATCH) as b:
            for step, n in PLAN:
                parts[step](b, n)

    @block.scalar
    def _(act):
        act.wait_ge(steps_ready, 1)
        for k in range(DK):
            nc.scalar.activation(dec[:, k, :], xnT[:, 0, :], ACT.Exp, scale=col("l3_time_decay", k))
        act.drain().then_inc(dec_ready, 1)

        def norms(b, hf):
            half = slice(hf * GROUP, (hf + 1) * GROUP)
            jobs.wait_filled(act, b, ("xnT", hf, 1))
            nc.scalar.activation(xnT[:, 1, half], jobs.bank(("xnT", hf, 1)), ACT.Copy).then_inc(xnT_act.sem, 1)
            jobs.free(act.drain(), ("xnT", hf, 1))
            jobs.wait_filled(act, b, ("xl", hf, 1))
            if hf == 0:
                act.wait_ge(reset_done.sem, reset_done.done(b))
            else:
                act.wait_ge(mix_ready.sem, mix_ready.done(b, 0))
            nc.scalar.activation(xlT[:, 1, 1:], jobs.bank(("xl", hf, 1)), ACT.Identity, bias=col("tm_b", 1),
                                 scale=col("tm_g", 1)).then_inc(xlT_act.sem, 1)
            jobs.free(act.drain(), ("xl", hf, 1))
            act.wait_ge(logits_ready.sem, logits_ready.done(b, hf))
            nc.scalar.activation(le[:, :, :], lg[:, :, :], ACT.Exp).then_inc(exp_ready.sem, 1)
            for n in range(DK):
                jobs.wait_filled(act, b, ("r", hf, n))
                nc.scalar.activation(rT[:, n, half], jobs.bank(("r", hf, n)), ACT.Sigmoid).then_inc(r_ready.sem, 1)
                jobs.free(act.drain(), ("r", hf, n))

        def hidden(b, n):
            for m in range(I_BLK):
                act.wait_ge(g_ready.sem, g_ready.done(b, n * I_BLK + m))
                nc.scalar.activation(s_[:, m, :], g_[:, m, :], ACT.Sigmoid, scale=ALPHA).then_inc(s_ready.sem, 1)

        def turn(b, hf):
            act.wait_ge(u_row_ready.sem, u_row_ready.done(b))
            if hf == 1:
                jobs.wait_filled(act, b, ("to", 0, GT // 2 - 1))
            for k in range(DK):
                last = nc.scalar.activation(toT[:, k, :], rT[:, k, hf * GROUP:(hf + 1) * GROUP], ACT.Copy,
                                            scale=ucol[:, k:k + 1])
            last.then_inc(to_ready.sem, 1)

        def channel(b, hf):
            jobs.wait_filled(act, b, ("xc", hf, 1))
            nc.scalar.activation(xcT[:, 1, 1:], jobs.bank(("xc", hf, 1)), ACT.Identity, bias=col("cm_b", 1),
                                 scale=col("cm_g", 1)).then_inc(xcT_act.sem, 1)
            jobs.free(act.drain(), ("xc", hf, 1))
            for t in range(GT // 2):
                jobs.wait_filled(act, b, ("rc", hf, t))
                nc.scalar.activation(rc[:, 2 * t:2 * t + 2, :].rearrange("p t d -> p (t d)"),
                                     jobs.bank(("rc", hf, t)), ACT.Sigmoid).then_inc(rc_ready.sem, 1)
                jobs.free(act.drain(), ("rc", hf, t))
            for f in range(CM_BLK):
                jobs.wait_filled(act, b, ("kc", hf, f))
                nc.scalar.activation(kcT[:, f, :], jobs.bank(("kc", hf, f)), ACT.Relu).then_inc(relu_ready.sem, 1)
                jobs.free(act.drain(), ("kc", hf, f))

        def nothing(b, n):
            pass

        parts = {"norms": norms, "hidden": hidden, "down": nothing, "time_row": nothing, "turn": turn,
                 "bias": nothing, "channel": channel}
        with act.Fori(0, BATCH) as b:
            for step, n in PLAN:
                parts[step](b, n)

    @block.gpsimd
    def _(pool):
        nc.gpsimd.iota(xnT[:, 0, :], pattern=[[-1, SEQ]], base=SEQ - 1, channel_multiplier=0,
                       allow_small_or_imprecise_dtypes=True).then_inc(steps_ready, 1)

        def power(b, n):
            pool.wait_ge(moments_ready.sem, moments_ready.done(b, n))
            nc.gpsimd.tensor_tensor(rstd[:, :], moments[:, :, 1], mem.neg_half[:, 0:GT], ALU.pow).then_inc(
                rstd_ready.sem, 1)

        def norms(b, hf):
            for i in range(3):
                power(b, 3 * hf + i)

        def hidden(b, n):
            for m in range(I_BLK):
                i = n * I_BLK + m
                pool.wait_ge(u_ready.sem, u_ready.done(b, i))
                pool.wait_ge(s_ready.sem, s_ready.done(b, i))
                nc.gpsimd.tensor_tensor(gs[:, m, :], g_[:, m, :], s_[:, m, :], ALU.mult)
                nc.gpsimd.tensor_scalar(u_[:, m, :], u_[:, m, :], -LIMIT, 1.0, ALU.max, ALU.add)
                pool.drain().then_inc(gs_ready.sem, 1)

        def turn(b, hf):
            for i in range(2):
                power(b, 3 * HALVES + 2 * hf + i)

        def channel(b, hf):
            for f in range(CM_BLK):
                pool.wait_ge(relu_ready.sem, relu_ready.done(b, hf * CM_BLK + f))
                nc.gpsimd.tensor_tensor(kcT[:, f, :], kcT[:, f, :], kcT[:, f, :], ALU.mult).then_inc(kc_ready.sem, 1)

        def nothing(b, n):
            pass

        parts = {"norms": norms, "hidden": hidden, "down": nothing, "time_row": nothing, "turn": turn,
                 "bias": nothing, "channel": channel}
        with pool.Fori(0, BATCH) as b:
            for step, n in PLAN:
                parts[step](b, n)

    @block.vector
    def _(dve):
        def normalise(b, n, src, dst, eps):
            for t in range(GT):
                nc.vector.bn_stats(stats[:, t, :], src(t))
            dve.drain()
            for t in range(GT):
                nc.vector.bn_aggr(moments[:, t, :], stats[:, t, :])
            dve.drain()
            nc.vector.tensor_scalar(moments[:, :, 1], moments[:, :, 1], eps, None, ALU.add).then_inc(
                moments_ready.sem, 1)
            dve.wait_ge(rstd_ready.sem, rstd_ready.done(b, n))
            for t in range(GT):
                last = nc.vector.tensor_scalar(dst(t), src(t), moments[:, t, 0:1], rstd[:, t:t + 1],
                                               ALU.subtract, ALU.mult)
            return last

        def affine(buf, gain, shift):
            dve.drain()
            nc.vector.tensor_tensor(buf, buf, spread(row(gain), 1, GT), ALU.mult)
            dve.drain()
            nc.vector.tensor_tensor(buf, buf, spread(row(shift), 1, GT), ALU.add)
            dve.drain()

        def norms(b, hf):
            t0, half = hf * GT, slice(hf * GROUP, (hf + 1) * GROUP)
            normalise(b, 3 * hf, lambda t: x[:, b * HB_TILES + t0 + t, :], lambda t: xn[:, t0 + t, :],
                      1e-5).then_inc(xn_ready.sem, 1)
            dve.drain()
            normalise(b, 3 * hf + 1, lambda t: xn[:, t0 + t, :], lambda t: tmp[:, t, :], L3_EPS)
            affine(tmp[:, :, :], "ln1_g", "ln1_b")
            jobs.wait_filled(dve, b, ("xnT", hf, 0))
            nc.vector.tensor_copy(xnT[:, 0, half], jobs.bank(("xnT", hf, 0))).then_inc(xnT_dve.sem, 1)
            jobs.free(dve.drain(), ("xnT", hf, 0))
            normalise(b, 3 * hf + 2, lambda t: tmp[:, t, :], lambda t: tmp[:, t, :], L3_EPS).then_inc(xl_ready.sem, 1)
            jobs.wait_filled(dve, b, ("route", hf))
            last = nc.vector.tensor_tensor(lg[:, :, :], jobs.bank(("route", hf))[:, 0:GT * N_EXP].rearrange(
                "p (t e) -> p t e", e=N_EXP), spread(row("router_bias"), 1, GT), ALU.add)
            jobs.free(last, ("route", hf))
            dve.drain()
            nc.vector.tensor_reduce(lmax[:, :], lg[:, :, :], AX.X, ALU.max)
            a, c = spread(lg[:, :, :], 2, N_EXP), spread(lg[:, :, :], 3, N_EXP)
            nc.vector.tensor_tensor(gt[:, :, :, :], a, c, ALU.is_gt)
            nc.vector.tensor_tensor(eq[:, :, :, :], a, c, ALU.is_equal)
            dve.drain()
            nc.vector.tensor_tensor(lg[:, :, :], lg[:, :, :], spread(lmax[:, :], 2, N_EXP), ALU.subtract).then_inc(
                logits_ready.sem, 1)
            nc.vector.tensor_tensor(eq[:, :, :, :], eq[:, :, :, :], spread(mem.lower[:, :, :], 1, GT), ALU.mult)
            dve.drain()
            nc.vector.tensor_tensor(gt[:, :, :, :], gt[:, :, :, :], eq[:, :, :, :], ALU.add)
            dve.drain()
            nc.vector.tensor_reduce(rank[:, :, :], gt[:, :, :, :], AX.X, ALU.add)
            dve.drain()
            nc.vector.tensor_scalar(rank[:, :, :], rank[:, :, :], 2.0, None, ALU.is_lt)
            jobs.wait_filled(dve, b, ("xl", hf, 0))
            nc.vector.tensor_scalar(xlT[:, 0, 1:], jobs.bank(("xl", hf, 0)), col("tm_g", 0), col("tm_b", 0),
                                    ALU.mult, ALU.add).then_inc(xlT_dve.sem, 1)
            jobs.free(dve.drain(), ("xl", hf, 0))
            dve.wait_ge(xlT_act.sem, xlT_act.done(b, hf))
            for k in range(DK):
                nc.vector.tensor_scalar(mixT[:, k, :], xlT[:, k, 0:GROUP], keep[:, k:k + 1], None, ALU.mult)
            dve.drain()
            for k in range(DK):
                nc.vector.scalar_tensor_tensor(out=mixT[:, k, :], in0=xlT[:, k, 1:], scalar=col("l3_time_first", k),
                                               in1=mixT[:, k, :], op0=ALU.mult, op1=ALU.add)
            nc.vector.tensor_copy(xlT[:, :, 0:1], xlT[:, :, GROUP:])
            dve.drain().then_inc(mix_ready.sem, 1)
            dve.wait_ge(exp_ready.sem, exp_ready.done(b, hf))
            cb = comb[:, t0:t0 + GT, :]
            nc.vector.tensor_tensor(cb, le[:, :, :], rank[:, :, :], ALU.mult)
            dve.drain()
            nc.vector.tensor_reduce(esum[:, :], cb, AX.X, ALU.add)
            dve.drain()
            nc.vector.reciprocal(esum[:, :], esum[:, :])
            dve.drain()
            nc.vector.tensor_tensor(cb, cb, spread(esum[:, :], 2, N_EXP), ALU.mult).then_inc(comb_ready.sem, 1)
            dve.drain()
            for k in range(DK):
                jobs.wait_filled(dve, b, ("v", hf, k))
                nc.vector.scalar_tensor_tensor(out=junk[:, :], in0=jobs.bank(("v", hf, k)), scalar=1.0,
                                               in1=dec[:, k, half], op0=ALU.mult, op1=ALU.mult,
                                               accum_out=vm[:, hf, k:k + 1])
                jobs.free(dve.drain(), ("v", hf, k))

        def hidden(b, n):
            e = n % N_EXP
            for m in range(I_BLK):
                jobs.wait_filled(dve, b, ("g", n, m))
                nc.vector.tensor_scalar(g_[:, m, :], jobs.bank(("g", n, m)), col("eb_gate", I_BLK * e + m), LIMIT,
                                        ALU.add, ALU.min).then_inc(g_ready.sem, 1)
                jobs.free(dve.drain(), ("g", n, m))
                jobs.wait_filled(dve, b, ("u", n, m))
                nc.vector.tensor_scalar(u_[:, m, :], jobs.bank(("u", n, m)), col("eb_up", I_BLK * e + m), LIMIT,
                                        ALU.add, ALU.min).then_inc(u_ready.sem, 1)
                jobs.free(dve.drain(), ("u", n, m))
            if n == 0:
                activate(b, 0)

        def activate(b, n):
            for m in range(I_BLK):
                dve.wait_ge(gs_ready.sem, gs_ready.done(b, n * I_BLK + m))
                last = nc.vector.tensor_tensor(hT[:, n % 2, m, :], u_[:, m, :], gs[:, m, :], ALU.mult)
            last.then_inc(h_ready.sem, 1)
            dve.drain()

        def down(b, n):
            hf, e = n // N_EXP, n % N_EXP
            for t in range(GT // 2):
                jobs.wait_filled(dve, b, ("d", n, t))
                for i in range(2):
                    tile = hf * GT + 2 * t + i
                    xt = x[:, b * HB_TILES + tile, :]
                    last = nc.vector.scalar_tensor_tensor(
                        out=xt, in0=jobs.bank(("d", n, t))[:, i * DIM:(i + 1) * DIM], scalar=comb[:, tile, e:e + 1],
                        in1=xt, op0=ALU.mult, op1=ALU.add)
                jobs.free(last, ("d", n, t))
            dve.drain()
            if n + 1 < N_UNITS:
                activate(b, n + 1)

        def time_row(b, _):
            nc.vector.tensor_tensor(vmix[:, :], vm[:, 0, :], vm[:, 1, :], ALU.add).then_inc(vmix_ready.sem, 1)
            jobs.wait_filled(dve, b, "time_row")
            bo = COL_AT["bo"]
            last = nc.vector.tensor_tensor(ucol[:, :], jobs.bank("time_row")[:, 0:DK], mem.cols[:, bo:bo + DK],
                                           ALU.add).then_inc(u_row_ready.sem, 1)
            jobs.free(dve.drain(), "time_row")

        def turn(b, hf):
            for t in range(GT // 2):
                jobs.wait_filled(dve, b, ("to", hf, t))
                t0 = hf * GT + 2 * t
                last = nc.vector.tensor_tensor(x2[:, 2 * t:2 * t + 2, :], xn[:, t0:t0 + 2, :],
                                               jobs.bank(("to", hf, t)).rearrange("p (t d) -> p t d", t=2), ALU.add)
                jobs.free(last, ("to", hf, t))
            dve.drain()
            base = 3 * HALVES + 2 * hf
            normalise(b, base, lambda t: x2[:, t, :], lambda t: tmp[:, t, :], L3_EPS)
            affine(tmp[:, :, :], "ln2_g", "ln2_b")
            normalise(b, base + 1, lambda t: tmp[:, t, :], lambda t: tmp[:, t, :], L3_EPS).then_inc(xc_ready.sem, 1)

        def channel(b, hf):
            jobs.wait_filled(dve, b, ("xc", hf, 0))
            nc.vector.tensor_scalar(xcT[:, 0, 1:], jobs.bank(("xc", hf, 0)), col("cm_g", 0), col("cm_b", 0),
                                    ALU.mult, ALU.add).then_inc(xcT_dve.sem, 1)
            jobs.free(dve.drain(), ("xc", hf, 0))
            xg = x[:, bass.ds(b * HB_TILES + hf * GT, GT), :]
            nc.vector.tensor_tensor(xg, xg, x2[:, :, :], ALU.add)
            dve.drain()
            for t in range(GT // 2):
                jobs.wait_filled(dve, b, ("vc", hf, t))
                dve.wait_ge(rc_ready.sem, rc_ready.done(b, hf * GT // 2 + t))
                rt = rc[:, 2 * t:2 * t + 2, :]
                last = nc.vector.tensor_tensor(rt, rt, jobs.bank(("vc", hf, t)).rearrange("p (t d) -> p t d", t=2),
                                               ALU.mult)
                jobs.free(last, ("vc", hf, t))
            dve.drain()
            nc.vector.tensor_tensor(xg, xg, rc[:, :, :], ALU.add)
            nc.vector.tensor_copy(xcT[:, :, 0:1], xcT[:, :, GROUP:])
            dve.drain()

        def bias(b, hf):
            jobs.wait_filled(dve, b, ("ct", hf))
            nc.vector.tensor_copy(combT[:, :], jobs.bank(("ct", hf))[0:N_EXP, :]).then_inc(combT_ready.sem, 1)
            jobs.free(dve.drain(), ("ct", hf))
            for t in range(GT // 2):
                jobs.wait_filled(dve, b, ("db", hf, t))
                xt = x[:, bass.ds(b * HB_TILES + hf * GT + 2 * t, 2), :]
                last = nc.vector.tensor_tensor(xt, xt, jobs.bank(("db", hf, t)).rearrange("p (t d) -> p t d", t=2),
                                               ALU.add)
                jobs.free(last, ("db", hf, t))
            dve.drain()

        parts = {"norms": norms, "hidden": hidden, "down": down, "time_row": time_row, "turn": turn,
                 "bias": bias, "channel": channel}
        jobs.grant(dve)
        tf = COL_AT["l3_time_first"]
        nc.vector.tensor_scalar(keep[:, :], mem.cols[:, tf:tf + DK], -1.0, 1.0, ALU.mult, ALU.add)
        dve.wait_ge(mem.row_ready, 16)
        dve.wait_ge(dec_ready, 1)
        with dve.Fori(0, BATCH) as b:
            nc.vector.memset(xlT[:, :, 0:1], 0.0)
            nc.vector.memset(xcT[:, :, 0:1], 0.0)
            dve.drain().then_inc(reset_done.sem, 1)
            for step, n in PLAN:
                parts[step](b, n)


class Named:
    pass


class Taker:

    def __init__(self, region):
        self.region, self.at = region, 0

    def __call__(self, blocks, width):
        part = self.region[:, self.at:self.at + blocks * width]
        self.at += blocks * width
        return part.rearrange("p (a b) -> p a b", a=blocks)


class Memory(Named):

    def __init__(self, nc, ctx):
        self.nc, self.ctx = nc, ctx

    def scoped(self, ctx, prefix):
        nc = self.nc

        def sb(name, shape, dt=F32):
            return ctx.enter_context(nc.sbuf_tensor(f"{prefix}_{name}", shape, dt))

        def ps(name, shape, dt=F32):
            return ctx.enter_context(nc.psum_tensor(name, shape, dt))

        def sem(name):
            return self.ctx.enter_context(nc.semaphore(name))

        return sb, ps, sem

    def after_l0(self):
        sb, _, sem = self.scoped(self.ctx, "mid")
        self.rows = sb("vector_rows", [P, N_ROWS])
        self.region_c = sb("region_c", [P, 4 * DK * DIM + 2 * DK * QH + Q_BLK * DIM])
        w = self.l2 = Named()
        take = Taker(self.region_c)
        w.k, w.v, w.r, w.o = [take(DK, DIM) for _ in range(4)]
        w.gate, w.up = [take(DK, QH) for _ in range(2)]
        w.down = take(Q_BLK, DIM)
        w.sem = sem("w_l2")
        self.psum_filled = [sem(f"psum_filled{b}") for b in range(8)]
        self.psum_freed = [sem(f"psum_freed{b}") for b in range(8)]
        self.filled_base, self.freed_base = [0] * 8, [0] * 8
        w = self.l3 = Named()
        w.sem, w.loads = sem("w_l3"), 10
        take = Taker(self.region_a)
        w.gate_up = take(N_EXP * DK, 2 * I_BLK * P)
        w.down = take(N_EXP * I_BLK, DIM)
        w.router = take(DK, N_EXP)
        w.down_bias = take(1, DIM)[0:N_EXP, 0, :]
        take = Taker(self.region_b)
        w.v, w.r, w.o, w.cr = [take(DK, DIM) for _ in range(4)]
        w.ck = take(DK, CM_BLK * P)
        w.cv = take(CM_BLK, DIM)

    def load_l2(self, sp, io):
        w = self.l2
        sp.dma_start(self.rows[:, :], io["rows"].broadcast_to([P, N_ROWS])).then_inc(self.row_ready, 16)
        for part, name in ((w.gate, "wq_gateT"), (w.up, "wq_upT")):
            sp.dma_start(part.bitcast(I32), io[name].rearrange("(k p) n -> p k n", p=P)).then_inc(w.sem, 16)
        full = (Q_BLK - 1) * P
        down = w.down.bitcast(I32)
        sp.dma_start(down[:, 0:Q_BLK - 1, :], io["wq_downT"][0:full, :].rearrange("(k p) n -> p k n", p=P)).then_inc(
            w.sem, 16)
        sp.dma_start(down[0:QH - full, Q_BLK - 1, :], io["wq_downT"][full:QH, :]).then_inc(w.sem, 16)
        for part, name in ((w.k, "l2_Wk"), (w.v, "l2_Wv"), (w.r, "l2_Wr"), (w.o, "l2_Wo")):
            sp.dma_start(part, io[name].rearrange("(k p) n -> p k n", p=P)).then_inc(w.sem, 16)

    def load_l3a(self, sp, io):
        w = self.l3
        for part, name in ((w.gate_up, "l3_gate_up"), (w.down, "l3_down"), (w.router, "l3_router")):
            sp.dma_start(part, io[name].rearrange("(k p) n -> p k n", p=P)).then_inc(w.sem, 16)
        sp.dma_start(w.down_bias, io["l3_down_bias"]).then_inc(w.sem, 16)

    def load_l3b(self, sp, io):
        w = self.l3
        for part, name in ((w.v, "l3_Wv"), (w.r, "l3_Wr"), (w.o, "l3_Wo"), (w.cr, "l3_Wcr"), (w.ck, "l3_Wck"),
                           (w.cv, "l3_Wcv")):
            sp.dma_start(part, io[name].rearrange("(k p) n -> p k n", p=P)).then_inc(w.sem, 16)

    def col(self, name, n=0):
        at = COL_AT[name] + n
        return self.cols[:, at:at + 1]

    def l0_row(self, name):
        at = L0_ROW_AT[name]
        return self.l0_rows[:, at:at + dict(L0_ROWS)[name]]

    def row(self, name):
        at = ROW_AT[name]
        return self.rows[:, at:at + dict(ROWS)[name]]


def start_up(nc, mem, ctx, io):
    sb, _, sem = mem.scoped(mem.ctx, "all")
    mem.x = sb("x", [P, TILES, DIM])
    mem.ident = sb("ident", [P, P])
    mem.ones = sb("ones", [P, P])
    mem.neg_half = sb("neg_half", [P, 8])
    mem.lower = sb("lower", [P, N_EXP, N_EXP])
    mem.cols = sb("cols", [P, N_COLS])
    mem.l0_rows = sb("l0_rows", [P, N_L0_ROWS])
    mem.x_ready, mem.col_ready = sem("x_ready"), sem("col_ready")
    mem.l0_row_ready, mem.row_ready = sem("l0_row_ready"), sem("row_ready")
    mem.const_ready, mem.n_const = sem("const_ready"), 1
    mem.region_a = sb("region_a", [P, 13088])
    mem.region_b = sb("region_b", [P, 6144])
    w = mem.l0 = Named()
    take = Taker(mem.region_a)

    w.win = take(DK, D_IN)
    w.router = take(DK, N_EXP)
    w.gate_up = take(N_EXP * DK, 256)
    w.sh_gate_up = take(DK, 1024)
    w.down = take(L0_UNITS, DIM)
    w.out = take(Z_BLK, DIM)
    take = Taker(mem.region_b)
    l1 = mem.l1 = Named()
    l1.qkv = take(DK, 3 * DIM)
    l1.out = take(DK, DIM)
    l1.w1 = take(DK, FFN_BLK * P)
    l1.w2 = take(FFN_BLK, DIM)
    l1.sem = sem("w_l1")
    w.in_sem, w.gate_sem, w.ffn_sem, w.out_sem = sem("w_in"), sem("w_gate"), sem("w_ffn"), sem("w_out")

    def gu(u, k, i):
        if u < N_EXP:
            return w.gate_up[:, u * DK + k, i * P:(i + 1) * P]
        at = i * 512 + (u - N_EXP) * P
        return w.sh_gate_up[:, k, at:at + P]

    w.gu = gu
    x_d = io["x"].rearrange("(g t p) d -> g p t d", p=P, t=GT)

    block = ctx.enter_context(nc.Block())

    @block.sync
    def _(sp):
        for g in range(TILES // GT):
            sp.dma_start(mem.x[:, g * GT:(g + 1) * GT, :], x_d[g]).then_inc(mem.x_ready, 16)
            if g == 0:
                sp.dma_start(w.win, io["W_inT"].rearrange("(k p) n -> p k n", p=P)).then_inc(w.in_sem, 16)
                sp.dma_start(mem.l0_rows[:, :], io["l0_rows"].broadcast_to([P, N_L0_ROWS])).then_inc(mem.l0_row_ready, 16)
                sp.dma_start(mem.cols[:, :], io["cols"]).then_inc(mem.col_ready, 16)
                sp.dma_start(w.router, io["w_gate"].rearrange("(k p) n -> p k n", p=P)).then_inc(w.gate_sem, 16)
                sp.dma_start(w.out, io["W_outT"].rearrange("(k p) n -> p k n", p=P)).then_inc(w.out_sem, 16)
        sp.dma_start(w.gate_up,
                     io["w_gate_up"].rearrange("(ek p) f -> p ek f", p=P)).then_inc(w.ffn_sem, 16)
        sp.dma_start(w.sh_gate_up, io["w_sh_gate_up"].rearrange("(k p) n -> p k n", p=P)).then_inc(w.ffn_sem, 16)
        sp.dma_start(w.down[:, 0:N_EXP, :], io["w_down"].rearrange("(e p) n -> p e n", p=P)).then_inc(w.ffn_sem, 16)
        sp.dma_start(w.down[:, N_EXP:, :], io["w_sh_down"].rearrange("(e p) n -> p e n", p=P)).then_inc(w.ffn_sem, 16)

        sp.dma_start(l1.qkv, io["w_qkvT"].rearrange("(k p) n -> p k n", p=P)).then_inc(l1.sem, 16)
        sp.dma_start(l1.out, io["w_attn_outT"].rearrange("(k p) n -> p k n", p=P)).then_inc(l1.sem, 16)
        sp.dma_start(l1.w1, io["w1T"].rearrange("(k p) n -> p k n", p=P)).then_inc(l1.sem, 16)
        sp.dma_start(l1.w2, io["w2T"].rearrange("(k p) n -> p k n", p=P)).then_inc(l1.sem, 16)

    @block.gpsimd
    def _(pool):
        nc.gpsimd.memset(mem.lower[:, :, :], 1.0)
        nc.gpsimd.memset(mem.ones[:, :], 1.0)
        nc.gpsimd.memset(mem.ident[:, :], 0.0)
        nc.gpsimd.memset(mem.neg_half[:, :], -0.5)
        pool.drain()
        nc.gpsimd.affine_select(out=mem.ident[:, :], in_=mem.ident[:, :], compare_op=ALU.not_equal, fill=1.0,
                                base=0, pattern=[[-1, P]], channel_multiplier=1)
        nc.gpsimd.affine_select(out=mem.lower[:, :, :], in_=mem.lower[:, :, :], compare_op=ALU.is_gt, fill=0.0,
                                base=0, pattern=[[1, N_EXP], [-1, N_EXP]], channel_multiplier=0)
        pool.drain().then_inc(mem.const_ready, 1)


def finish(nc, mem, ctx, out):
    sem = mem.ctx.enter_context(nc.semaphore("out_written"))
    out_d = out.rearrange("(g t p) d -> g p t d", p=P, t=GT)
    block = ctx.enter_context(nc.Block())

    @block.sync
    def _(sp):
        for g in range(TILES // GT):
            sp.dma_start(out_d[g], mem.x[:, g * GT:(g + 1) * GT, :]).then_inc(sem, 16)
        sp.wait_ge(sem, 16 * (TILES // GT))


def build(nc, io, out):
    with ExitStack() as whole:
        mem = Memory(nc, whole)
        with ExitStack() as ctx:
            start_up(nc, mem, ctx, io)
        with ExitStack() as ctx:
            layer0(nc, mem, ctx, io)
        mem.after_l0()
        for layer in (layer1, layer2, layer3):
            with ExitStack() as ctx:
                layer(nc, mem, ctx, io)
        with ExitStack() as ctx:
            finish(nc, mem, ctx, out)


def lay_out(v):
    import numpy as np

    def blocks(vec, n):
        full = np.zeros((n * P,), np.float32)
        full[:vec.shape[0]] = vec
        return full.reshape(n, P).T

    def rows(*parts):
        return np.ascontiguousarray(np.concatenate([p.reshape(-1) for p in parts]).reshape(1, -1))

    def turned(m):
        return np.ascontiguousarray(m.T)

    conv = v["L0_attn_conv_w"].reshape(CONV_BLK, P, CONV_K).transpose(1, 0, 2).reshape(P, -1)
    gub = v["L3_ffn_gate_up_proj_bias"]
    parts = {
        "conv_w": conv, "D": blocks(np.repeat(v["L0_attn_D"], HEAD_P), 4), "norm_w": blocks(v["L0_attn_norm_w"], 4),
        "b_qkv": blocks(v["L1_attn_b_qkv"], 6), "b1": blocks(v["L1_ffn_b1"], 8),
        "ln_scale": blocks(v["L2_attn_ln_scale"], 2), "ln_bias": blocks(v["L2_attn_ln_bias"], 2),
        "mix_k": blocks(v["L2_attn_mix_k"], 2), "mix_v": blocks(v["L2_attn_mix_v"], 2),
        "mix_r": blocks(v["L2_attn_mix_r"], 2), "time_first": blocks(v["L2_attn_time_first"], 2),
        "time_decay": blocks(v["L2_attn_time_decay"], 2), "s_gate": blocks(v["L2_ffn_s_gate"], 6),
        "s_up": blocks(v["L2_ffn_s_up"], 6), "l3_time_decay": blocks(v["L3_attn_time_decay"], 2),
        "l3_time_first": blocks(v["L3_attn_time_first"], 2),
        "eb_gate": blocks(gub[:, 0::2].reshape(-1), 16), "eb_up": blocks(gub[:, 1::2].reshape(-1), 16),
        "tm_g": blocks(v["L3_attn_tm_g"], 2), "tm_b": blocks(v["L3_attn_tm_b"], 2),
        "cm_g": blocks(v["L3_attn_cm_g"], 2), "cm_b": blocks(v["L3_attn_cm_b"], 2), "bo": blocks(v["L3_attn_bo"], 2),
    }
    cols = np.ascontiguousarray(np.concatenate([parts[n] for n, _ in COLS], axis=1))
    b_v = v["L1_attn_b_qkv"][2 * DIM:]
    r = {"dt_bias": "L0_attn_dt_bias", "A_log": "L0_attn_A_log", "b_out": "L1_attn_b_out", "b2": "L1_ffn_b2",
         "s_down": "L2_ffn_s_down", "ln1_g": "L3_attn_ln1_g", "ln1_b": "L3_attn_ln1_b",
         "ln2_g": "L3_attn_ln2_g", "ln2_b": "L3_attn_ln2_b", "router_bias": "L3_ffn_router_bias"}
    gate_up = v["L3_ffn_gate_up_proj"]
    apart = np.concatenate([gate_up[:, :, 0::2], gate_up[:, :, 1::2]], axis=2)
    return {
        "x": v["L0_attn_x"].reshape(TOKENS, DIM), "cols": cols, "rows": rows(b_v, *[v[r[n]] for n, _ in ROWS[1:]]),
        "l0_rows": rows(*[v[r[n]] for n, _ in L0_ROWS]),
        "W_inT": turned(v["L0_attn_W_in"]), "W_outT": turned(v["L0_attn_W_out"]),
        "w_gate": v["L0_ffn_w_gate"], "w_gate_up": v["L0_ffn_w_gate_up"].reshape(-1, 256),
        "w_down": v["L0_ffn_w_down"].reshape(-1, DIM), "w_sh_gate_up": v["L0_ffn_w_sh_gate_up"],
        "w_sh_down": v["L0_ffn_w_sh_down"],
        "w_qkvT": turned(v["L1_attn_w_qkv"]), "w_attn_outT": turned(v["L1_attn_w_out"]),
        "wq_gateT": turned(v["L2_ffn_wq_gate"]), "wq_upT": turned(v["L2_ffn_wq_up"]),
        "wq_downT": turned(v["L2_ffn_wq_down"]), "l2_Wk": v["L2_attn_Wk"], "l2_Wv": v["L2_attn_Wv"],
        "l2_Wr": v["L2_attn_Wr"], "l2_Wo": v["L2_attn_Wo"],
        "l3_Wv": v["L3_attn_Wv"], "l3_Wr": v["L3_attn_Wr"], "l3_Wo": v["L3_attn_Wo"], "l3_Wcr": v["L3_attn_Wcr"],
        "l3_Wck": v["L3_attn_Wck"], "l3_Wcv": v["L3_attn_Wcv"], "l3_gate_up": apart.reshape(-1, 2 * I_BLK * P),
        "l3_down": v["L3_ffn_down_proj"].reshape(-1, DIM), "l3_router": turned(v["L3_ffn_router_weight"]),
        "l3_down_bias": v["L3_ffn_down_proj_bias"],
        "w1T": turned(v["L1_ffn_w1"]), "w2T": turned(v["L1_ffn_w2"]),
    }


def kernel(**inputs):
    import numpy as np
    import concourse.bacc as bacc
    from concourse.bass_utils import run_bass_kernel_spmd

    arrays = {n: np.ascontiguousarray(a) for n, a in lay_out({n: np.asarray(a) for n, a in inputs.items()}).items()}
    nc = bacc.Bacc("TRN2", target_bir_lowering=False, num_devices=1)
    io = {n: nc.dram_tensor(n, a.shape, mybir.dt.from_np(a.dtype), kind="ExternalInput").ap()
          for n, a in arrays.items()}
    out = nc.dram_tensor("out", (TOKENS, DIM), F32, kind="ExternalOutput").ap()
    build(nc, io, out)
    got = run_bass_kernel_spmd(nc, [arrays], core_ids=[0])
    return got.results[0]["out"].reshape(BATCH, SEQ, DIM)
```

```python
from contextlib import ExitStack

import concourse.bass as bass
from concourse import mybir
from concourse.alu_op_type import AluOpType as ALU

F32 = mybir.dt.float32
BF16 = mybir.dt.bfloat16
I32 = mybir.dt.int32
ACT = mybir.ActivationFunctionType
AX = mybir.AxisListType

P = 128
BATCH, SEQ, DIM = 2, 1024, 256
TOKENS = BATCH * SEQ
TILES = TOKENS // P
GROUP = 512
GT = GROUP // P
HALVES = SEQ // GROUP
DK = DIM // P

HID, HEADS, HEAD_P, STATE, CONV_K = 512, 64, 8, 128, 4
CONV_BLK = (HID + 2 * STATE) // P
Z_BLK = HID // P
D_IN = 2 * HID + 2 * STATE + HEADS
N_EXP = 8
SHARED = 4
L0_UNITS = SHARED + N_EXP

COLS = [("conv_w", CONV_BLK * CONV_K), ("D", Z_BLK), ("norm_w", Z_BLK), ("b_qkv", 6), ("b1", 8),
        ("ln_scale", 2), ("ln_bias", 2), ("mix_k", 2), ("mix_v", 2), ("mix_r", 2),
        ("time_first", 2), ("time_decay", 2), ("s_gate", 6), ("s_up", 6),
        ("l3_time_decay", 2), ("l3_time_first", 2), ("eb_gate", 16), ("eb_up", 16),
        ("tm_g", 2), ("tm_b", 2), ("cm_g", 2), ("cm_b", 2), ("bo", 2)]
L0_ROWS = [("dt_bias", HEADS), ("A_log", HEADS)]
ROWS = [("b_v", DIM), ("b_out", DIM), ("b2", DIM), ("s_down", DIM),
        ("ln1_g", DIM), ("ln1_b", DIM), ("ln2_g", DIM), ("ln2_b", DIM), ("router_bias", N_EXP)]


def offsets(table):
    at, found = 0, {}
    for name, n in table:
        found[name] = at
        at += n
    return found, at


COL_AT, N_COLS = offsets(COLS)
ROW_AT, N_ROWS = offsets(ROWS)
L0_ROW_AT, N_L0_ROWS = offsets(L0_ROWS)


QH = 704
Q_BLK = -(-QH // P)
ZERO_POINT = 128.0


def q_rows(u):
    return min(P, QH - u * P)


class Event:

    def __init__(self, sem, per, credit=0, base=0):
        self.sem, self.per, self.credit, self.base = sem, per, credit, base

    def grant(self, eng):
        eng.sem_inc(self.sem, self.credit)

    def done(self, trip, n=None):
        n = self.per - 1 if n is None else n
        return self.base + self.credit + trip * self.per + n + 1

    def room(self, trip, n=0):
        return self.base + trip * self.per + n + 1


class Bank:

    def __init__(self, sem, name, per):
        self.filled = Event(sem(name + "_filled"), per)
        self.freed = Event(sem(name + "_freed"), per, credit=1)

    def wait_room(self, pe, trip, n):
        pe.wait_ge(self.freed.sem, self.freed.room(trip, n))

    def wait_filled(self, eng, trip, n):
        eng.wait_ge(self.filled.sem, self.filled.done(trip, n))


def spread(ap, axis, n):
    wide = ap.unsqueeze(axis)
    shape = list(wide.shape)
    shape[axis] = n
    return wide.broadcast_to(shape)


def layer0(nc, mem, ctx, io):
    sb, ps, sem = mem.scoped(ctx, "l0")
    RING = 4
    CPARTS, HPH = 3, HEADS // 2
    x, ident, ones = mem.x, mem.ident, mem.ones
    col, row = mem.col, mem.l0_row
    w = mem.l0

    before = sb("before", [P, 1, P])
    after = sb("after", [P, P])
    lower = mem.lower
    exp_a = sb("exp_a", [P, HEADS])
    stats = sb("stats", [P, TILES, 6])
    moments = sb("moments", [P, TILES, 2])
    rstd = sb("rstd", [P, TILES])
    xn = sb("xn", [P, GT, DIM])
    xnT = sb("xnT", [P, DK, GROUP])
    pre = sb("pre", [P, CONV_BLK, CONV_K - 1 + GROUP])
    xbc = sb("xbc", [P, CONV_BLK, GROUP])
    zs = sb("zs", [P, Z_BLK, GROUP])
    hT = sb("hT", [P, L0_UNITS, GROUP])
    lg = sb("lg", [P, GT, N_EXP])
    lmax = sb("lmax", [P, GT])
    le = sb("le", [P, GT, N_EXP])
    rank = sb("rank", [P, GT, N_EXP])
    esum = sb("esum", [P, GT])
    comb = sb("comb", [P, GT, N_EXP])
    dtp = sb("dtp", [P, GT, HEADS])
    dta = sb("dta", [P, GT, HEADS])
    dt = sb("dt", [P, GT, HEADS])
    a = sb("a", [P, GT, HEADS])
    decay = sb("decay", [P, 3, GT, HEADS])
    wdt = sb("wdt", [P, GT, HEADS])
    xp = sb("xp", [P, 2, HEADS, 32])
    wx = sb("wx", [P, HID])
    btok = sb("btok", [P, STATE])
    cbm = sb("cbm", [P, 2, P])
    yoff = sb("yoff", [P, HID])
    st = sb("st", [P, HID])
    ncum = sb("ncum", [P, GT, HEADS])
    cum = sb("cum", [CPARTS * HPH, 2, GROUP], BF16)
    future = sb("future", [P, P], BF16)
    ident_b = sb("ident_b", [P, P], BF16)
    pick = sb("pick", [CPARTS * HPH, HPH], BF16)
    e = sb("e", [P, RING, 4, P])
    sg = e[:, 0:2, :, :].rearrange("p a h i -> p a (h i)")
    pair = e[:, 2:4, :, :].rearrange("p a h i -> p a (h i)")[:, :, 0:GT * N_EXP * N_EXP]
    gt = pair[:, 0, :].rearrange("p (t e f) -> p t e f", t=GT, e=N_EXP)
    eq = pair[:, 1, :].rearrange("p (t e f) -> p t e f", t=GT, e=N_EXP)
    yg = sb("yg", [P, Z_BLK, P])
    ysq = sb("ysq", [P, Z_BLK, P])
    rest = ysq[0:CPARTS * HPH, :, :].rearrange("p k i -> p (k i)")
    yr = sb("yr", [P, 2])

    bank = [ps(f"l0_b{i}", [P, GROUP]) for i in range(8)]
    HB = 16
    NCH = GT
    WIDE = 1 + 5 + L0_UNITS
    gate_b = Bank(sem, "l0_gate_bank", WIDE + NCH * HB // RING)
    up_b = Bank(sem, "l0_up_bank", WIDE + NCH * HB // RING)
    diff_b = [Bank(sem, f"l0_diff_bank{i}", NCH * HB // RING) for i in range(2)]

    def diff_slot(n):
        i, use = n % RING, n // RING
        return ((diff_b[0], 0, use), (diff_b[1], 1, use), (gate_b, 4, WIDE + use), (up_b, 5, WIDE + use))[i]

    y_b = Bank(sem, "l0_y_bank", 1 + NCH)
    tok_b = Bank(sem, "l0_tok_bank", 1 + 2 * NCH)
    down_b = Bank(sem, "l0_down_bank", L0_UNITS * GT // 2)
    misc_b = Bank(sem, "l0_misc_bank", 3 + 3 * NCH)

    moments_ready = Event(sem("l0_moments_ready"), 1)
    rstd_ready = Event(sem("l0_rstd_ready"), 1)
    xn_ready = Event(sem("l0_xn_ready"), 1)
    xnT_dve = Event(sem("l0_xnT_dve"), 1)
    xnT_act = Event(sem("l0_xnT_act"), 1)
    pre_ready = Event(sem("l0_pre_ready"), CONV_BLK)
    z_ready = Event(sem("l0_z_ready"), Z_BLK)
    conv_ready = Event(sem("l0_conv_ready"), CONV_BLK, credit=CONV_BLK)
    xbc_ready = Event(sem("l0_xbc_ready"), CONV_BLK)
    silu_ready = Event(sem("l0_silu_ready"), L0_UNITS)
    hid_ready = Event(sem("l0_hid_ready"), L0_UNITS, credit=2)
    scores_ready = Event(sem("l0_scores_ready"), 1)
    soft_ready = Event(sem("l0_soft_ready"), 1)
    a_ready = Event(sem("l0_a_ready"), 1)
    decay_ready = Event(sem("l0_decay_ready"), 2)
    bc_ready = Event(sem("l0_bc_ready"), NCH)
    xs_ready = Event(sem("l0_xs_ready"), NCH)
    yoff_ready = Event(sem("l0_yoff_ready"), NCH)
    state_ready = Event(sem("l0_state_ready"), NCH, credit=1)
    cum_ready = Event(sem("l0_cum_ready"), 1)
    e_ready = Event(sem("l0_e_ready"), NCH * HB)
    m_ready = Event(sem("l0_m_ready"), NCH * HB)
    strip_done = Event(sem("l0_strip_done"), NCH * HB, credit=RING)
    y_ready = Event(sem("l0_y_ready"), NCH)
    yg_ready = Event(sem("l0_yg_ready"), NCH)
    ysq_ready = Event(sem("l0_ysq_ready"), NCH)
    ssq_ready = Event(sem("l0_ssq_ready"), NCH)
    yr_ready = Event(sem("l0_yr_ready"), NCH)
    mask_ready = Event(sem("l0_mask_ready"), 1)
    expa_ready = Event(sem("l0_expa_ready"), 1)
    wn_ready = Event(sem("l0_wn_ready"), 1)
    reset_done = Event(sem("l0_reset_done"), 1)
    group_done = Event(sem("l0_group_done"), 1, credit=1)

    def heads_of(k):
        return [16 * (k // 4) + 4 * s + k % 4 for s in range(4)]

    def down_job(n):
        return n // 2, (2 * (n % 2), 2 * (n % 2) + 1)

    def bc_job(c):
        return 3 if c == 0 else 2 + 3 * c

    def off_job(c):
        return bc_job(c) + 1

    def out_job(c):
        return 4 + 3 * (c + 1) if c < NCH - 1 else 2 + 3 * NCH

    AHEAD = RING - 1
    EARLY = 2 * SHARED
    SOFT_AT = 8

    block = ctx.enter_context(nc.Block())

    @block.tensor
    def _(pe):
        def mm(out, lhsT, rhs, start=True, stop=True, **kw):
            return nc.tensor.matmul(out, lhsT, rhs, start=start, stop=stop, **kw)

        def down(g, n):
            u, tiles = down_job(n)
            down_b.wait_room(pe, g, n)
            if n % 2 == 0:
                pe.wait_ge(hid_ready.sem, hid_ready.done(g, u))
            for i, t in enumerate(tiles):
                last = mm(bank[6][:, DIM * i:DIM * (i + 1)], hT[:, u, t * P:(t + 1) * P], w.down[:, u, :])
            last.then_inc(down_b.filled.sem, 1)

        def out_proj(g, c):
            if c == 0:
                pe.wait_ge(wn_ready.sem, 1)
            pe.wait_ge(yg_ready.sem, yg_ready.done(g, c))
            pe.wait_ge(ysq_ready.sem, ysq_ready.done(g, c))
            misc_b.wait_room(pe, g, out_job(c))
            for k in range(Z_BLK):
                mm(bank[7][:, 256:257], ysq[:, k, :], ones[:, 0:1], k == 0, k == Z_BLK - 1)
            for k in range(Z_BLK):
                last = mm(bank[7][:, 0:DIM], yg[:, k, :], w.out[:, k, :], k == 0, k == Z_BLK - 1)
            last.then_inc(misc_b.filled.sem, 1)

        pe.wait_ge(mem.const_ready, mem.n_const)
        pe.wait_ge(mask_ready.sem, 1)
        with pe.Fori(0, BATCH) as b:
            with pe.Fori(0, HALVES) as half:
                g = b * HALVES + half
                pe.wait_ge(xn_ready.sem, xn_ready.done(g))
                for k, bk in ((0, gate_b), (1, up_b)):
                    bk.wait_room(pe, g, 0)
                    for t in range(GT):
                        last = nc.tensor.transpose(bank[4 + k][:, t * P:(t + 1) * P],
                                                   xn[:, t, k * P:(k + 1) * P], ident[:, :])
                    last.then_inc(bk.filled.sem, 1)
                pe.wait_ge(xnT_dve.sem, xnT_dve.done(g))
                pe.wait_ge(xnT_act.sem, xnT_act.done(g))
                pe.wait_ge(w.gate_sem, 16)
                pe.wait_ge(w.in_sem, 16)
                misc_b.wait_room(pe, g, 0)
                for t in range(GT):
                    for k in range(DK):
                        xt = xnT[:, k, t * P:(t + 1) * P]
                        mm(bank[7][:, 8 * t:8 * t + 8], xt, w.router[:, k, :], k == 0, k == DK - 1)
                    for k in range(DK):
                        xt = xnT[:, k, t * P:(t + 1) * P]
                        last = mm(bank[7][:, 64 + 64 * t:128 + 64 * t], xt,
                                  w.win[:, k, D_IN - HEADS:D_IN], k == 0, k == DK - 1)
                last.then_inc(misc_b.filled.sem, 1)
                for j in range(CONV_BLK + Z_BLK):
                    c0 = HID + j * P if j < CONV_BLK else (j - CONV_BLK) * P
                    bk = (gate_b, up_b)[j % 2]
                    bk.wait_room(pe, g, 1 + j // 2)
                    for k in range(DK):
                        last = mm(bank[4 + j % 2][:, :], w.win[:, k, c0:c0 + P], xnT[:, k, :],
                                  k == 0, k == DK - 1)
                    last.then_inc(bk.filled.sem, 1)
                pe.wait_ge(w.ffn_sem, 16 * 4)
                for u in range(L0_UNITS):
                    if u >= SHARED:
                        down(g, u - SHARED)
                    if u == L0_UNITS - 1:
                        pe.wait_ge(a_ready.sem, a_ready.done(g))
                        for q, (bk, at) in enumerate(((y_b, 2), (tok_b, 3))):
                            bk.wait_room(pe, g, 0)
                            for c in range(NCH):
                                for i in range(CPARTS):
                                    last = mm(bank[at][i * HPH:(i + 1) * HPH, c * P:(c + 1) * P],
                                              a[:, c, q * HPH:(q + 1) * HPH], before[:, 0, :],
                                              skip_group_check=True)
                            last.then_inc(bk.filled.sem, 1)
                        misc_b.wait_room(pe, g, 1)
                        a_all = a[:, :, :].rearrange("p c h -> p (c h)")
                        mm(bank[7][:, 0:256], before[:, 0, :], a_all)
                        mm(bank[7][:, 256:512], after[:, :], a_all).then_inc(misc_b.filled.sem, 1)
                    for i, bk in ((0, gate_b), (1, up_b)):
                        bk.wait_room(pe, g, 6 + u)
                        for k in range(DK):
                            last = mm(bank[4 + i][:, :], w.gu(u, k, i), xnT[:, k, :],
                                      k == 0, k == DK - 1)
                        last.then_inc(bk.filled.sem, 1)
                pe.wait_ge(xbc_ready.sem, xbc_ready.done(g))

                def by_tokens(c):
                    tok_b.wait_room(pe, g, 2 * c + 1)
                    for k in range(Z_BLK):
                        last = nc.tensor.transpose(bank[3][:, k * P:(k + 1) * P], xbc[:, k, c * P:(c + 1) * P],
                                                   ident[:, :])
                    last.then_inc(tok_b.filled.sem, 1)

                def b_and_cb(c):
                    tok = slice(c * P, (c + 1) * P)
                    misc_b.wait_room(pe, g, bc_job(c))
                    nc.tensor.transpose(bank[7][:, 0:P], xbc[:, 4, tok], ident[:, :])
                    mm(bank[7][:, P:2 * P], xbc[:, 4, tok], xbc[:, 5, tok]).then_inc(misc_b.filled.sem, 1)

                def diff(n):
                    bk, at, use = diff_slot(n)
                    bk.wait_room(pe, g, use)
                    c, k = n // HB, n % HB
                    mm(bank[at][:, :], ident_b[:, :], spread(future[:, :], 1, 4), True, False, skip_group_check=True)
                    for s, h in enumerate(heads_of(k)):
                        last = mm(bank[at][:, s * P:(s + 1) * P],
                                  pick[:, h % HPH:h % HPH + 1].broadcast_to([CPARTS * HPH, P]),
                                  cum[:, h // HPH, c * P:(c + 1) * P], False, True, skip_group_check=True)
                    last.then_inc(bk.filled.sem, 1)

                pe.wait_ge(cum_ready.sem, cum_ready.done(g))
                by_tokens(0)
                for n in range(AHEAD):
                    diff(n)
                misc_b.wait_room(pe, g, 2)
                mm(bank[7][:, 0:256], ones[:, 0:P], a_all).then_inc(misc_b.filled.sem, 1)
                b_and_cb(0)
                for c in range(NCH):
                    tok = slice(c * P, (c + 1) * P)
                    if c == 0:
                        pe.wait_ge(reset_done.sem, reset_done.done(b))
                    pe.wait_ge(state_ready.sem, state_ready.room(g, c))
                    misc_b.wait_room(pe, g, off_job(c))
                    mm(bank[7][:, :], xbc[:, 5, tok], st[:, :]).then_inc(misc_b.filled.sem, 1)
                    pe.wait_ge(xs_ready.sem, xs_ready.done(g, c))
                    pe.wait_ge(bc_ready.sem, bc_ready.done(g, c))
                    tok_b.wait_room(pe, g, 2 * c + 2)
                    mm(bank[3][:, :], btok[:, :], wx[:, :]).then_inc(tok_b.filled.sem, 1)
                    for k in range(HB):
                        n = c * HB + k
                        blk = k // 4
                        if k == 0:
                            y_b.wait_room(pe, g, 1 + c)
                        pe.wait_ge(m_ready.sem, m_ready.done(g, n))
                        for s, h in enumerate(heads_of(k)):
                            last = mm(bank[2][32 * s:32 * s + 32, blk * P:(blk + 1) * P],
                                      xp[:, c % 2, h, :], e[:, n % RING, s, :], k % 4 == 0, False,
                                      skip_group_check=True)
                        last.then_inc(strip_done.sem, 1)
                        if n + AHEAD < NCH * HB:
                            diff(n + AHEAD)
                        if k % 4 == 3:
                            if k == 3:
                                pe.wait_ge(yoff_ready.sem, yoff_ready.done(g, c))
                            last = mm(bank[2][:, blk * P:(blk + 1) * P], yoff[:, blk * P:(blk + 1) * P],
                                      ident[:, :], False, True, skip_group_check=True)
                            if k == HB - 1:
                                last.then_inc(y_b.filled.sem, 1)
                        if k % 4 == 1:
                            down(g, EARLY + c * 4 + k // 4)
                        if k == 8 and c > 0:
                            out_proj(g, c - 1)
                        if k == 6 and c + 1 < NCH:
                            by_tokens(c + 1)
                        if k == 14 and c + 1 < NCH:
                            b_and_cb(c + 1)
                out_proj(g, NCH - 1)

    @block.scalar
    def _(act):
        act.wait_ge(mem.l0_row_ready, 16)
        nc.scalar.activation(exp_a[:, :], row("A_log"), ACT.Exp).then_inc(expa_ready.sem, 1)
        with act.Fori(0, BATCH) as b:
            with act.Fori(0, HALVES) as half:
                g = b * HALVES + half
                up_b.wait_filled(act, g, 0)
                nc.scalar.activation(xnT[:, 1, :], bank[5][:, :], ACT.Copy).then_inc(xnT_act.sem, 1)
                act.drain().then_inc(up_b.freed.sem, 1)
                for j in range(CONV_BLK + Z_BLK):
                    bk = (gate_b, up_b)[j % 2]
                    bk.wait_filled(act, g, 1 + j // 2)
                    if j < CONV_BLK:
                        if j == 0:
                            act.wait_ge(conv_ready.sem, conv_ready.room(g, CONV_BLK - 1))
                            act.wait_ge(reset_done.sem, reset_done.done(b))
                        nc.scalar.activation(pre[:, j, CONV_K - 1:], bank[4 + j % 2][:, :],
                                             ACT.Copy).then_inc(pre_ready.sem, 1)
                    else:
                        if j == CONV_BLK:
                            act.wait_ge(group_done.sem, group_done.room(g))
                        nc.scalar.activation(zs[:, j - CONV_BLK, :], bank[4 + j % 2][:, :],
                                             ACT.Silu).then_inc(z_ready.sem, 1)
                    act.drain().then_inc(bk.freed.sem, 1)

                def softplus():
                    act.wait_ge(scores_ready.sem, scores_ready.done(g))
                    nc.scalar.activation(dta[:, :, :], dtp[:, :, :], ACT.Abs)
                    nc.scalar.activation(le[:, :, :], lg[:, :, :], ACT.Exp)
                    act.drain()
                    nc.scalar.activation(dta[:, :, :], dta[:, :, :], ACT.Exp, scale=-1.0)
                    act.drain()
                    nc.scalar.activation(dta[:, :, :], dta[:, :, :], ACT.Ln, bias=1.0).then_inc(soft_ready.sem, 1)

                for u in range(L0_UNITS):
                    gate_b.wait_filled(act, g, 6 + u)
                    act.wait_ge(hid_ready.sem, hid_ready.room(g, u))
                    nc.scalar.activation(sg[:, u % 2, :], bank[4][:, :], ACT.Silu).then_inc(silu_ready.sem, 1)
                    act.drain().then_inc(gate_b.freed.sem, 1)
                    if u < CONV_BLK:
                        act.wait_ge(conv_ready.sem, conv_ready.done(g, u))
                        nc.scalar.activation(xbc[:, u, :], xbc[:, u, :], ACT.Silu).then_inc(xbc_ready.sem, 1)
                    if u == SOFT_AT:
                        softplus()
                misc_b.wait_filled(act, g, 1)
                nc.scalar.activation(ncum[:, :, :].rearrange("p c h -> p (c h)"), bank[7][:, 0:256], ACT.Copy,
                                     scale=-1.0)
                nc.scalar.activation(decay[:, 0:2, :, :].rearrange("p s c h -> p (s c h)"), bank[7][:, :],
                                     ACT.Exp).then_inc(decay_ready.sem, 1)
                act.drain().then_inc(misc_b.freed.sem, 1)
                misc_b.wait_filled(act, g, 2)
                nc.scalar.activation(decay[:, 2, :, :].rearrange("p c h -> p (c h)"), bank[7][:, 0:256],
                                     ACT.Exp).then_inc(decay_ready.sem, 1)
                act.drain().then_inc(misc_b.freed.sem, 1)

                act.wait_ge(hid_ready.sem, hid_ready.done(g, L0_UNITS - 1))

                def take_y(c):
                    y_b.wait_filled(act, g, 1 + c)
                    if c > 0:
                        act.wait_ge(misc_b.filled.sem, misc_b.filled.done(g, out_job(c - 1)))
                    nc.scalar.activation(yg[:, :, :].rearrange("p k i -> p (k i)"), bank[2][:, :],
                                         ACT.Copy).then_inc(y_ready.sem, 1)
                    act.drain().then_inc(y_b.freed.sem, 1)

                def square(c):
                    act.wait_ge(yg_ready.sem, yg_ready.done(g, c))
                    nc.scalar.activation(ysq[:, :, :], yg[:, :, :], ACT.Square).then_inc(ysq_ready.sem, 1)

                for c in range(NCH):
                    for k in range(HB):
                        n = c * HB + k
                        bk, at, use = diff_slot(n)
                        bk.wait_filled(act, g, use)
                        act.wait_ge(strip_done.sem, strip_done.room(g, n))
                        for s, h in enumerate(heads_of(k)):
                            last = nc.scalar.activation(e[:, n % RING, s, :], bank[at][:, s * P:(s + 1) * P],
                                                        ACT.Exp, bias=ncum[:, c, h:h + 1])
                        last.then_inc(e_ready.sem, 1)
                        act.drain().then_inc(bk.freed.sem, 1)
                        if k == AHEAD - 1 and c > 0:
                            take_y(c - 1)
                        if k == 5 and c > 0:
                            square(c - 1)
                take_y(NCH - 1)
                square(NCH - 1)

    @block.gpsimd
    def _(pool):
        nc.gpsimd.memset(before[:, :, :], 1.0)
        nc.gpsimd.memset(after[:, :], 1.0)
        nc.gpsimd.memset(future[:, :], 0.0)
        pool.drain()
        nc.gpsimd.affine_select(out=before[:, 0, :], in_=before[:, 0, :], compare_op=ALU.is_ge, fill=0.0,
                                base=0, pattern=[[1, P]], channel_multiplier=-1)
        nc.gpsimd.affine_select(out=future[:, :], in_=future[:, :], compare_op=ALU.is_ge, fill=-1e30,
                                base=0, pattern=[[1, P]], channel_multiplier=-1)
        nc.gpsimd.affine_select(out=after[:, :], in_=after[:, :], compare_op=ALU.is_gt, fill=0.0,
                                base=0, pattern=[[-1, P]], channel_multiplier=1)
        pool.drain().then_inc(mask_ready.sem, 1)
        pool.wait_ge(moments_ready.sem, 1)
        nc.gpsimd.tensor_tensor(rstd[:, :], moments[:, :, 1], mem.neg_half[:, :], ALU.pow).then_inc(rstd_ready.sem, 1)
        pool.wait_ge(mem.col_ready, 16)
        pool.wait_ge(w.out_sem, 16)
        for k in range(Z_BLK):
            nc.gpsimd.tensor_scalar(w.out[:, k, :], w.out[:, k, :], col("norm_w", k), None, ALU.mult)
        pool.drain().then_inc(wn_ready.sem, 1)
        with pool.Fori(0, BATCH) as b:
            with pool.Fori(0, HALVES) as half:
                g = b * HALVES + half
                def out_scale(c):
                    pool.wait_ge(ssq_ready.sem, ssq_ready.done(g, c))
                    nc.gpsimd.tensor_tensor(yr[:, 1:2], yr[:, 0:1], mem.neg_half[:, 0:1], ALU.pow).then_inc(
                        yr_ready.sem, 1)

                def finish_y(c):
                    tok = slice(c * P, (c + 1) * P)
                    if c == 0:
                        pool.wait_ge(xbc_ready.sem, xbc_ready.done(g))
                        pool.wait_ge(z_ready.sem, z_ready.done(g))
                        pool.wait_ge(cum_ready.sem, cum_ready.done(g))
                    else:
                        pool.wait_ge(misc_b.filled.sem, misc_b.filled.done(g, out_job(c - 1)))
                    d0 = COL_AT["D"]
                    nc.gpsimd.tensor_tensor(ysq[:, :, :], xbc[:, 0:Z_BLK, tok],
                                            spread(mem.cols[:, d0:d0 + Z_BLK], 2, P), ALU.mult)
                    pool.drain()
                    pool.wait_ge(y_ready.sem, y_ready.done(g, c))
                    nc.gpsimd.tensor_tensor(yg[:, :, :], yg[:, :, :], ysq[:, :, :], ALU.add)
                    pool.drain()
                    nc.gpsimd.tensor_tensor(yg[:, :, :], yg[:, :, :], zs[:, :, tok], ALU.mult).then_inc(
                        yg_ready.sem, 1)

                for c in range(NCH):
                    finish_y(c)
                    if c < NCH - 1:
                        out_scale(c)
                out_scale(NCH - 1)

    @block.vector
    def _(dve):
        def down_add(g, n):
            u, tiles = down_job(n)
            dve.drain()
            down_b.wait_filled(dve, g, n)
            for i, t in enumerate(tiles):
                xt = x[:, g * GT + t, :]
                scale = comb[:, t, u - SHARED:u - SHARED + 1] if u >= SHARED else 1.0
                last = nc.vector.scalar_tensor_tensor(out=xt, in0=bank[6][:, DIM * i:DIM * (i + 1)], scalar=scale,
                                                      in1=xt, op0=ALU.mult, op1=ALU.add)
            last.then_inc(down_b.freed.sem, 1)

        def out_stats(g, c):
            misc_b.wait_filled(dve, g, out_job(c))
            nc.vector.tensor_scalar(yr[:, 0:1], bank[7][:, 256:257], 1.0 / HID, 1e-5, ALU.mult, ALU.add).then_inc(
                ssq_ready.sem, 1)

        def out_add(g, c):
            dve.drain()
            dve.wait_ge(yr_ready.sem, yr_ready.done(g, c))
            xt = x[:, g * GT + c, :]
            nc.vector.scalar_tensor_tensor(out=xt, in0=bank[7][:, 0:DIM], scalar=yr[:, 1:2], in1=xt,
                                           op0=ALU.mult, op1=ALU.add).then_inc(misc_b.freed.sem, 1)

        for bk in (gate_b, up_b, *diff_b, y_b, tok_b, down_b, misc_b):
            bk.freed.grant(dve)
        for ev in (conv_ready, hid_ready, group_done, state_ready, strip_done):
            ev.grant(dve)
        dve.wait_ge(mem.col_ready, 16)
        dve.wait_ge(mem.const_ready, mem.n_const)
        dve.wait_ge(mask_ready.sem, 1)
        dve.wait_ge(expa_ready.sem, 1)
        dve.wait_ge(mem.l0_row_ready, 16)
        nc.vector.tensor_copy(ident_b[:, :], ident[:, :])
        for i in range(CPARTS):
            rows = slice(i * HPH, (i + 1) * HPH)
            nc.vector.tensor_copy(pick[rows, :], ident[rows, rows])
        dve.wait_ge(mem.x_ready, 16 * (TILES // GT))
        for t in range(TILES):
            nc.vector.bn_stats(stats[:, t, :], x[:, t, :])
        dve.drain()
        for t in range(TILES):
            nc.vector.bn_aggr(moments[:, t, :], stats[:, t, :])
        dve.drain()
        nc.vector.tensor_scalar(moments[:, :, 1], moments[:, :, 1], 1e-5, None, ALU.add).then_inc(
            moments_ready.sem, 1)
        nc.vector.memset(xp[:, :, :, :], 0.0)
        dve.wait_ge(rstd_ready.sem, 1)
        with dve.Fori(0, BATCH) as b:
            nc.vector.memset(pre[:, :, 0:CONV_K - 1], 0.0)
            nc.vector.memset(st[:, :], 0.0)
            dve.drain().then_inc(reset_done.sem, 1)
            with dve.Fori(0, HALVES) as half:
                g = b * HALVES + half
                for t in range(GT):
                    at = g * GT + t
                    last = nc.vector.tensor_scalar(xn[:, t, :], x[:, at, :], moments[:, at, 0:1],
                                                   rstd[:, bass.ds(at, 1)], ALU.subtract, ALU.mult)
                last.then_inc(xn_ready.sem, 1)
                gate_b.wait_filled(dve, g, 0)
                nc.vector.tensor_copy(xnT[:, 0, :], bank[4][:, :]).then_inc(xnT_dve.sem, 1)
                dve.drain().then_inc(gate_b.freed.sem, 1)
                misc_b.wait_filled(dve, g, 0)
                nc.vector.tensor_copy(lg[:, :, :], bank[7][:, 0:32].rearrange("p (t e) -> p t e", e=N_EXP))
                nc.vector.tensor_tensor(dtp[:, :, :], bank[7][:, 64:320].rearrange("p (t h) -> p t h", h=HEADS),
                                        spread(row("dt_bias"), 1, GT), ALU.add)
                dve.drain().then_inc(misc_b.freed.sem, 1)
                nc.vector.tensor_reduce(lmax[:, :], lg[:, :, :], AX.X, ALU.max)
                nc.vector.tensor_tensor(gt[:, :, :, :], spread(lg[:, :, :], 2, N_EXP), spread(lg[:, :, :], 3, N_EXP),
                                        ALU.is_gt)
                nc.vector.tensor_tensor(eq[:, :, :, :], spread(lg[:, :, :], 2, N_EXP), spread(lg[:, :, :], 3, N_EXP),
                                        ALU.is_equal)
                dve.drain()
                nc.vector.tensor_tensor(lg[:, :, :], lg[:, :, :], spread(lmax[:, :], 2, N_EXP), ALU.subtract)
                nc.vector.tensor_tensor(eq[:, :, :, :], eq[:, :, :, :], spread(lower[:, :, :], 1, GT), ALU.mult)
                dve.drain().then_inc(scores_ready.sem, 1)
                nc.vector.tensor_tensor(gt[:, :, :, :], gt[:, :, :, :], eq[:, :, :, :], ALU.add)
                dve.drain()
                nc.vector.tensor_reduce(rank[:, :, :], gt[:, :, :, :], AX.X, ALU.add)
                dve.drain()
                nc.vector.tensor_scalar(rank[:, :, :], rank[:, :, :], 2.0, None, ALU.is_lt)

                def conv(j):
                    dve.wait_ge(pre_ready.sem, pre_ready.done(g, j))
                    nc.vector.tensor_scalar(xbc[:, j, :], pre[:, j, 0:GROUP], col("conv_w", j * CONV_K), None, ALU.mult)
                    for i in range(1, CONV_K):
                        dve.drain()
                        nc.vector.scalar_tensor_tensor(out=xbc[:, j, :], in0=pre[:, j, i:i + GROUP],
                                                       scalar=col("conv_w", j * CONV_K + i), in1=xbc[:, j, :],
                                                       op0=ALU.mult, op1=ALU.add)
                    nc.vector.tensor_copy(pre[:, j, 0:CONV_K - 1], pre[:, j, GROUP:])
                    dve.drain().then_inc(conv_ready.sem, 1)

                def expert_weights():
                    dve.wait_ge(soft_ready.sem, soft_ready.done(g))
                    nc.vector.scalar_tensor_tensor(out=dt[:, :, :], in0=dtp[:, :, :], scalar=0.0, in1=dta[:, :, :],
                                                   op0=ALU.max, op1=ALU.add)
                    nc.vector.tensor_tensor(comb[:, :, :], le[:, :, :], rank[:, :, :], ALU.mult)
                    dve.drain()
                    nc.vector.scalar_tensor_tensor(out=a[:, :, :], in0=dt[:, :, :], scalar=-1.0,
                                                   in1=spread(exp_a[:, :], 1, GT), op0=ALU.mult, op1=ALU.mult)
                    nc.vector.tensor_reduce(esum[:, :], comb[:, :, :], AX.X, ALU.add)
                    dve.drain().then_inc(a_ready.sem, 1)
                    nc.vector.reciprocal(esum[:, :], esum[:, :])
                    dve.drain()
                    nc.vector.tensor_tensor(comb[:, :, :], comb[:, :, :], spread(esum[:, :], 2, N_EXP), ALU.mult)
                    dve.drain()

                def split_cum():
                    mid, low = slice(0, 2 * HPH), slice(0, HPH)
                    for q, (bk, at) in enumerate(((y_b, 2), (tok_b, 3))):
                        bk.wait_filled(dve, g, 0)
                        nc.vector.tensor_copy(cum[:, q, :], bank[at][0:CPARTS * HPH, :])
                        dve.drain()
                        nc.vector.tensor_tensor(rest[:, :], bank[at][0:CPARTS * HPH, :], cum[:, q, :], ALU.subtract)
                        dve.drain().then_inc(bk.freed.sem, 1)
                        nc.vector.tensor_copy(cum[mid, q, :], rest[mid, :])
                        dve.drain()
                        nc.vector.tensor_tensor(cum[low, q, :], rest[low, :], cum[low, q, :], ALU.subtract)
                        dve.drain()
                    dve.drain().then_inc(cum_ready.sem, 1)

                for j in range(CONV_BLK - 2):
                    conv(j)
                for u in range(L0_UNITS):
                    if u >= SHARED:
                        down_add(g, u - SHARED)
                    up_b.wait_filled(dve, g, 6 + u)
                    dve.wait_ge(silu_ready.sem, silu_ready.done(g, u))
                    nc.vector.tensor_tensor(hT[:, u, :], sg[:, u % 2, :], bank[5][:, :], ALU.mult).then_inc(
                        hid_ready.sem, 1)
                    dve.drain().then_inc(up_b.freed.sem, 1)
                    if u < 2:
                        conv(CONV_BLK - 2 + u)
                    if u == SOFT_AT + 1:
                        expert_weights()
                    if u == L0_UNITS - 2:
                        split_cum()
                dve.wait_ge(decay_ready.sem, decay_ready.done(g, 0))
                nc.vector.tensor_tensor(wdt[:, :, :], decay[:, 1, :, :], dt[:, :, :], ALU.mult)
                dve.drain()

                xs3 = bank[3][:, :].rearrange("p (h e) -> p h e", e=HEAD_P)

                def take_xs(c):
                    tok_b.wait_filled(dve, g, 2 * c + 1)
                    for q in range(4):
                        nc.vector.tensor_tensor(
                            xp[:, c % 2, q::4, 8 * q:8 * q + 8],
                            xs3[:, q::4, :], spread(dt[:, c, q::4], 2, HEAD_P), ALU.mult)
                    nc.vector.tensor_tensor(wx[:, :].rearrange("p (h e) -> p h e", e=HEAD_P), xs3,
                                            spread(wdt[:, c, :], 2, HEAD_P), ALU.mult)
                    dve.drain().then_inc(xs_ready.sem, 1)
                    dve.drain().then_inc(tok_b.freed.sem, 1)

                def take_cb(c):
                    misc_b.wait_filled(dve, g, bc_job(c))
                    nc.vector.tensor_copy(btok[:, :], bank[7][:, 0:P])
                    nc.vector.tensor_tensor(cbm[:, c % 2, :], bank[7][:, P:2 * P], before[:, 0, :], ALU.mult)
                    dve.drain().then_inc(bc_ready.sem, 1)
                    dve.drain().then_inc(misc_b.freed.sem, 1)

                take_xs(0)
                take_cb(0)
                for c in range(NCH):
                    for k in range(HB):
                        n = c * HB + k
                        dve.wait_ge(e_ready.sem, e_ready.done(g, n))
                        nc.vector.scalar_tensor_tensor(out=e[:, n % RING, :, :], in0=e[:, n % RING, :, :], scalar=1.0,
                                                       in1=spread(cbm[:, c % 2, :], 1, 4), op0=ALU.min,
                                                       op1=ALU.mult).then_inc(m_ready.sem, 1)
                        if k == 0:
                            misc_b.wait_filled(dve, g, off_job(c))
                            nc.vector.tensor_tensor(yoff[:, :].rearrange("p (h e) -> p h e", e=HEAD_P),
                                                    bank[7][:, :].rearrange("p (h e) -> p h e", e=HEAD_P),
                                                    spread(decay[:, 0, c, :], 2, HEAD_P), ALU.mult).then_inc(
                                yoff_ready.sem, 1)
                            dve.drain().then_inc(misc_b.freed.sem, 1)
                            if c == 0:
                                dve.wait_ge(decay_ready.sem, decay_ready.done(g, 1))
                            st3 = st[:, :].rearrange("p (h e) -> p h e", e=HEAD_P)
                            nc.vector.tensor_tensor(st3, st3, spread(decay[:, 2, c, :], 2, HEAD_P), ALU.mult)
                            dve.drain()
                            tok_b.wait_filled(dve, g, 2 * c + 2)
                            nc.vector.tensor_tensor(st[:, :], st[:, :], bank[3][:, :], ALU.add).then_inc(
                                state_ready.sem, 1)
                            dve.drain().then_inc(tok_b.freed.sem, 1)
                        if k % 4 == 3:
                            down_add(g, EARLY + c * 4 + k // 4)
                        if k == 8 and c + 1 < NCH:
                            take_xs(c + 1)
                        if k == 10 and c > 0:
                            out_stats(g, c - 1)
                        if k == 13 and c > 0:
                            out_add(g, c - 1)
                        if k == 15 and c + 1 < NCH:
                            take_cb(c + 1)
                out_stats(g, NCH - 1)
                out_add(g, NCH - 1)
                dve.drain().then_inc(group_done.sem, 1)



class Jobs:

    def __init__(self, mem, banks, trips, order):
        self.banks, self.place = banks, {}
        uses = {}
        for job, b in order:
            self.place[job] = (b, uses.get(b, 0))
            uses[b] = uses.get(b, 0) + 1
        self.filled, self.freed = {}, {}
        for b, n in uses.items():
            self.filled[b] = Event(mem.psum_filled[b], n, base=mem.filled_base[b])
            self.freed[b] = Event(mem.psum_freed[b], n, credit=1, base=mem.freed_base[b])
            mem.filled_base[b] += trips * n
            mem.freed_base[b] += trips * n + 1

    def grant(self, eng):
        for event in self.freed.values():
            event.grant(eng)

    def bank(self, job):
        return self.banks[:, self.place[job][0], :]

    def wait_room(self, pe, trip, job):
        b, n = self.place[job]
        pe.wait_ge(self.freed[b].sem, self.freed[b].room(trip, n))

    def fill(self, last, job):
        last.then_inc(self.filled[self.place[job][0]].sem, 1)

    def wait_filled(self, eng, trip, job):
        b, n = self.place[job]
        eng.wait_ge(self.filled[b].sem, self.filled[b].done(trip, n))

    def free(self, last, job):
        last.then_inc(self.freed[self.place[job][0]].sem, 1)


HB_TILES = SEQ // P
FFN_BLK = 8
BIT_EPS = 1e-8


def layer1(nc, mem, ctx, io):
    sb, ps, sem = mem.scoped(ctx, "l1")
    x, ident, ones, col, row, w = mem.x, mem.ident, mem.ones, mem.col, mem.row, mem.l1

    stats = sb("stats", [P, TILES, 6])
    moments = sb("moments", [P, TILES, 2])
    rstd = sb("rstd", [P, TILES])
    xn = sb("xn", [P, GT, DIM])
    xnT = sb("xnT", [P, DK, GROUP])
    qT = sb("qT", [P, DK, SEQ])
    kT = sb("kT", [P, DK, SEQ])
    v = sb("v", [P, HB_TILES, DIM])
    hT = sb("hT", [P, FFN_BLK, GROUP])
    prob = sb("prob", [P, 2, SEQ])
    pT = sb("pT", [P, HB_TILES, GROUP])
    cT = sb("cT", [P, DK, GROUP])
    nmax = sb("nmax", [P, 2, 1])
    prob_sum = sb("prob_sum", [P, HB_TILES])
    rsum = sb("rsum", [P, GT])
    bias_row = sb("bias_row", [P, DIM])
    wabs = sb("wabs", [P, 2])
    thr = sb("thr", [P, 2, 2])
    below = pT[:, 0:4, :].rearrange("p a n -> p (a n)")
    banks = ps("l1_banks", [P, 8, GROUP])

    order = []
    at = 0
    for hf in range(HALVES):
        names = [("xnT", hf, k) for k in range(DK)] + [("k", hf, k) for k in range(DK)]
        names += [("q", hf, k) for k in range(DK)] + [("v", hf, t) for t in range(GT // 2)]
        names += [("f", hf, k) for k in range(FFN_BLK)] + [("d", hf, t) for t in range(GT // 2)]
        for n in names:
            order.append((n, at % 8))
            at += 1

    def score_jobs(qt):
        return [(("s", qt, i), 2 * (qt % 2) + i) for i in range(2)]

    order += score_jobs(0)
    for qt in range(HB_TILES):
        if qt + 1 < HB_TILES:
            order += score_jobs(qt + 1)
        order += [(("t", qt, i), 4 + i) for i in range(2)]
        if qt % GT == GT - 1:
            hf = qt // GT
            order += [(("c", hf, k), 6 + k) for k in range(DK)]
            order += [(("o", hf, t), 6 + t) for t in range(GT // 2)]
    jobs = Jobs(mem, banks, BATCH, order)

    moments_ready = Event(sem("l1_moments_ready"), 1)
    rstd_ready = Event(sem("l1_rstd_ready"), 1)
    xn_ready = Event(sem("l1_xn_ready"), HALVES)
    xnT_dve = Event(sem("l1_xnT_dve"), HALVES)
    xnT_act = Event(sem("l1_xnT_act"), HALVES)
    bias_added = Event(sem("l1_bias_added"), HALVES)
    kq_ready = Event(sem("l1_kq_ready"), 4 * HALVES)
    v_ready = Event(sem("l1_v_ready"), 2 * HALVES)
    h_ready = Event(sem("l1_h_ready"), FFN_BLK * HALVES)
    nmax_ready = Event(sem("l1_nmax_ready"), HB_TILES)
    prob_ready = Event(sem("l1_prob_ready"), HB_TILES)
    pT_dve = Event(sem("l1_pT_dve"), HB_TILES)
    pT_act = Event(sem("l1_pT_act"), HB_TILES)
    c_ready = Event(sem("l1_c_ready"), 2 * HALVES)
    weight_sum = sem("l1_weight_sum")
    weight_mean = sem("l1_weight_mean")
    ternary = sem("l1_ternary")

    block = ctx.enter_context(nc.Block())

    @block.sync
    def _(sp):
        mem.load_l2(sp, io)
        mem.load_l3a(sp, io)

    @block.tensor
    def _(pe):
        def mm(out, lhsT, rhs, start=True, stop=True):
            return nc.tensor.matmul(out, lhsT, rhs, start=start, stop=stop)

        pe.wait_ge(weight_sum, 1)
        mm(banks[:, 0, 0:2], ones[:, :], wabs[:, :]).then_inc(weight_mean, 1)
        pe.wait_ge(w.sem, 16 * 4)
        pe.wait_ge(ternary, 1)
        with pe.Fori(0, BATCH) as b:
            for hf in range(HALVES):
                pe.wait_ge(xn_ready.sem, xn_ready.done(b, hf))
                for k in range(DK):
                    jobs.wait_room(pe, b, ("xnT", hf, k))
                    for t in range(GT):
                        last = nc.tensor.transpose(jobs.bank(("xnT", hf, k))[:, t * P:(t + 1) * P],
                                                   xn[:, t, k * P:(k + 1) * P], ident[:, :])
                    jobs.fill(last, ("xnT", hf, k))
                pe.wait_ge(xnT_dve.sem, xnT_dve.done(b, hf))
                pe.wait_ge(xnT_act.sem, xnT_act.done(b, hf))
                for name, base in (("k", DIM), ("q", 0)):
                    for m in range(DK):
                        jobs.wait_room(pe, b, (name, hf, m))
                        for k in range(DK):
                            last = mm(jobs.bank((name, hf, m)), w.qkv[:, k, base + m * P:base + (m + 1) * P],
                                      xnT[:, k, :], k == 0, k == DK - 1)
                        jobs.fill(last, (name, hf, m))
                for t in range(GT // 2):
                    jobs.wait_room(pe, b, ("v", hf, t))
                    for i in range(2):
                        for k in range(DK):
                            last = mm(jobs.bank(("v", hf, t))[:, i * DIM:(i + 1) * DIM],
                                      xnT[:, k, (2 * t + i) * P:(2 * t + i + 1) * P], w.qkv[:, k, 2 * DIM:],
                                      k == 0, k == DK - 1)
                    jobs.fill(last, ("v", hf, t))
                for f in range(FFN_BLK):
                    jobs.wait_room(pe, b, ("f", hf, f))
                    for k in range(DK):
                        last = mm(jobs.bank(("f", hf, f)), w.w1[:, k, f * P:(f + 1) * P], xnT[:, k, :],
                                  k == 0, k == DK - 1)
                    jobs.fill(last, ("f", hf, f))
                pe.wait_ge(h_ready.sem, h_ready.done(b, (hf + 1) * FFN_BLK - 1))
                for t in range(GT // 2):
                    jobs.wait_room(pe, b, ("d", hf, t))
                    for i in range(2):
                        for f in range(FFN_BLK):
                            last = mm(jobs.bank(("d", hf, t))[:, i * DIM:(i + 1) * DIM],
                                      hT[:, f, (2 * t + i) * P:(2 * t + i + 1) * P], w.w2[:, f, :],
                                      f == 0, f == FFN_BLK - 1)
                    jobs.fill(last, ("d", hf, t))

            def scores(qt):
                for i in range(2):
                    jobs.wait_room(pe, b, ("s", qt, i))
                    for k in range(DK):
                        last = mm(jobs.bank(("s", qt, i)), qT[:, k, qt * P:(qt + 1) * P],
                                  kT[:, k, i * GROUP:(i + 1) * GROUP], k == 0, k == DK - 1)
                    jobs.fill(last, ("s", qt, i))

            pe.wait_ge(kq_ready.sem, kq_ready.done(b))
            pe.wait_ge(v_ready.sem, v_ready.done(b))
            scores(0)
            for qt in range(HB_TILES):
                if qt + 1 < HB_TILES:
                    scores(qt + 1)
                pe.wait_ge(prob_ready.sem, prob_ready.done(b, qt))
                for i in range(2):
                    jobs.wait_room(pe, b, ("t", qt, i))
                    for t in range(GT):
                        kt = i * GT + t
                        last = nc.tensor.transpose(jobs.bank(("t", qt, i))[:, t * P:(t + 1) * P],
                                                   prob[:, qt % 2, kt * P:(kt + 1) * P], ident[:, :])
                    jobs.fill(last, ("t", qt, i))
                if qt % GT == GT - 1:
                    hf = qt // GT
                    pe.wait_ge(pT_dve.sem, pT_dve.done(b, qt))
                    pe.wait_ge(pT_act.sem, pT_act.done(b, qt))
                    for m in range(DK):
                        jobs.wait_room(pe, b, ("c", hf, m))
                        for kt in range(HB_TILES):
                            last = mm(jobs.bank(("c", hf, m)), v[:, kt, m * P:(m + 1) * P], pT[:, kt, :],
                                      kt == 0, kt == HB_TILES - 1)
                        jobs.fill(last, ("c", hf, m))
                    pe.wait_ge(c_ready.sem, c_ready.done(b, 2 * hf + 1))
                    for t in range(GT // 2):
                        jobs.wait_room(pe, b, ("o", hf, t))
                        for i in range(2):
                            for k in range(DK):
                                last = mm(jobs.bank(("o", hf, t))[:, i * DIM:(i + 1) * DIM],
                                          cT[:, k, (2 * t + i) * P:(2 * t + i + 1) * P], w.out[:, k, :],
                                          k == 0, k == DK - 1)
                        jobs.fill(last, ("o", hf, t))

    @block.scalar
    def _(act):
        act.wait_ge(w.sem, 16 * 4)
        for i, part in enumerate((w.w1, w.w2)):
            last = nc.scalar.activation(below[:, :], part.rearrange("p a n -> p (a n)"), ACT.Abs,
                                        accum_out=wabs[:, i:i + 1])
            act.drain()
        act.drain().then_inc(weight_sum, 1)
        with act.Fori(0, BATCH) as b:
            for hf in range(HALVES):
                half = slice(hf * GROUP, (hf + 1) * GROUP)
                jobs.wait_filled(act, b, ("xnT", hf, 1))
                nc.scalar.activation(xnT[:, 1, :], jobs.bank(("xnT", hf, 1)), ACT.Copy).then_inc(xnT_act.sem, 1)
                jobs.free(act.drain(), ("xnT", hf, 1))
                for name, dst, base in (("k", kT, 2), ("q", qT, 0)):
                    for m in range(DK):
                        jobs.wait_filled(act, b, (name, hf, m))
                        nc.scalar.activation(dst[:, m, half], jobs.bank((name, hf, m)), ACT.Identity,
                                             bias=col("b_qkv", base + m)).then_inc(kq_ready.sem, 1)
                        jobs.free(act.drain(), (name, hf, m))
                for f in range(FFN_BLK):
                    jobs.wait_filled(act, b, ("f", hf, f))
                    nc.scalar.activation(hT[:, f, :], jobs.bank(("f", hf, f)), ACT.Gelu,
                                         bias=col("b1", f)).then_inc(h_ready.sem, 1)
                    jobs.free(act.drain(), ("f", hf, f))

            def turn(qt):
                jobs.wait_filled(act, b, ("t", qt, 1))
                if qt % GT == 0 and qt > 0:
                    jobs.wait_filled(act, b, ("c", qt // GT - 1, 1))
                at = (qt % GT) * P
                nc.scalar.activation(pT[:, GT:, at:at + P],
                                     jobs.bank(("t", qt, 1)).rearrange("p (t q) -> p t q", t=GT),
                                     ACT.Copy).then_inc(pT_act.sem, 1)
                jobs.free(act.drain(), ("t", qt, 1))

            def context(hf):
                for k in range(DK):
                    jobs.wait_filled(act, b, ("c", hf, k))
                    nc.scalar.activation(cT[:, k, :], jobs.bank(("c", hf, k)), ACT.Copy).then_inc(c_ready.sem, 1)
                    jobs.free(act.drain(), ("c", hf, k))

            for qt in range(HB_TILES):
                act.wait_ge(nmax_ready.sem, nmax_ready.done(b, qt))
                if qt >= 2:
                    jobs.wait_filled(act, b, ("t", qt - 2, 1))
                s0 = 2 * (qt % 2)
                nc.scalar.activation(prob[:, qt % 2, :], banks[:, s0:s0 + 2, :].rearrange("p a k -> p (a k)"),
                                     ACT.Exp, bias=nmax[:, qt % 2, :], scale=1.0 / DIM ** 0.5,
                                     accum_out=prob_sum[:, qt:qt + 1])
                act.drain().then_inc(prob_ready.sem, 1)
                for i in range(2):
                    jobs.free(act.drain(), ("s", qt, i))
                if qt > 0:
                    turn(qt - 1)
                if qt % GT == 0 and qt > 0:
                    context(qt // GT - 1)
            turn(HB_TILES - 1)
            context(HALVES - 1)

    @block.gpsimd
    def _(pool):
        pool.wait_ge(moments_ready.sem, 1)
        nc.gpsimd.tensor_tensor(rstd[:, :], moments[:, :, 1], mem.neg_half[:, :], ALU.pow).then_inc(rstd_ready.sem, 1)
        pool.wait_ge(mem.row_ready, 16)
        nc.gpsimd.tensor_tensor(bias_row[:, :], row("b_out"), row("b2"), ALU.add)
        pool.drain()
        with pool.Fori(0, BATCH) as b:
            for hf in range(HALVES):
                pool.wait_ge(xn_ready.sem, xn_ready.done(b, hf))
                xg = x[:, bass.ds(b * HB_TILES + hf * GT, GT), :]
                nc.gpsimd.tensor_tensor(xg, xg, spread(bias_row[:, :], 1, GT), ALU.add).then_inc(bias_added.sem, 1)

        w2 = mem.l2
        pool.wait_ge(w2.sem, 16 * 8)
        for part in (w2.gate, w2.up):
            nc.gpsimd.tensor_scalar(part, part.bitcast(I32), ZERO_POINT, None, ALU.subtract)
        downs = [w2.down[0:rows, lo:hi, :] for lo, hi, rows in (
            (0, Q_BLK - 1, P), (Q_BLK - 1, Q_BLK, q_rows(Q_BLK - 1)))]
        for d in downs:
            nc.gpsimd.tensor_scalar(d, d.bitcast(I32), ZERO_POINT, None, ALU.subtract)
        pool.drain()
        for d in downs:
            nc.gpsimd.tensor_tensor(d, d, spread(row("s_down"), 1, d.shape[1])[0:d.shape[0]], ALU.mult)

    @block.vector
    def _(dve):
        jobs.grant(dve)
        for t in range(TILES):
            nc.vector.bn_stats(stats[:, t, :], x[:, t, :])
        dve.drain()
        for t in range(TILES):
            nc.vector.bn_aggr(moments[:, t, :], stats[:, t, :])
        dve.drain()
        nc.vector.tensor_scalar(moments[:, :, 1], moments[:, :, 1], 1e-5, None, ALU.add).then_inc(
            moments_ready.sem, 1)
        dve.wait_ge(weight_mean, 1)
        n_w = DIM * FFN_BLK * P
        nc.vector.tensor_scalar(thr[:, 0, :], banks[:, 0, 0:2], 1.0 / n_w, BIT_EPS, ALU.mult, ALU.max)
        dve.drain()
        nc.vector.tensor_scalar(thr[:, 1, :], thr[:, 0, :], -0.5, None, ALU.mult)
        dve.drain()
        nc.vector.tensor_scalar(thr[:, 0, :], thr[:, 0, :], 0.5, None, ALU.mult)
        dve.drain()
        for i, part in enumerate((w.w1, w.w2)):
            flat = part.rearrange("p a n -> p (a n)")
            nc.vector.tensor_scalar(below[:, :], flat, thr[:, 1, i:i + 1], None, ALU.is_lt)
            dve.drain()
            nc.vector.scalar_tensor_tensor(out=flat, in0=flat, scalar=thr[:, 0, i:i + 1], in1=below[:, :],
                                           op0=ALU.is_gt, op1=ALU.subtract)
            dve.drain()
        dve.drain().then_inc(ternary, 1)
        dve.wait_ge(mem.row_ready, 16)
        dve.wait_ge(rstd_ready.sem, 1)
        with dve.Fori(0, BATCH) as b:
            for hf in range(HALVES):
                t0 = b * HB_TILES + hf * GT
                for t in range(GT):
                    at = t0 + t
                    last = nc.vector.tensor_scalar(xn[:, t, :], x[:, at, :], moments[:, at, 0:1],
                                                   rstd[:, bass.ds(at, 1)], ALU.subtract, ALU.mult)
                last.then_inc(xn_ready.sem, 1)
                jobs.wait_filled(dve, b, ("xnT", hf, 0))
                nc.vector.tensor_copy(xnT[:, 0, :], jobs.bank(("xnT", hf, 0))).then_inc(xnT_dve.sem, 1)
                jobs.free(dve.drain(), ("xnT", hf, 0))
                for t in range(GT // 2):
                    jobs.wait_filled(dve, b, ("v", hf, t))
                    at = hf * GT + 2 * t
                    nc.vector.tensor_tensor(v[:, at:at + 2, :],
                                            jobs.bank(("v", hf, t)).rearrange("p (t d) -> p t d", t=2),
                                            spread(row("b_v"), 1, 2), ALU.add).then_inc(v_ready.sem, 1)
                    jobs.free(dve.drain(), ("v", hf, t))
                dve.wait_ge(bias_added.sem, bias_added.done(b, hf))
                for t in range(GT // 2):
                    jobs.wait_filled(dve, b, ("d", hf, t))
                    xt = x[:, bass.ds(t0 + 2 * t, 2), :]
                    last = nc.vector.tensor_tensor(xt, xt, jobs.bank(("d", hf, t)).rearrange(
                        "p (t d) -> p t d", t=2), ALU.add)
                    jobs.free(last, ("d", hf, t))

            def turn(qt):
                jobs.wait_filled(dve, b, ("t", qt, 0))
                if qt % GT == 0 and qt > 0:
                    jobs.wait_filled(dve, b, ("c", qt // GT - 1, 1))
                at = (qt % GT) * P
                nc.vector.tensor_copy(pT[:, 0:GT, at:at + P],
                                      jobs.bank(("t", qt, 0)).rearrange("p (t q) -> p t q", t=GT)).then_inc(
                    pT_dve.sem, 1)
                jobs.free(dve.drain(), ("t", qt, 0))

            def project(hf):
                dve.wait_ge(prob_ready.sem, prob_ready.done(b, hf * GT + GT - 1))
                nc.vector.reciprocal(rsum[:, :], prob_sum[:, hf * GT:(hf + 1) * GT])
                dve.drain()
                for t in range(GT // 2):
                    jobs.wait_filled(dve, b, ("o", hf, t))
                    for i in range(2):
                        xt = x[:, b * HB_TILES + hf * GT + 2 * t + i, :]
                        last = nc.vector.scalar_tensor_tensor(
                            out=xt, in0=jobs.bank(("o", hf, t))[:, i * DIM:(i + 1) * DIM],
                            scalar=rsum[:, 2 * t + i:2 * t + i + 1], in1=xt, op0=ALU.mult, op1=ALU.add)
                    jobs.free(last, ("o", hf, t))

            for qt in range(HB_TILES):
                jobs.wait_filled(dve, b, ("s", qt, 1))
                s0 = 2 * (qt % 2)
                nc.vector.tensor_reduce(nmax[:, qt % 2, :], banks[:, s0:s0 + 2, :].rearrange("p a k -> p (a k)"),
                                        AX.X, ALU.max, negate=True)
                dve.drain()
                nc.vector.tensor_scalar(nmax[:, qt % 2, :], nmax[:, qt % 2, :], 1.0 / DIM ** 0.5, None,
                                        ALU.mult).then_inc(nmax_ready.sem, 1)
                if qt > 0:
                    turn(qt - 1)
                if qt % GT == 0 and qt > 0:
                    project(qt // GT - 1)
            turn(HB_TILES - 1)
            project(HALVES - 1)
            dve.drain()



P_START = 1.0 - 1e30




def layer2(nc, mem, ctx, io):
    sb, ps, sem = mem.scoped(ctx, "l2")
    x, ident, ones, col, row, w = mem.x, mem.ident, mem.ones, mem.col, mem.row, mem.l2

    stats = sb("stats", [P, TILES, 6])
    moments = sb("moments", [P, TILES, 2])
    rstd = sb("rstd", [P, TILES])
    moments2 = sb("moments2", [P, GT, 2])
    rstd2 = sb("rstd2", [P, GT])
    xn = sb("xn", [P, GT, DIM])
    xnT = sb("xnT", [P, DK, GROUP])
    x2T = sb("x2T", [P, DK, 1 + GROUP])
    keep = sb("keep", [P, 3, DK])
    part = sb("part", [P, DK, GROUP])
    x2 = part[:, :, :].rearrange("p a n -> p (a n)").rearrange("p (t d) -> p t d", t=GT)
    q = part
    mixed = sb("mixed", [P, 3, DK, GROUP])
    wdec = sb("wdec", [P, DK])
    kk = sb("kk", [P, DK, GROUP])
    vv = sb("vv", [P, DK, GROUP])
    rr = sb("rr", [P, DK, GROUP])
    pmax = sb("pmax", [P, DK, 1 + GROUP])
    num = sb("num", [P, DK, 1 + GROUP])
    den = sb("den", [P, DK, 1 + GROUP])
    e1 = sb("e1", [P, DK, GROUP])
    e2 = sb("e2", [P, DK, GROUP])
    c1, c2, c2v = mixed[:, 0, :, :], mixed[:, 1, :, :], mixed[:, 2, :, :]
    e2v = xn[:, :, :].rearrange("p t d -> p (t d)").rearrange("p (a n) -> p a n", a=DK)
    rw = c2v
    sg = sb("sg", [P, 2, GROUP])
    hT = sb("hT", [P, Q_BLK, GROUP])
    banks = ps("l2_banks", [P, 8, GROUP])

    ORDER = ["xnT", 0, 1, "x2T", 2, "k", "v", "r", 3, 4, 5, "down", "o"]
    names = []
    for part_ in ORDER:
        if isinstance(part_, int):
            names += [("g", part_), ("u", part_)]
        else:
            names += [(part_, k) for k in range(2)]
    jobs = Jobs(mem, banks, BATCH * HALVES, [(n, i % 8) for i, n in enumerate(names)])

    moments_ready = Event(sem("l2_moments_ready"), 1)
    rstd_ready = Event(sem("l2_rstd_ready"), 1)
    moments2_ready = Event(sem("l2_moments2_ready"), 1)
    rstd2_ready = Event(sem("l2_rstd2_ready"), 1)
    xn_ready = Event(sem("l2_xn_ready"), 2)
    xT_dve = Event(sem("l2_xT_dve"), 2)
    xT_act = Event(sem("l2_xT_act"), 2)
    skip_added = Event(sem("l2_skip_added"), 1)
    mix_ready = Event(sem("l2_mix_ready"), 3)
    kvr_ready = Event(sem("l2_kvr_ready"), 6)
    max_ready = Event(sem("l2_max_ready"), 1)
    q_ready = Event(sem("l2_q_ready"), 1)
    arg_dve = Event(sem("l2_arg_dve"), 2)
    arg_pool = Event(sem("l2_arg_pool"), 2)
    exp_ready = Event(sem("l2_exp_ready"), 4)
    old_part = Event(sem("l2_old_part"), 1)
    gated = Event(sem("l2_gated"), 1)
    rw_ready = Event(sem("l2_rw_ready"), 1)
    silu_ready = Event(sem("l2_silu_ready"), Q_BLK)
    h_ready = Event(sem("l2_h_ready"), Q_BLK, credit=2)
    decay_exp = sem("l2_decay_exp")
    reset_done = Event(sem("l2_reset_done"), 1)

    block = ctx.enter_context(nc.Block())

    @block.sync
    def _(sp):
        mem.load_l3b(sp, io)

    @block.tensor
    def _(pe):
        def mm(out, lhsT, rhs, start=True, stop=True):
            return nc.tensor.matmul(out, lhsT, rhs, start=start, stop=stop)

        def turn(g, name, src):
            for k in range(DK):
                jobs.wait_room(pe, g, (name, k))
                for t in range(GT):
                    last = nc.tensor.transpose(jobs.bank((name, k))[:, t * P:(t + 1) * P],
                                               src[:, t, k * P:(k + 1) * P], ident[:, :])
                jobs.fill(last, (name, k))

        pe.wait_ge(w.sem, 16 * 8)
        with pe.Fori(0, BATCH) as b:
            with pe.Fori(0, HALVES) as half:
                g = b * HALVES + half

                def hidden(u):
                    rows = q_rows(u)
                    for name, m in (("g", w.gate), ("u", w.up)):
                        jobs.wait_room(pe, g, (name, u))
                        for k in range(DK):
                            last = mm(jobs.bank((name, u))[0:rows, :], m[:, k, u * P:u * P + rows], xnT[:, k, :],
                                      k == 0, k == DK - 1)
                        jobs.fill(last, (name, u))

                def time_mix(i, name, m):
                    pe.wait_ge(mix_ready.sem, mix_ready.done(g, i))
                    for n in range(DK):
                        jobs.wait_room(pe, g, (name, n))
                        for k in range(DK):
                            last = mm(jobs.bank((name, n)), m[:, k, n * P:(n + 1) * P], mixed[:, i, k, :],
                                      k == 0, k == DK - 1)
                        jobs.fill(last, (name, n))

                pe.wait_ge(xn_ready.sem, xn_ready.done(g, 0))
                turn(g, "xnT", xn)
                pe.wait_ge(xT_dve.sem, xT_dve.done(g, 0))
                pe.wait_ge(xT_act.sem, xT_act.done(g, 0))
                hidden(0)
                hidden(1)
                pe.wait_ge(xn_ready.sem, xn_ready.done(g, 1))
                turn(g, "x2T", x2)
                hidden(2)
                time_mix(0, "k", w.k)
                time_mix(1, "v", w.v)
                time_mix(2, "r", w.r)
                for u in range(3, Q_BLK):
                    hidden(u)
                pe.wait_ge(h_ready.sem, h_ready.done(g))
                for t in range(GT // 2):
                    jobs.wait_room(pe, g, ("down", t))
                    for i in range(2):
                        out = jobs.bank(("down", t))[:, i * DIM:(i + 1) * DIM]
                        tok = slice((2 * t + i) * P, (2 * t + i + 1) * P)
                        for u in range(Q_BLK):
                            rows = q_rows(u)
                            last = mm(out, hT[0:rows, u, tok], w.down[0:rows, u, :], u == 0, u == Q_BLK - 1)
                    jobs.fill(last, ("down", t))
                pe.wait_ge(rw_ready.sem, rw_ready.done(g))
                for t in range(GT // 2):
                    jobs.wait_room(pe, g, ("o", t))
                    for i in range(2):
                        out = jobs.bank(("o", t))[:, i * DIM:(i + 1) * DIM]
                        tok = slice((2 * t + i) * P, (2 * t + i + 1) * P)
                        for k in range(DK):
                            last = mm(out, rw[:, k, tok], w.o[:, k, :], k == 0, k == DK - 1)
                    jobs.fill(last, ("o", t))

    @block.scalar
    def _(act):
        act.wait_ge(mem.col_ready, 16)
        nc.scalar.activation(wdec[:, :], mem.cols[:, COL_AT["time_decay"]:COL_AT["time_decay"] + DK],
                             ACT.Exp).then_inc(decay_exp, 1)
        with act.Fori(0, BATCH) as b:
            with act.Fori(0, HALVES) as half:
                g = b * HALVES + half

                def silu(u):
                    rows = q_rows(u)
                    jobs.wait_filled(act, g, ("g", u))
                    act.wait_ge(h_ready.sem, h_ready.room(g, u))
                    nc.scalar.activation(sg[0:rows, u % 2, :], jobs.bank(("g", u))[0:rows, :], ACT.Silu,
                                         scale=col("s_gate", u)[0:rows, :]).then_inc(silu_ready.sem, 1)
                    jobs.free(act.drain(), ("g", u))

                jobs.wait_filled(act, g, ("xnT", 1))
                nc.scalar.activation(xnT[:, 1, :], jobs.bank(("xnT", 1)), ACT.Copy).then_inc(xT_act.sem, 1)
                jobs.free(act.drain(), ("xnT", 1))
                silu(0)
                silu(1)
                jobs.wait_filled(act, g, ("x2T", 1))
                act.wait_ge(reset_done.sem, reset_done.done(b))
                nc.scalar.activation(x2T[:, 1, 1:], jobs.bank(("x2T", 1)), ACT.Identity, bias=col("ln_bias", 1),
                                     scale=col("ln_scale", 1)).then_inc(xT_act.sem, 1)
                jobs.free(act.drain(), ("x2T", 1))
                silu(2)
                for name, dst in (("k", kk), ("v", vv)):
                    for n in range(DK):
                        jobs.wait_filled(act, g, (name, n))
                        nc.scalar.activation(dst[:, n, :], jobs.bank((name, n)), ACT.Copy).then_inc(kvr_ready.sem, 1)
                        jobs.free(act.drain(), (name, n))
                for n in range(DK):
                    jobs.wait_filled(act, g, ("r", n))
                    nc.scalar.activation(rr[:, n, :], jobs.bank(("r", n)), ACT.Sigmoid).then_inc(kvr_ready.sem, 1)
                    jobs.free(act.drain(), ("r", n))
                for buf, event, n in ((c1, arg_dve, 0), (c2, arg_pool, 0), (e2, arg_dve, 1), (e1, arg_pool, 1)):
                    act.wait_ge(event.sem, event.done(g, n))
                    nc.scalar.activation(buf[:, :, :], buf[:, :, :], ACT.Exp).then_inc(exp_ready.sem, 1)
                for u in range(3, Q_BLK):
                    silu(u)

    @block.gpsimd
    def _(pool):
        pool.wait_ge(moments_ready.sem, 1)
        nc.gpsimd.tensor_tensor(rstd[:, :], moments[:, :, 1], mem.neg_half[:, :], ALU.pow).then_inc(rstd_ready.sem, 1)
        with pool.Fori(0, BATCH) as b:
            with pool.Fori(0, HALVES) as half:
                g = b * HALVES + half
                pool.wait_ge(moments2_ready.sem, moments2_ready.done(g))
                nc.gpsimd.tensor_tensor(rstd2[:, :], moments2[:, :, 1], mem.neg_half[:, 0:GT], ALU.pow).then_inc(
                    rstd2_ready.sem, 1)
                xg = x[:, bass.ds(g * GT, GT), :]
                nc.gpsimd.tensor_tensor(xg, xg, xn[:, :, :], ALU.add).then_inc(skip_added.sem, 1)
                pool.wait_ge(kvr_ready.sem, kvr_ready.done(g, 3))
                pool.wait_ge(max_ready.sem, max_ready.done(g))
                nc.gpsimd.tensor_tensor(c2[:, :, :], kk[:, :, :], pmax[:, :, 1:], ALU.subtract).then_inc(
                    arg_pool.sem, 1)
                pool.wait_ge(q_ready.sem, q_ready.done(g))
                nc.gpsimd.tensor_tensor(e1[:, :, :], pmax[:, :, 0:GROUP], q[:, :, :], ALU.subtract).then_inc(
                    arg_pool.sem, 1)
                pool.wait_ge(exp_ready.sem, exp_ready.done(g, 2))
                nc.gpsimd.tensor_tensor(e2v[:, :, :], e2[:, :, :], vv[:, :, :], ALU.mult)
                pool.drain()
                pool.wait_ge(old_part.sem, old_part.done(g))
                nc.gpsimd.tensor_tensor(c2v[:, :, :], c2v[:, :, :], e2v[:, :, :], ALU.add)
                pool.drain()
                nc.gpsimd.tensor_tensor(c2v[:, :, :], c2v[:, :, :], rr[:, :, :], ALU.mult).then_inc(gated.sem, 1)

    @block.vector
    def _(dve):
        jobs.grant(dve)
        dve.wait_ge(mem.col_ready, 16)
        h_ready.grant(dve)
        for t in range(TILES):
            nc.vector.bn_stats(stats[:, t, :], x[:, t, :])
        dve.drain()
        for t in range(TILES):
            nc.vector.bn_aggr(moments[:, t, :], stats[:, t, :])
        dve.drain()
        nc.vector.tensor_scalar(moments[:, :, 1], moments[:, :, 1], 1e-5, None, ALU.add).then_inc(
            moments_ready.sem, 1)
        mix0 = COL_AT["mix_k"]
        nc.vector.tensor_scalar(keep[:, :, :].rearrange("p a b -> p (a b)"), mem.cols[:, mix0:mix0 + 3 * DK],
                                -1.0, 1.0, ALU.mult, ALU.add)
        dve.wait_ge(rstd_ready.sem, 1)
        dve.wait_ge(decay_exp, 1)
        nc.vector.tensor_scalar(wdec[:, :], wdec[:, :], -1.0, None, ALU.mult)
        dve.drain()
        with dve.Fori(0, BATCH) as b:
            nc.vector.memset(x2T[:, :, 0:1], 0.0)
            nc.vector.memset(pmax[:, :, 0:1], P_START)
            nc.vector.memset(num[:, :, 0:1], 0.0)
            nc.vector.memset(den[:, :, 0:1], 0.0)
            dve.drain().then_inc(reset_done.sem, 1)
            with dve.Fori(0, HALVES) as half:
                g = b * HALVES + half

                def hidden(u):
                    rows = q_rows(u)
                    jobs.wait_filled(dve, g, ("u", u))
                    dve.wait_ge(silu_ready.sem, silu_ready.done(g, u))
                    nc.vector.scalar_tensor_tensor(out=hT[0:rows, u, :], in0=jobs.bank(("u", u))[0:rows, :],
                                                   scalar=col("s_up", u)[0:rows, :], in1=sg[0:rows, u % 2, :],
                                                   op0=ALU.mult, op1=ALU.mult).then_inc(h_ready.sem, 1)
                    jobs.free(dve.drain(), ("u", u))

                def add(name):
                    for t in range(GT // 2):
                        jobs.wait_filled(dve, g, (name, t))
                        xt = x[:, bass.ds(g * GT + 2 * t, 2), :]
                        last = nc.vector.tensor_tensor(xt, xt, jobs.bank((name, t)).rearrange(
                            "p (t d) -> p t d", t=2), ALU.add)
                        jobs.free(last, (name, t))
                    dve.drain()

                for t in range(GT):
                    at = g * GT + t
                    last = nc.vector.tensor_scalar(xn[:, t, :], x[:, at, :], moments[:, at, 0:1],
                                                   rstd[:, bass.ds(at, 1)], ALU.subtract, ALU.mult)
                last.then_inc(xn_ready.sem, 1)
                dve.drain()
                for t in range(GT):
                    nc.vector.bn_stats(stats[:, t, :], xn[:, t, :])
                dve.drain()
                for t in range(GT):
                    nc.vector.bn_aggr(moments2[:, t, :], stats[:, t, :])
                dve.drain()
                nc.vector.tensor_scalar(moments2[:, :, 1], moments2[:, :, 1], 1e-5, None, ALU.add).then_inc(
                    moments2_ready.sem, 1)
                jobs.wait_filled(dve, g, ("xnT", 0))
                nc.vector.tensor_copy(xnT[:, 0, :], jobs.bank(("xnT", 0))).then_inc(xT_dve.sem, 1)
                jobs.free(dve.drain(), ("xnT", 0))
                dve.wait_ge(rstd2_ready.sem, rstd2_ready.done(g))
                for t in range(GT):
                    last = nc.vector.tensor_scalar(x2[:, t, :], xn[:, t, :], moments2[:, t, 0:1], rstd2[:, t:t + 1],
                                                   ALU.subtract, ALU.mult)
                last.then_inc(xn_ready.sem, 1)
                dve.drain()
                hidden(0)
                jobs.wait_filled(dve, g, ("x2T", 0))
                nc.vector.tensor_scalar(x2T[:, 0, 1:], jobs.bank(("x2T", 0)), col("ln_scale", 0), col("ln_bias", 0),
                                        ALU.mult, ALU.add).then_inc(xT_dve.sem, 1)
                jobs.free(dve.drain(), ("x2T", 0))
                dve.wait_ge(xT_act.sem, xT_act.done(g))
                for i, name in enumerate(("mix_k", "mix_v", "mix_r")):
                    for k in range(DK):
                        nc.vector.tensor_scalar(part[:, k, :], x2T[:, k, 0:GROUP], keep[:, i, k:k + 1], None, ALU.mult)
                    dve.drain()
                    for k in range(DK):
                        last = nc.vector.scalar_tensor_tensor(out=mixed[:, i, k, :], in0=x2T[:, k, 1:],
                                                              scalar=col(name, k), in1=part[:, k, :],
                                                              op0=ALU.mult, op1=ALU.add)
                    last.then_inc(mix_ready.sem, 1)
                    dve.drain()
                    if i == 0:
                        hidden(1)
                nc.vector.tensor_copy(x2T[:, :, 0:1], x2T[:, :, GROUP:])
                hidden(2)
                dve.wait_ge(kvr_ready.sem, kvr_ready.done(g, 1))
                for k in range(DK):
                    nc.vector.tensor_tensor_scan(pmax[:, k, 1:], wdec[:, k:k + 1].broadcast_to([P, GROUP]), kk[:, k, :],
                                                 initial=pmax[:, k, 0:1], op0=ALU.add, op1=ALU.max)
                dve.drain().then_inc(max_ready.sem, 1)
                for k in range(DK):
                    nc.vector.scalar_tensor_tensor(out=c1[:, k, :], in0=pmax[:, k, 0:GROUP], scalar=wdec[:, k:k + 1],
                                                   in1=pmax[:, k, 1:], op0=ALU.add, op1=ALU.subtract)
                dve.drain().then_inc(arg_dve.sem, 1)
                for k in range(DK):
                    nc.vector.scalar_tensor_tensor(out=q[:, k, :], in0=kk[:, k, :], scalar=col("time_first", k),
                                                   in1=pmax[:, k, 0:GROUP], op0=ALU.add, op1=ALU.max)
                dve.drain().then_inc(q_ready.sem, 1)
                for k in range(DK):
                    nc.vector.scalar_tensor_tensor(out=e2[:, k, :], in0=kk[:, k, :], scalar=col("time_first", k),
                                                   in1=q[:, k, :], op0=ALU.add, op1=ALU.subtract)
                dve.drain().then_inc(arg_dve.sem, 1)
                dve.wait_ge(kvr_ready.sem, kvr_ready.done(g))
                dve.wait_ge(exp_ready.sem, exp_ready.done(g, 1))
                nc.vector.tensor_tensor(c2v[:, :, :], c2[:, :, :], vv[:, :, :], ALU.mult)
                for k in range(DK):
                    nc.vector.tensor_tensor_scan(den[:, k, 1:], c1[:, k, :], c2[:, k, :], initial=den[:, k, 0:1],
                                                 op0=ALU.mult, op1=ALU.add)
                dve.drain()
                for k in range(DK):
                    nc.vector.tensor_tensor_scan(num[:, k, 1:], c1[:, k, :], c2v[:, k, :], initial=num[:, k, 0:1],
                                                 op0=ALU.mult, op1=ALU.add)
                hidden(3)
                hidden(4)
                dve.wait_ge(exp_ready.sem, exp_ready.done(g, 3))
                nc.vector.tensor_tensor(c2v[:, :, :], e1[:, :, :], num[:, :, 0:GROUP], ALU.mult).then_inc(
                    old_part.sem, 1)
                nc.vector.tensor_tensor(c1[:, :, :], e1[:, :, :], den[:, :, 0:GROUP], ALU.mult)
                dve.drain()
                nc.vector.tensor_tensor(c1[:, :, :], c1[:, :, :], e2[:, :, :], ALU.add)
                dve.drain()
                nc.vector.scalar_tensor_tensor(out=c2[:, :, :], in0=c1[:, :, :], scalar=0.0, in1=c1[:, :, :],
                                               op0=ALU.is_equal, op1=ALU.add)
                for s in (pmax, num, den):
                    nc.vector.tensor_copy(s[:, :, 0:1], s[:, :, GROUP:])
                hidden(5)
                nc.vector.reciprocal(c2[:, :, :], c2[:, :, :])
                dve.drain()
                nc.vector.scalar_tensor_tensor(out=c2[:, :, :], in0=c1[:, :, :], scalar=0.0, in1=c2[:, :, :],
                                               op0=ALU.not_equal, op1=ALU.mult)
                dve.drain()
                dve.wait_ge(gated.sem, gated.done(g))
                nc.vector.tensor_tensor(rw[:, :, :], c2v[:, :, :], c2[:, :, :], ALU.mult).then_inc(rw_ready.sem, 1)
                dve.wait_ge(skip_added.sem, skip_added.done(g))
                add("down")
                add("o")



L3_EPS = 1e-12
LIMIT = 7.0
ALPHA = 1.702
I_BLK = 2
CM_BLK = 8


def layer3(nc, mem, ctx, io):
    sb, ps, sem = mem.scoped(ctx, "l3")
    x, ident, ones, col, row, w = mem.x, mem.ident, mem.ones, mem.col, mem.row, mem.l3

    stats = sb("stats", [P, GT, 6])
    moments = sb("moments", [P, GT, 2])
    rstd = sb("rstd", [P, GT])
    xn = sb("xn", [P, HB_TILES, DIM])
    tmp = sb("tmp", [P, GT, DIM])
    xnT = sb("xnT", [P, DK, SEQ])
    xlT = sb("xlT", [P, DK, 1 + GROUP])
    mixT = sb("mixT", [P, DK, GROUP])
    dec = sb("dec", [P, DK, SEQ])
    junk = sb("junk", [P, GROUP])
    toT = sb("toT", [P, DK, GROUP])
    g_ = sb("g_", [P, I_BLK, GROUP])
    s_ = sb("s_", [P, I_BLK, GROUP])
    u_ = sb("u_", [P, I_BLK, GROUP])
    gs = sb("gs", [P, I_BLK, GROUP])
    hT = sb("hT", [P, 2, I_BLK, GROUP])
    x2 = sb("x2", [P, GT, DIM])
    xcT = sb("xcT", [P, DK, 1 + GROUP])
    rc = sb("rc", [P, GT, DIM])
    lg = sb("lg", [P, GT, N_EXP])
    lmax = sb("lmax", [P, GT])
    le = sb("le", [P, GT, N_EXP])
    pairs = GT * N_EXP * N_EXP
    gt, eq = [junk[:, i * pairs:(i + 1) * pairs].rearrange("p (t e f) -> p t e f", e=N_EXP, f=N_EXP) for i in range(2)]
    rank = sb("rank", [P, GT, N_EXP])
    esum = sb("esum", [P, GT])
    comb = sb("comb", [P, HB_TILES, N_EXP])
    combT = sb("combT", [N_EXP, GROUP])
    vm = sb("vm", [P, HALVES, DK])
    vmix = sb("vmix", [P, DK])
    ucol = sb("ucol", [P, DK])
    up_bias = sb("up_bias", [P, N_EXP * I_BLK])
    keep = sb("keep", [P, DK])
    kcT = mem.region_c[:, 0:CM_BLK * GROUP].rearrange("p (a n) -> p a n", a=CM_BLK)
    rT = mem.region_c[:, CM_BLK * GROUP:CM_BLK * GROUP + DK * SEQ].rearrange("p (a n) -> p a n", a=DK)
    banks = ps("l3_banks", [P, 8, GROUP])

    N_UNITS = HALVES * N_EXP
    PLAN = [("norm_x", 0), ("norm_l", 0), ("hidden", 0), ("norm_m", 0), ("activate", 0), ("hidden", 1),
            ("activate", 1), ("hidden", 2), ("turn_l", 0)]
    extra = {2: [("mix", 0), ("norm_x", 1)], 3: [("norm_l", 1)], 4: [("norm_m", 1)], 5: [("turn_l", 1)],
             6: [("mix", 1)], 7: [("time_row", 0), ("scale", 0), ("turn_comb", 0)], 8: [("turn", 0), ("bias", 0)],
             9: [("norm_c", 0), ("turn_comb", 1)], 10: [("turn_c", 0), ("bias", 1)],
             11: [("kc", 0), ("scale", 1)], 12: [("vc", 0), ("turn", 1)], 13: [("norm_c", 1)],
             14: [("turn_c", 1)], 15: [("kc", 1)]}
    for n in range(2, N_UNITS):
        PLAN += [("down", n - 2), *extra[n], ("activate", n)]
        if n + 1 < N_UNITS:
            PLAN.append(("hidden", n + 1))
    PLAN += [("down", N_UNITS - 2), ("vc", 1), ("down", N_UNITS - 1)]

    names = []
    for step, n in PLAN:
        if step == "norm_x":
            names += [("xnT", n, k) for k in range(DK)] + [("route", n)]
        elif step == "turn_l":
            names += [("xl", n, k) for k in range(DK)]
        elif step == "mix":
            names += [("v", n, k) for k in range(DK)] + [("r", n, k) for k in range(DK)]
        elif step == "hidden":
            for m in range(I_BLK):
                names += [("g", n, m), ("u", n, m)]
        elif step == "down":
            names += [("d", n, t) for t in range(GT // 2)]
        elif step == "time_row":
            names += ["time_row"]
        elif step == "turn":
            names += [("to", n, t) for t in range(GT // 2)]
        elif step == "turn_comb":
            names += [("ct", n)]
        elif step == "bias":
            names += [("db", n, t) for t in range(GT // 2)]
        elif step == "turn_c":
            names += [("xc", n, k) for k in range(DK)]
        elif step == "kc":
            names += [("rc", n, t) for t in range(GT // 2)] + [("kc", n, f) for f in range(CM_BLK)]
        elif step == "vc":
            names += [("vc", n, t) for t in range(GT // 2)]
    jobs = Jobs(mem, banks, BATCH, [(n, i % 8) for i, n in enumerate(names)])

    norm_steps = [(step, n) for step, n in PLAN if step in ("norm_x", "norm_l", "norm_m", "turn", "norm_c")]
    norm_at = {step: i for i, step in enumerate(norm_steps)}
    NORMS = len(norm_steps)
    moments_ready = Event(sem("l3_moments_ready"), NORMS)
    rstd_ready = Event(sem("l3_rstd_ready"), NORMS)
    plain_ready = Event(sem("l3_plain_ready"), 2 * HALVES)
    affine_done = Event(sem("l3_affine_done"), 2 * HALVES)
    xn_ready = Event(sem("l3_xn_ready"), HALVES)
    xl_ready = Event(sem("l3_xl_ready"), HALVES)
    xnT_dve = Event(sem("l3_xnT_dve"), HALVES)
    xnT_act = Event(sem("l3_xnT_act"), HALVES)
    xlT_dve = Event(sem("l3_xlT_dve"), HALVES)
    xlT_act = Event(sem("l3_xlT_act"), HALVES)
    mix_ready = Event(sem("l3_mix_ready"), HALVES)
    r_ready = Event(sem("l3_r_ready"), HALVES * DK)
    logits_ready = Event(sem("l3_logits_ready"), HALVES)
    exp_ready = Event(sem("l3_exp_ready"), HALVES)
    comb_ready = Event(sem("l3_comb_ready"), HALVES)
    g_ready = Event(sem("l3_g_ready"), N_UNITS * I_BLK)
    s_ready = Event(sem("l3_s_ready"), N_UNITS * I_BLK)
    gs_ready = Event(sem("l3_gs_ready"), N_UNITS * I_BLK)
    h_ready = Event(sem("l3_h_ready"), N_UNITS)
    vmix_ready = Event(sem("l3_vmix_ready"), 1)
    u_row_ready = Event(sem("l3_u_row_ready"), 1)
    to_ready = Event(sem("l3_to_ready"), HALVES)
    xc_ready = Event(sem("l3_xc_ready"), HALVES)
    xcT_dve = Event(sem("l3_xcT_dve"), HALVES)
    xcT_act = Event(sem("l3_xcT_act"), HALVES)
    rc_ready = Event(sem("l3_rc_ready"), HALVES * GT // 2)
    relu_ready = Event(sem("l3_relu_ready"), HALVES * CM_BLK)
    kc_ready = Event(sem("l3_kc_ready"), HALVES * CM_BLK)
    combT_ready = Event(sem("l3_combT_ready"), HALVES)
    reset_done = Event(sem("l3_reset_done"), 1)
    steps_ready = sem("l3_steps_ready")
    dec_ready = sem("l3_dec_ready")

    block = ctx.enter_context(nc.Block())

    @block.tensor
    def _(pe):
        def mm(out, lhsT, rhs, start=True, stop=True):
            return nc.tensor.matmul(out, lhsT, rhs, start=start, stop=stop)

        def turn(b, name, hf, src, t0):
            for k in range(DK):
                jobs.wait_room(pe, b, (name, hf, k))
                for t in range(GT):
                    last = nc.tensor.transpose(jobs.bank((name, hf, k))[:, t * P:(t + 1) * P],
                                               src[:, t0 + t, k * P:(k + 1) * P], ident[:, :])
                jobs.fill(last, (name, hf, k))

        def norm_x(b, hf):
            pe.wait_ge(xn_ready.sem, xn_ready.done(b, hf))
            turn(b, "xnT", hf, xn, hf * GT)
            pe.wait_ge(xnT_dve.sem, xnT_dve.done(b, hf))
            pe.wait_ge(xnT_act.sem, xnT_act.done(b, hf))
            jobs.wait_room(pe, b, ("route", hf))
            for t in range(GT):
                at = (hf * GT + t) * P
                for k in range(DK):
                    last = mm(jobs.bank(("route", hf))[:, N_EXP * t:N_EXP * (t + 1)], xnT[:, k, at:at + P],
                              w.router[:, k, :], k == 0, k == DK - 1)
            jobs.fill(last, ("route", hf))

        def turn_l(b, hf):
            pe.wait_ge(xl_ready.sem, xl_ready.done(b, hf))
            turn(b, "xl", hf, tmp, 0)

        def mix(b, hf):
            pe.wait_ge(xlT_dve.sem, xlT_dve.done(b, hf))
            pe.wait_ge(xlT_act.sem, xlT_act.done(b, hf))
            for name, m, src in (("v", w.v, xlT[:, :, 1:]), ("r", w.r, mixT)):
                if name == "r":
                    pe.wait_ge(mix_ready.sem, mix_ready.done(b, hf))
                for n in range(DK):
                    jobs.wait_room(pe, b, (name, hf, n))
                    for k in range(DK):
                        last = mm(jobs.bank((name, hf, n)), m[:, k, n * P:(n + 1) * P], src[:, k, :],
                                  k == 0, k == DK - 1)
                    jobs.fill(last, (name, hf, n))

        def hidden(b, n):
            hf, e = n // N_EXP, n % N_EXP
            for m in range(I_BLK):
                for name, base in (("g", 0), ("u", I_BLK * P)):
                    jobs.wait_room(pe, b, (name, n, m))
                    c0 = base + m * P
                    for k in range(DK):
                        last = mm(jobs.bank((name, n, m)), w.gate_up[:, e * DK + k, c0:c0 + P],
                                  xnT[:, k, hf * GROUP:(hf + 1) * GROUP], k == 0, k == DK - 1)
                    jobs.fill(last, (name, n, m))

        def down(b, n):
            e = n % N_EXP
            pe.wait_ge(h_ready.sem, h_ready.done(b, n))
            for t in range(GT // 2):
                jobs.wait_room(pe, b, ("d", n, t))
                for i in range(2):
                    at = (2 * t + i) * P
                    for m in range(I_BLK):
                        last = mm(jobs.bank(("d", n, t))[:, i * DIM:(i + 1) * DIM], hT[:, n % 2, m, at:at + P],
                                  w.down[:, e * I_BLK + m, :], m == 0, m == I_BLK - 1)
                jobs.fill(last, ("d", n, t))

        def time_row(b, _):
            pe.wait_ge(vmix_ready.sem, vmix_ready.done(b))
            jobs.wait_room(pe, b, "time_row")
            for n in range(DK):
                for k in range(DK):
                    last = mm(jobs.bank("time_row")[:, n:n + 1], w.o[:, k, n * P:(n + 1) * P], vmix[:, k:k + 1],
                              k == 0, k == DK - 1)
            jobs.fill(last, "time_row")

        def turn_back(b, hf):
            pe.wait_ge(to_ready.sem, to_ready.done(b, hf))
            for t in range(GT // 2):
                jobs.wait_room(pe, b, ("to", hf, t))
                for i in range(2):
                    for k in range(DK):
                        at = (2 * t + i) * P
                        last = nc.tensor.transpose(
                            jobs.bank(("to", hf, t))[:, i * DIM + k * P:i * DIM + (k + 1) * P],
                            toT[:, k, at:at + P], ident[:, :])
                jobs.fill(last, ("to", hf, t))

        def turn_comb(b, hf):
            pe.wait_ge(comb_ready.sem, comb_ready.done(b, hf))
            jobs.wait_room(pe, b, ("ct", hf))
            for t in range(GT):
                last = nc.tensor.transpose(jobs.bank(("ct", hf))[0:N_EXP, t * P:(t + 1) * P],
                                           comb[:, hf * GT + t, :], ident[:, :])
            jobs.fill(last, ("ct", hf))

        def bias(b, hf):
            pe.wait_ge(combT_ready.sem, combT_ready.done(b, hf))
            for t in range(GT // 2):
                jobs.wait_room(pe, b, ("db", hf, t))
                for i in range(2):
                    at = (2 * t + i) * P
                    last = mm(jobs.bank(("db", hf, t))[:, i * DIM:(i + 1) * DIM], combT[:, at:at + P],
                              w.down_bias[0:N_EXP, :])
                jobs.fill(last, ("db", hf, t))

        def turn_c(b, hf):
            pe.wait_ge(xc_ready.sem, xc_ready.done(b, hf))
            turn(b, "xc", hf, tmp, 0)

        def channel_in(b, hf):
            pe.wait_ge(xcT_dve.sem, xcT_dve.done(b, hf))
            pe.wait_ge(xcT_act.sem, xcT_act.done(b, hf))
            for t in range(GT // 2):
                jobs.wait_room(pe, b, ("rc", hf, t))
                for i in range(2):
                    at = 1 + (2 * t + i) * P
                    for k in range(DK):
                        last = mm(jobs.bank(("rc", hf, t))[:, i * DIM:(i + 1) * DIM], xcT[:, k, at:at + P],
                                  w.cr[:, k, :], k == 0, k == DK - 1)
                jobs.fill(last, ("rc", hf, t))
            for f in range(CM_BLK):
                jobs.wait_room(pe, b, ("kc", hf, f))
                for k in range(DK):
                    last = mm(jobs.bank(("kc", hf, f)), w.ck[:, k, f * P:(f + 1) * P], xcT[:, k, 0:GROUP],
                              k == 0, k == DK - 1)
                jobs.fill(last, ("kc", hf, f))

        def channel_out(b, hf):
            pe.wait_ge(kc_ready.sem, kc_ready.done(b, (hf + 1) * CM_BLK - 1))
            for t in range(GT // 2):
                jobs.wait_room(pe, b, ("vc", hf, t))
                for i in range(2):
                    at = (2 * t + i) * P
                    for f in range(CM_BLK):
                        last = mm(jobs.bank(("vc", hf, t))[:, i * DIM:(i + 1) * DIM], kcT[:, f, at:at + P],
                                  w.cv[:, f, :], f == 0, f == CM_BLK - 1)
                jobs.fill(last, ("vc", hf, t))

        def nothing(b, n):
            pass

        parts = {"norm_x": norm_x, "norm_l": nothing, "norm_m": nothing, "turn_l": turn_l, "mix": mix,
                 "hidden": hidden, "activate": nothing, "down": down, "time_row": time_row, "scale": nothing,
                 "turn": turn_back, "norm_c": nothing, "turn_c": turn_c, "kc": channel_in, "vc": channel_out,
                 "turn_comb": turn_comb, "bias": bias}
        pe.wait_ge(w.sem, 16 * w.loads)
        with pe.Fori(0, BATCH) as b:
            for step, n in PLAN:
                parts[step](b, n)

    @block.scalar
    def _(act):
        act.wait_ge(steps_ready, 1)
        for k in range(DK):
            nc.scalar.activation(dec[:, k, :], xnT[:, 0, :], ACT.Exp, scale=col("l3_time_decay", k))
        act.drain().then_inc(dec_ready, 1)

        def norm_x(b, hf):
            half = slice(hf * GROUP, (hf + 1) * GROUP)
            jobs.wait_filled(act, b, ("xnT", hf, 1))
            nc.scalar.activation(xnT[:, 1, half], jobs.bank(("xnT", hf, 1)), ACT.Copy).then_inc(xnT_act.sem, 1)
            jobs.free(act.drain(), ("xnT", hf, 1))

        def norm_m(b, hf):
            act.wait_ge(logits_ready.sem, logits_ready.done(b, hf))
            nc.scalar.activation(le[:, :, :], lg[:, :, :], ACT.Exp).then_inc(exp_ready.sem, 1)

        def turn_l(b, hf):
            jobs.wait_filled(act, b, ("xl", hf, 1))
            if hf == 0:
                act.wait_ge(reset_done.sem, reset_done.done(b))
            else:
                act.wait_ge(mix_ready.sem, mix_ready.done(b, 0))
            nc.scalar.activation(xlT[:, 1, 1:], jobs.bank(("xl", hf, 1)), ACT.Identity, bias=col("tm_b", 1),
                                 scale=col("tm_g", 1)).then_inc(xlT_act.sem, 1)
            jobs.free(act.drain(), ("xl", hf, 1))

        def mix(b, hf):
            half = slice(hf * GROUP, (hf + 1) * GROUP)
            for n in range(DK):
                jobs.wait_filled(act, b, ("r", hf, n))
                nc.scalar.activation(rT[:, n, half], jobs.bank(("r", hf, n)), ACT.Sigmoid).then_inc(r_ready.sem, 1)
                jobs.free(act.drain(), ("r", hf, n))

        def hidden(b, n):
            for m in range(I_BLK):
                act.wait_ge(g_ready.sem, g_ready.done(b, n * I_BLK + m))
                nc.scalar.activation(s_[:, m, :], g_[:, m, :], ACT.Sigmoid, scale=ALPHA).then_inc(s_ready.sem, 1)

        def scale(b, hf):
            act.wait_ge(u_row_ready.sem, u_row_ready.done(b))
            if hf == 1:
                jobs.wait_filled(act, b, ("to", 0, GT // 2 - 1))
            for k in range(DK):
                last = nc.scalar.activation(toT[:, k, :], rT[:, k, hf * GROUP:(hf + 1) * GROUP], ACT.Copy,
                                            scale=ucol[:, k:k + 1])
            last.then_inc(to_ready.sem, 1)

        def turn_c(b, hf):
            jobs.wait_filled(act, b, ("xc", hf, 1))
            nc.scalar.activation(xcT[:, 1, 1:], jobs.bank(("xc", hf, 1)), ACT.Identity, bias=col("cm_b", 1),
                                 scale=col("cm_g", 1)).then_inc(xcT_act.sem, 1)
            jobs.free(act.drain(), ("xc", hf, 1))

        def channel_in(b, hf):
            for t in range(GT // 2):
                jobs.wait_filled(act, b, ("rc", hf, t))
                nc.scalar.activation(rc[:, 2 * t:2 * t + 2, :].rearrange("p t d -> p (t d)"),
                                     jobs.bank(("rc", hf, t)), ACT.Sigmoid).then_inc(rc_ready.sem, 1)
                jobs.free(act.drain(), ("rc", hf, t))
            for f in range(CM_BLK):
                jobs.wait_filled(act, b, ("kc", hf, f))
                nc.scalar.activation(kcT[:, f, :], jobs.bank(("kc", hf, f)), ACT.Relu).then_inc(relu_ready.sem, 1)
                jobs.free(act.drain(), ("kc", hf, f))

        def nothing(b, n):
            pass

        parts = {"norm_x": norm_x, "norm_l": nothing, "norm_m": norm_m, "turn_l": turn_l, "mix": mix,
                 "hidden": hidden, "activate": nothing, "down": nothing, "time_row": nothing, "scale": scale,
                 "turn": nothing, "norm_c": nothing, "turn_c": turn_c, "kc": channel_in, "vc": nothing,
                 "turn_comb": nothing, "bias": nothing}
        with act.Fori(0, BATCH) as b:
            for step, n in PLAN:
                parts[step](b, n)

    @block.gpsimd
    def _(pool):
        nc.gpsimd.iota(xnT[:, 0, :], pattern=[[-1, SEQ]], base=SEQ - 1, channel_multiplier=0,
                       allow_small_or_imprecise_dtypes=True).then_inc(steps_ready, 1)

        def power(b, n):
            pool.wait_ge(moments_ready.sem, moments_ready.done(b, n))
            nc.gpsimd.tensor_tensor(rstd[:, :], moments[:, :, 1], mem.neg_half[:, 0:GT], ALU.pow).then_inc(
                rstd_ready.sem, 1)

        def one_norm(step):
            return lambda b, hf: power(b, norm_at[step, hf])

        def affine(b, n, gain, shift):
            pool.wait_ge(plain_ready.sem, plain_ready.done(b, n))
            nc.gpsimd.tensor_tensor(tmp[:, :, :], tmp[:, :, :], spread(row(gain), 1, GT), ALU.mult)
            pool.drain()
            nc.gpsimd.tensor_tensor(tmp[:, :, :], tmp[:, :, :], spread(row(shift), 1, GT), ALU.add).then_inc(
                affine_done.sem, 1)

        def norm_l(b, hf):
            power(b, norm_at["norm_l", hf])
            affine(b, hf, "ln1_g", "ln1_b")

        def turn(b, hf):
            power(b, norm_at["turn", hf])
            affine(b, HALVES + hf, "ln2_g", "ln2_b")

        def hidden(b, n):
            for m in range(I_BLK):
                i = n * I_BLK + m
                pool.wait_ge(s_ready.sem, s_ready.done(b, i))
                nc.gpsimd.tensor_tensor(gs[:, m, :], g_[:, m, :], s_[:, m, :], ALU.mult).then_inc(gs_ready.sem, 1)

        def channel_in(b, hf):
            for f in range(CM_BLK):
                pool.wait_ge(relu_ready.sem, relu_ready.done(b, hf * CM_BLK + f))
                nc.gpsimd.tensor_tensor(kcT[:, f, :], kcT[:, f, :], kcT[:, f, :], ALU.mult).then_inc(kc_ready.sem, 1)

        def nothing(b, n):
            pass

        parts = {"norm_x": one_norm("norm_x"), "norm_l": norm_l, "norm_m": one_norm("norm_m"), "turn_l": nothing,
                 "mix": nothing, "hidden": hidden, "activate": nothing, "down": nothing, "time_row": nothing,
                 "scale": nothing, "turn": turn, "norm_c": one_norm("norm_c"), "turn_c": nothing,
                 "kc": channel_in, "vc": nothing, "turn_comb": nothing, "bias": nothing}
        with pool.Fori(0, BATCH) as b:
            for step, n in PLAN:
                parts[step](b, n)

    @block.vector
    def _(dve):
        def normalise(b, n, src, dst, eps):
            for t in range(GT):
                nc.vector.bn_stats(stats[:, t, :], src(t))
            dve.drain()
            for t in range(GT):
                nc.vector.bn_aggr(moments[:, t, :], stats[:, t, :])
            dve.drain()
            nc.vector.tensor_scalar(moments[:, :, 1], moments[:, :, 1], eps, None, ALU.add).then_inc(
                moments_ready.sem, 1)
            dve.wait_ge(rstd_ready.sem, rstd_ready.done(b, n))
            for t in range(GT):
                last = nc.vector.tensor_scalar(dst(t), src(t), moments[:, t, 0:1], rstd[:, t:t + 1],
                                               ALU.subtract, ALU.mult)
            return last

        def norm_x(b, hf):
            t0, half = hf * GT, slice(hf * GROUP, (hf + 1) * GROUP)
            normalise(b, norm_at["norm_x", hf], lambda t: x[:, b * HB_TILES + t0 + t, :], lambda t: xn[:, t0 + t, :],
                      1e-5).then_inc(xn_ready.sem, 1)
            jobs.wait_filled(dve, b, ("xnT", hf, 0))
            nc.vector.tensor_copy(xnT[:, 0, half], jobs.bank(("xnT", hf, 0))).then_inc(xnT_dve.sem, 1)
            jobs.free(dve.drain(), ("xnT", hf, 0))
            jobs.wait_filled(dve, b, ("route", hf))
            last = nc.vector.tensor_tensor(lg[:, :, :], jobs.bank(("route", hf))[:, 0:GT * N_EXP].rearrange(
                "p (t e) -> p t e", e=N_EXP), spread(row("router_bias"), 1, GT), ALU.add)
            jobs.free(last, ("route", hf))
            dve.drain()

        def norm_l(b, hf):
            t0 = hf * GT
            normalise(b, norm_at["norm_l", hf], lambda t: xn[:, t0 + t, :], lambda t: tmp[:, t, :], L3_EPS).then_inc(
                plain_ready.sem, 1)

        def norm_m(b, hf):
            dve.wait_ge(affine_done.sem, affine_done.done(b, hf))
            normalise(b, norm_at["norm_m", hf], lambda t: tmp[:, t, :], lambda t: tmp[:, t, :], L3_EPS).then_inc(
                xl_ready.sem, 1)
            nc.vector.tensor_reduce(lmax[:, :], lg[:, :, :], AX.X, ALU.max)
            a, c = spread(lg[:, :, :], 2, N_EXP), spread(lg[:, :, :], 3, N_EXP)
            nc.vector.tensor_tensor(gt[:, :, :, :], a, c, ALU.is_gt)
            nc.vector.tensor_tensor(eq[:, :, :, :], a, c, ALU.is_equal)
            dve.drain()
            nc.vector.tensor_tensor(lg[:, :, :], lg[:, :, :], spread(lmax[:, :], 2, N_EXP), ALU.subtract).then_inc(
                logits_ready.sem, 1)
            nc.vector.tensor_tensor(eq[:, :, :, :], eq[:, :, :, :], spread(mem.lower[:, :, :], 1, GT), ALU.mult)
            dve.drain()
            nc.vector.tensor_tensor(gt[:, :, :, :], gt[:, :, :, :], eq[:, :, :, :], ALU.add)
            dve.drain()
            nc.vector.tensor_reduce(rank[:, :, :], gt[:, :, :, :], AX.X, ALU.add)
            dve.drain()
            nc.vector.tensor_scalar(rank[:, :, :], rank[:, :, :], 2.0, None, ALU.is_lt)

        def turn_l(b, hf):
            t0 = hf * GT
            jobs.wait_filled(dve, b, ("xl", hf, 0))
            nc.vector.tensor_scalar(xlT[:, 0, 1:], jobs.bank(("xl", hf, 0)), col("tm_g", 0), col("tm_b", 0),
                                    ALU.mult, ALU.add).then_inc(xlT_dve.sem, 1)
            jobs.free(dve.drain(), ("xl", hf, 0))
            dve.wait_ge(xlT_act.sem, xlT_act.done(b, hf))
            for k in range(DK):
                nc.vector.tensor_scalar(mixT[:, k, :], xlT[:, k, 0:GROUP], keep[:, k:k + 1], None, ALU.mult)
            dve.drain()
            for k in range(DK):
                nc.vector.scalar_tensor_tensor(out=mixT[:, k, :], in0=xlT[:, k, 1:], scalar=col("l3_time_first", k),
                                               in1=mixT[:, k, :], op0=ALU.mult, op1=ALU.add)
            nc.vector.tensor_copy(xlT[:, :, 0:1], xlT[:, :, GROUP:])
            dve.drain().then_inc(mix_ready.sem, 1)
            dve.wait_ge(exp_ready.sem, exp_ready.done(b, hf))
            cb = comb[:, t0:t0 + GT, :]
            nc.vector.tensor_tensor(cb, le[:, :, :], rank[:, :, :], ALU.mult)
            dve.drain()
            nc.vector.tensor_reduce(esum[:, :], cb, AX.X, ALU.add)
            dve.drain()
            nc.vector.reciprocal(esum[:, :], esum[:, :])
            dve.drain()
            nc.vector.tensor_tensor(cb, cb, spread(esum[:, :], 2, N_EXP), ALU.mult)
            dve.drain().then_inc(comb_ready.sem, 1)

        def mix(b, hf):
            half = slice(hf * GROUP, (hf + 1) * GROUP)
            dve.drain()
            for k in range(DK):
                jobs.wait_filled(dve, b, ("v", hf, k))
                nc.vector.scalar_tensor_tensor(out=junk[:, :], in0=jobs.bank(("v", hf, k)), scalar=1.0,
                                               in1=dec[:, k, half], op0=ALU.mult, op1=ALU.mult,
                                               accum_out=vm[:, hf, k:k + 1])
                jobs.free(dve.drain(), ("v", hf, k))

        def hidden(b, n):
            e = n % N_EXP
            for m in range(I_BLK):
                jobs.wait_filled(dve, b, ("g", n, m))
                nc.vector.tensor_scalar(g_[:, m, :], jobs.bank(("g", n, m)), col("eb_gate", I_BLK * e + m), LIMIT,
                                        ALU.add, ALU.min).then_inc(g_ready.sem, 1)
                jobs.free(dve.drain(), ("g", n, m))
                jobs.wait_filled(dve, b, ("u", n, m))
                i = I_BLK * e + m
                nc.vector.tensor_scalar(u_[:, m, :], jobs.bank(("u", n, m)), up_bias[:, i:i + 1],
                                        LIMIT + 1.0, ALU.add, ALU.min)
                jobs.free(dve.drain(), ("u", n, m))

        def activate(b, n):
            for m in range(I_BLK):
                dve.wait_ge(gs_ready.sem, gs_ready.done(b, n * I_BLK + m))
                last = nc.vector.scalar_tensor_tensor(out=hT[:, n % 2, m, :], in0=u_[:, m, :], scalar=1.0 - LIMIT,
                                                      in1=gs[:, m, :], op0=ALU.max, op1=ALU.mult)
            last.then_inc(h_ready.sem, 1)
            dve.drain()

        def down(b, n):
            hf, e = n // N_EXP, n % N_EXP
            for t in range(GT // 2):
                jobs.wait_filled(dve, b, ("d", n, t))
                for i in range(2):
                    tile = hf * GT + 2 * t + i
                    xt = x[:, b * HB_TILES + tile, :]
                    last = nc.vector.scalar_tensor_tensor(
                        out=xt, in0=jobs.bank(("d", n, t))[:, i * DIM:(i + 1) * DIM], scalar=comb[:, tile, e:e + 1],
                        in1=xt, op0=ALU.mult, op1=ALU.add)
                jobs.free(last, ("d", n, t))
            dve.drain()

        def time_row(b, _):
            nc.vector.tensor_tensor(vmix[:, :], vm[:, 0, :], vm[:, 1, :], ALU.add).then_inc(vmix_ready.sem, 1)
            jobs.wait_filled(dve, b, "time_row")
            bo = COL_AT["bo"]
            last = nc.vector.tensor_tensor(ucol[:, :], jobs.bank("time_row")[:, 0:DK], mem.cols[:, bo:bo + DK],
                                           ALU.add).then_inc(u_row_ready.sem, 1)
            jobs.free(dve.drain(), "time_row")

        def turn(b, hf):
            for t in range(GT // 2):
                jobs.wait_filled(dve, b, ("to", hf, t))
                t0 = hf * GT + 2 * t
                last = nc.vector.tensor_tensor(x2[:, 2 * t:2 * t + 2, :], xn[:, t0:t0 + 2, :],
                                               jobs.bank(("to", hf, t)).rearrange("p (t d) -> p t d", t=2), ALU.add)
                jobs.free(last, ("to", hf, t))
            dve.drain()
            normalise(b, norm_at["turn", hf], lambda t: x2[:, t, :], lambda t: tmp[:, t, :], L3_EPS).then_inc(
                plain_ready.sem, 1)

        def norm_c(b, hf):
            xg = x[:, bass.ds(b * HB_TILES + hf * GT, GT), :]
            nc.vector.tensor_tensor(xg, xg, x2[:, :, :], ALU.add)
            dve.wait_ge(affine_done.sem, affine_done.done(b, HALVES + hf))
            normalise(b, norm_at["norm_c", hf], lambda t: tmp[:, t, :], lambda t: tmp[:, t, :], L3_EPS).then_inc(
                xc_ready.sem, 1)

        def turn_c(b, hf):
            jobs.wait_filled(dve, b, ("xc", hf, 0))
            nc.vector.tensor_scalar(xcT[:, 0, 1:], jobs.bank(("xc", hf, 0)), col("cm_g", 0), col("cm_b", 0),
                                    ALU.mult, ALU.add).then_inc(xcT_dve.sem, 1)
            jobs.free(dve.drain(), ("xc", hf, 0))

        def channel_out(b, hf):
            xg = x[:, bass.ds(b * HB_TILES + hf * GT, GT), :]
            for t in range(GT // 2):
                jobs.wait_filled(dve, b, ("vc", hf, t))
                dve.wait_ge(rc_ready.sem, rc_ready.done(b, hf * GT // 2 + t))
                rt = rc[:, 2 * t:2 * t + 2, :]
                last = nc.vector.tensor_tensor(rt, rt, jobs.bank(("vc", hf, t)).rearrange("p (t d) -> p t d", t=2),
                                               ALU.mult)
                jobs.free(last, ("vc", hf, t))
            dve.drain()
            nc.vector.tensor_tensor(xg, xg, rc[:, :, :], ALU.add)
            nc.vector.tensor_copy(xcT[:, :, 0:1], xcT[:, :, GROUP:])
            dve.drain()

        def turn_comb(b, hf):
            jobs.wait_filled(dve, b, ("ct", hf))
            nc.vector.tensor_copy(combT[:, :], jobs.bank(("ct", hf))[0:N_EXP, :]).then_inc(combT_ready.sem, 1)
            jobs.free(dve.drain(), ("ct", hf))

        def bias(b, hf):
            for t in range(GT // 2):
                jobs.wait_filled(dve, b, ("db", hf, t))
                xt = x[:, bass.ds(b * HB_TILES + hf * GT + 2 * t, 2), :]
                last = nc.vector.tensor_tensor(xt, xt, jobs.bank(("db", hf, t)).rearrange("p (t d) -> p t d", t=2),
                                               ALU.add)
                jobs.free(last, ("db", hf, t))
            dve.drain()

        def nothing(b, n):
            pass

        parts = {"norm_x": norm_x, "norm_l": norm_l, "norm_m": norm_m, "turn_l": turn_l, "mix": mix,
                 "hidden": hidden, "activate": activate, "down": down, "time_row": time_row, "scale": nothing,
                 "turn": turn, "norm_c": norm_c, "turn_c": turn_c, "kc": nothing, "vc": channel_out,
                 "turn_comb": turn_comb, "bias": bias}
        jobs.grant(dve)
        tf = COL_AT["l3_time_first"]
        nc.vector.tensor_scalar(keep[:, :], mem.cols[:, tf:tf + DK], -1.0, 1.0, ALU.mult, ALU.add)
        eb = COL_AT["eb_up"]
        nc.vector.tensor_scalar(up_bias[:, :], mem.cols[:, eb:eb + N_EXP * I_BLK], 1.0, None, ALU.add)
        dve.wait_ge(mem.row_ready, 16)
        dve.wait_ge(dec_ready, 1)
        with dve.Fori(0, BATCH) as b:
            nc.vector.memset(xlT[:, :, 0:1], 0.0)
            nc.vector.memset(xcT[:, :, 0:1], 0.0)
            dve.drain().then_inc(reset_done.sem, 1)
            for step, n in PLAN:
                parts[step](b, n)


class Named:
    pass


class Taker:

    def __init__(self, region):
        self.region, self.at = region, 0

    def __call__(self, blocks, width):
        part = self.region[:, self.at:self.at + blocks * width]
        self.at += blocks * width
        return part.rearrange("p (a b) -> p a b", a=blocks)


class Memory(Named):

    def __init__(self, nc, ctx):
        self.nc, self.ctx = nc, ctx

    def scoped(self, ctx, prefix):
        nc = self.nc

        def sb(name, shape, dt=F32):
            return ctx.enter_context(nc.sbuf_tensor(f"{prefix}_{name}", shape, dt))

        def ps(name, shape, dt=F32):
            return ctx.enter_context(nc.psum_tensor(name, shape, dt))

        def sem(name):
            return self.ctx.enter_context(nc.semaphore(name))

        return sb, ps, sem

    def after_l0(self):
        sb, _, sem = self.scoped(self.ctx, "mid")
        self.rows = sb("vector_rows", [P, N_ROWS])
        self.region_c = sb("region_c", [P, 4 * DK * DIM + 2 * DK * QH + Q_BLK * DIM])
        w = self.l2 = Named()
        take = Taker(self.region_c)
        w.k, w.v, w.r, w.o = [take(DK, DIM) for _ in range(4)]
        w.gate, w.up = [take(DK, QH) for _ in range(2)]
        w.down = take(Q_BLK, DIM)
        w.sem = sem("w_l2")
        self.psum_filled = [sem(f"psum_filled{b}") for b in range(8)]
        self.psum_freed = [sem(f"psum_freed{b}") for b in range(8)]
        self.filled_base, self.freed_base = [0] * 8, [0] * 8
        w = self.l3 = Named()
        w.sem, w.loads = sem("w_l3"), 10
        take = Taker(self.region_a)
        w.gate_up = take(N_EXP * DK, 2 * I_BLK * P)
        w.down = take(N_EXP * I_BLK, DIM)
        w.router = take(DK, N_EXP)
        w.down_bias = take(1, DIM)[0:N_EXP, 0, :]
        take = Taker(self.region_b)
        w.v, w.r, w.o, w.cr = [take(DK, DIM) for _ in range(4)]
        w.ck = take(DK, CM_BLK * P)
        w.cv = take(CM_BLK, DIM)

    def load_l2(self, sp, io):
        w = self.l2
        sp.dma_start(self.rows[:, :], io["rows"].broadcast_to([P, N_ROWS])).then_inc(self.row_ready, 16)
        for part, name in ((w.gate, "wq_gateT"), (w.up, "wq_upT")):
            sp.dma_start(part.bitcast(I32), io[name].rearrange("(k p) n -> p k n", p=P)).then_inc(w.sem, 16)
        full = (Q_BLK - 1) * P
        down = w.down.bitcast(I32)
        sp.dma_start(down[:, 0:Q_BLK - 1, :], io["wq_downT"][0:full, :].rearrange("(k p) n -> p k n", p=P)).then_inc(
            w.sem, 16)
        sp.dma_start(down[0:QH - full, Q_BLK - 1, :], io["wq_downT"][full:QH, :]).then_inc(w.sem, 16)
        for part, name in ((w.k, "l2_Wk"), (w.v, "l2_Wv"), (w.r, "l2_Wr"), (w.o, "l2_Wo")):
            sp.dma_start(part, io[name].rearrange("(k p) n -> p k n", p=P)).then_inc(w.sem, 16)

    def load_l3a(self, sp, io):
        w = self.l3
        for part, name in ((w.gate_up, "l3_gate_up"), (w.down, "l3_down"), (w.router, "l3_router")):
            sp.dma_start(part, io[name].rearrange("(k p) n -> p k n", p=P)).then_inc(w.sem, 16)
        sp.dma_start(w.down_bias, io["l3_down_bias"]).then_inc(w.sem, 16)

    def load_l3b(self, sp, io):
        w = self.l3
        for part, name in ((w.v, "l3_Wv"), (w.r, "l3_Wr"), (w.o, "l3_Wo"), (w.cr, "l3_Wcr"), (w.ck, "l3_Wck"),
                           (w.cv, "l3_Wcv")):
            sp.dma_start(part, io[name].rearrange("(k p) n -> p k n", p=P)).then_inc(w.sem, 16)

    def col(self, name, n=0):
        at = COL_AT[name] + n
        return self.cols[:, at:at + 1]

    def l0_row(self, name):
        at = L0_ROW_AT[name]
        return self.l0_rows[:, at:at + dict(L0_ROWS)[name]]

    def row(self, name):
        at = ROW_AT[name]
        return self.rows[:, at:at + dict(ROWS)[name]]


def start_up(nc, mem, ctx, io):
    sb, _, sem = mem.scoped(mem.ctx, "all")
    mem.x = sb("x", [P, TILES, DIM])
    mem.ident = sb("ident", [P, P])
    mem.ones = sb("ones", [P, P])
    mem.neg_half = sb("neg_half", [P, TILES])
    mem.lower = sb("lower", [P, N_EXP, N_EXP])
    mem.cols = sb("cols", [P, N_COLS])
    mem.l0_rows = sb("l0_rows", [P, N_L0_ROWS])
    mem.x_ready, mem.col_ready = sem("x_ready"), sem("col_ready")
    mem.l0_row_ready, mem.row_ready = sem("l0_row_ready"), sem("row_ready")
    mem.const_ready, mem.n_const = sem("const_ready"), 1
    mem.region_a = sb("region_a", [P, 13088])
    mem.region_b = sb("region_b", [P, 6144])
    w = mem.l0 = Named()
    take = Taker(mem.region_a)

    w.win = take(DK, D_IN)
    w.router = take(DK, N_EXP)
    w.gate_up = take(N_EXP * DK, 256)
    w.sh_gate_up = take(DK, 1024)
    w.down = take(L0_UNITS, DIM)
    w.out = take(Z_BLK, DIM)
    take = Taker(mem.region_b)
    l1 = mem.l1 = Named()
    l1.qkv = take(DK, 3 * DIM)
    l1.out = take(DK, DIM)
    l1.w1 = take(DK, FFN_BLK * P)
    l1.w2 = take(FFN_BLK, DIM)
    l1.sem = sem("w_l1")
    w.in_sem, w.gate_sem, w.ffn_sem, w.out_sem = sem("w_in"), sem("w_gate"), sem("w_ffn"), sem("w_out")

    def gu(u, k, i):
        if u >= SHARED:
            return w.gate_up[:, (u - SHARED) * DK + k, i * P:(i + 1) * P]
        at = i * 512 + u * P
        return w.sh_gate_up[:, k, at:at + P]

    w.gu = gu
    x_d = io["x"].rearrange("(g t p) d -> g p t d", p=P, t=GT)

    block = ctx.enter_context(nc.Block())

    @block.sync
    def _(sp):
        for g in range(TILES // GT):
            sp.dma_start(mem.x[:, g * GT:(g + 1) * GT, :], x_d[g]).then_inc(mem.x_ready, 16)
        sp.dma_start(mem.l0_rows[:, :], io["l0_rows"].broadcast_to([P, N_L0_ROWS])).then_inc(mem.l0_row_ready, 16)
        sp.dma_start(mem.cols[:, :], io["cols"]).then_inc(mem.col_ready, 16)
        sp.dma_start(w.router, io["w_gate"].rearrange("(k p) n -> p k n", p=P)).then_inc(w.gate_sem, 16)
        sp.dma_start(w.win, io["W_inT"].rearrange("(k p) n -> p k n", p=P)).then_inc(w.in_sem, 16)
        sp.dma_start(w.out, io["W_outT"].rearrange("(k p) n -> p k n", p=P)).then_inc(w.out_sem, 16)
        sp.dma_start(w.gate_up,
                     io["w_gate_up"].rearrange("(ek p) f -> p ek f", p=P)).then_inc(w.ffn_sem, 16)
        sp.dma_start(w.sh_gate_up, io["w_sh_gate_up"].rearrange("(k p) n -> p k n", p=P)).then_inc(w.ffn_sem, 16)
        sp.dma_start(w.down[:, SHARED:, :], io["w_down"].rearrange("(e p) n -> p e n", p=P)).then_inc(w.ffn_sem, 16)
        sp.dma_start(w.down[:, 0:SHARED, :], io["w_sh_down"].rearrange("(e p) n -> p e n", p=P)).then_inc(w.ffn_sem, 16)

        sp.dma_start(l1.qkv, io["w_qkvT"].rearrange("(k p) n -> p k n", p=P)).then_inc(l1.sem, 16)
        sp.dma_start(l1.out, io["w_attn_outT"].rearrange("(k p) n -> p k n", p=P)).then_inc(l1.sem, 16)
        sp.dma_start(l1.w1, io["w1T"].rearrange("(k p) n -> p k n", p=P)).then_inc(l1.sem, 16)
        sp.dma_start(l1.w2, io["w2T"].rearrange("(k p) n -> p k n", p=P)).then_inc(l1.sem, 16)

    @block.gpsimd
    def _(pool):
        nc.gpsimd.memset(mem.lower[:, :, :], 1.0)
        nc.gpsimd.memset(mem.ones[:, :], 1.0)
        nc.gpsimd.memset(mem.ident[:, :], 0.0)
        nc.gpsimd.memset(mem.neg_half[:, :], -0.5)
        pool.drain()
        nc.gpsimd.affine_select(out=mem.ident[:, :], in_=mem.ident[:, :], compare_op=ALU.not_equal, fill=1.0,
                                base=0, pattern=[[-1, P]], channel_multiplier=1)
        nc.gpsimd.affine_select(out=mem.lower[:, :, :], in_=mem.lower[:, :, :], compare_op=ALU.is_gt, fill=0.0,
                                base=0, pattern=[[1, N_EXP], [-1, N_EXP]], channel_multiplier=0)
        pool.drain().then_inc(mem.const_ready, 1)


def finish(nc, mem, ctx, out):
    sem = mem.ctx.enter_context(nc.semaphore("out_written"))
    out_d = out.rearrange("(g t p) d -> g p t d", p=P, t=GT)
    block = ctx.enter_context(nc.Block())

    @block.sync
    def _(sp):
        for g in range(TILES // GT):
            sp.dma_start(out_d[g], mem.x[:, g * GT:(g + 1) * GT, :]).then_inc(sem, 16)
        sp.wait_ge(sem, 16 * (TILES // GT))


def build(nc, io, out):
    with ExitStack() as whole:
        mem = Memory(nc, whole)
        with ExitStack() as ctx:
            start_up(nc, mem, ctx, io)
        with ExitStack() as ctx:
            layer0(nc, mem, ctx, io)
        mem.after_l0()
        for layer in (layer1, layer2, layer3):
            with ExitStack() as ctx:
                layer(nc, mem, ctx, io)
        with ExitStack() as ctx:
            finish(nc, mem, ctx, out)


def lay_out(v):
    import numpy as np

    def blocks(vec, n):
        full = np.zeros((n * P,), np.float32)
        full[:vec.shape[0]] = vec
        return full.reshape(n, P).T

    def rows(*parts):
        return np.ascontiguousarray(np.concatenate([p.reshape(-1) for p in parts]).reshape(1, -1))

    def turned(m):
        return np.ascontiguousarray(m.T)

    conv = v["L0_attn_conv_w"].reshape(CONV_BLK, P, CONV_K).transpose(1, 0, 2).reshape(P, -1)
    gub = v["L3_ffn_gate_up_proj_bias"]
    parts = {
        "conv_w": conv, "D": blocks(np.repeat(v["L0_attn_D"], HEAD_P), 4), "norm_w": blocks(v["L0_attn_norm_w"], 4),
        "b_qkv": blocks(v["L1_attn_b_qkv"], 6), "b1": blocks(v["L1_ffn_b1"], 8),
        "ln_scale": blocks(v["L2_attn_ln_scale"], 2), "ln_bias": blocks(v["L2_attn_ln_bias"], 2),
        "mix_k": blocks(v["L2_attn_mix_k"], 2), "mix_v": blocks(v["L2_attn_mix_v"], 2),
        "mix_r": blocks(v["L2_attn_mix_r"], 2), "time_first": blocks(v["L2_attn_time_first"], 2),
        "time_decay": blocks(v["L2_attn_time_decay"], 2), "s_gate": blocks(v["L2_ffn_s_gate"], 6),
        "s_up": blocks(v["L2_ffn_s_up"], 6), "l3_time_decay": blocks(v["L3_attn_time_decay"], 2),
        "l3_time_first": blocks(v["L3_attn_time_first"], 2),
        "eb_gate": blocks(gub[:, 0::2].reshape(-1), 16), "eb_up": blocks(gub[:, 1::2].reshape(-1), 16),
        "tm_g": blocks(v["L3_attn_tm_g"], 2), "tm_b": blocks(v["L3_attn_tm_b"], 2),
        "cm_g": blocks(v["L3_attn_cm_g"], 2), "cm_b": blocks(v["L3_attn_cm_b"], 2), "bo": blocks(v["L3_attn_bo"], 2),
    }
    cols = np.ascontiguousarray(np.concatenate([parts[n] for n, _ in COLS], axis=1))
    b_v = v["L1_attn_b_qkv"][2 * DIM:]
    r = {"dt_bias": "L0_attn_dt_bias", "A_log": "L0_attn_A_log", "b_out": "L1_attn_b_out", "b2": "L1_ffn_b2",
         "s_down": "L2_ffn_s_down", "ln1_g": "L3_attn_ln1_g", "ln1_b": "L3_attn_ln1_b",
         "ln2_g": "L3_attn_ln2_g", "ln2_b": "L3_attn_ln2_b", "router_bias": "L3_ffn_router_bias"}
    gate_up = v["L3_ffn_gate_up_proj"]
    apart = np.concatenate([gate_up[:, :, 0::2], gate_up[:, :, 1::2]], axis=2)
    return {
        "x": v["L0_attn_x"].reshape(TOKENS, DIM), "cols": cols, "rows": rows(b_v, *[v[r[n]] for n, _ in ROWS[1:]]),
        "l0_rows": rows(*[v[r[n]] for n, _ in L0_ROWS]),
        "W_inT": turned(v["L0_attn_W_in"]), "W_outT": turned(v["L0_attn_W_out"]),
        "w_gate": v["L0_ffn_w_gate"], "w_gate_up": v["L0_ffn_w_gate_up"].reshape(-1, 256),
        "w_down": v["L0_ffn_w_down"].reshape(-1, DIM), "w_sh_gate_up": v["L0_ffn_w_sh_gate_up"],
        "w_sh_down": v["L0_ffn_w_sh_down"],
        "w_qkvT": turned(v["L1_attn_w_qkv"]), "w_attn_outT": turned(v["L1_attn_w_out"]),
        "wq_gateT": turned(v["L2_ffn_wq_gate"]), "wq_upT": turned(v["L2_ffn_wq_up"]),
        "wq_downT": turned(v["L2_ffn_wq_down"]), "l2_Wk": v["L2_attn_Wk"], "l2_Wv": v["L2_attn_Wv"],
        "l2_Wr": v["L2_attn_Wr"], "l2_Wo": v["L2_attn_Wo"],
        "l3_Wv": v["L3_attn_Wv"], "l3_Wr": v["L3_attn_Wr"], "l3_Wo": v["L3_attn_Wo"], "l3_Wcr": v["L3_attn_Wcr"],
        "l3_Wck": v["L3_attn_Wck"], "l3_Wcv": v["L3_attn_Wcv"], "l3_gate_up": apart.reshape(-1, 2 * I_BLK * P),
        "l3_down": v["L3_ffn_down_proj"].reshape(-1, DIM), "l3_router": turned(v["L3_ffn_router_weight"]),
        "l3_down_bias": v["L3_ffn_down_proj_bias"],
        "w1T": turned(v["L1_ffn_w1"]), "w2T": turned(v["L1_ffn_w2"]),
    }


def kernel(**inputs):
    import numpy as np
    import concourse.bacc as bacc
    from concourse.bass_utils import run_bass_kernel_spmd

    arrays = {n: np.ascontiguousarray(a) for n, a in lay_out({n: np.asarray(a) for n, a in inputs.items()}).items()}
    nc = bacc.Bacc("TRN2", target_bir_lowering=False, num_devices=1)
    io = {n: nc.dram_tensor(n, a.shape, mybir.dt.from_np(a.dtype), kind="ExternalInput").ap()
          for n, a in arrays.items()}
    out = nc.dram_tensor("out", (TOKENS, DIM), F32, kind="ExternalOutput").ap()
    build(nc, io, out)
    got = run_bass_kernel_spmd(nc, [arrays], core_ids=[0])
    return got.results[0]["out"].reshape(BATCH, SEQ, DIM)
```
